# Optimizing a Trainium2 kernel written in Bass

```python
import numpy as np
import jax
import jax.numpy as jnp

def _softmax(x, axis=-1):
    return jax.nn.softmax(x, axis=axis)

def _gelu(x):
    return jax.nn.gelu(x, approximate=True)

def _silu(x):
    return jax.nn.silu(x)

def _sigmoid(x):
    return jax.nn.sigmoid(x)

def _layernorm(x, axis=-1, eps=1e-05):
    m = jnp.mean(x, axis=axis, keepdims=True)
    v = jnp.var(x, axis=axis, keepdims=True)
    return (x - m) / jnp.sqrt(v + eps)

def _scatter_add(tgt, idx, src, axis=0):
    return tgt.at[idx].add(src)

def _segment_sum(src, seg, n):
    return jax.ops.segment_sum(src, seg, n)
kernel_name = 'mk_audio_tower_d1_tok_audfeat1024_r4_3d906a'

def setup_inputs(seed: int=0):
    np.random.seed(seed)
    _w = jnp.asarray

    def _rec_inputs():
        import jax
        import jax.numpy as jnp
        _rk = jax.random.key(seed)
        x = -0.000125008 + 0.999885 * jax.random.normal(jax.random.fold_in(_rk, 1), (32, 750, 256), jnp.float32)
        return x
    x = _rec_inputs()

    def _L0_tok_setup():
        import jax, jax.numpy as jnp
        from jax import lax
        import numpy as np
        B, L, D, J = (8, 1024, 256, 6)
        K = 2 * J
        PAD = (K - 2) // 2
        EPS = 1e-05

        def _conv1d(x, W, b):
            y = lax.conv_general_dilated(x, W, window_strides=(2,), padding=((PAD, PAD),), dimension_numbers=('NCH', 'OIH', 'NCH'))
            return y + b[None, :, None]
        key = jax.random.key(seed)
        ks = jax.random.split(key, 6)
        fan = 1.0 / np.sqrt(D * K)
        h = jax.random.normal(ks[0], (B, L, D), dtype=jnp.float32)
        W1 = jax.random.uniform(ks[1], (D, D, K), jnp.float32, -fan, fan)
        b1 = jax.random.uniform(ks[2], (D,), jnp.float32, -fan, fan)
        W2 = jax.random.uniform(ks[3], (D, D, K), jnp.float32, -fan, fan)
        b2 = jax.random.uniform(ks[4], (D,), jnp.float32, -fan, fan)
        gamma = jnp.ones((D,), jnp.float32)
        beta = jnp.zeros((D,), jnp.float32)
        adpfactor = jnp.float32(1.0)
        return {'h': h, 'W1': W1, 'b1': b1, 'W2': W2, 'b2': b2, 'gamma': gamma, 'beta': beta, 'adpfactor': adpfactor}
    _L0_tok_all = _L0_tok_setup()
    _L0_tok_in = {k: v for k, v in _L0_tok_all.items() if k in ('W1', 'b1', 'W2', 'b2', 'gamma', 'beta', 'adpfactor')}
    del _L0_tok_all

    def _L0_attn_setup():
        import jax, jax.numpy as jnp
        import numpy as np
        FEATS = 256
        HEAD = 16
        HEAD_DIM = FEATS // HEAD
        EPS = 1e-12

        def _l2norm(t):
            n = jnp.sqrt(jnp.sum(t * t, axis=-1, keepdims=True))
            return t / jnp.maximum(n, EPS)
        key = jax.random.key(seed)
        ks = jax.random.split(key, 10)
        s = 0.02
        inp = {'x': jax.random.normal(ks[0], (4, 512, FEATS), dtype=jnp.float32), 'Wq': jax.random.normal(ks[1], (FEATS, FEATS), dtype=jnp.float32) * s, 'bq': jnp.zeros((FEATS,), dtype=jnp.float32), 'Wk': jax.random.normal(ks[2], (FEATS, FEATS), dtype=jnp.float32) * s, 'bk': jnp.zeros((FEATS,), dtype=jnp.float32), 'Wv': jax.random.normal(ks[3], (FEATS, FEATS), dtype=jnp.float32) * s, 'bv': jnp.zeros((FEATS,), dtype=jnp.float32), 'Wo': jax.random.normal(ks[4], (FEATS, FEATS), dtype=jnp.float32) * s, 'bo': jnp.zeros((FEATS,), dtype=jnp.float32), 'm': jnp.full((HEAD,), 0.5, dtype=jnp.float32)}
        return inp
    _L0_attn_all = _L0_attn_setup()
    _L0_attn_in = {k: v for k, v in _L0_attn_all.items() if k in ('Wq', 'bq', 'Wk', 'bk', 'Wv', 'bv', 'Wo', 'bo', 'm')}
    del _L0_attn_all

    def _L0_ffn_setup():
        import jax, jax.numpy as jnp
        import numpy as np
        BLOCK = 32
        W_BITS = 4
        ACT_BITS = 16

        def act_qdq(x):
            qmax = 2.0 ** (ACT_BITS - 1) - 1.0
            scale = jnp.maximum(jnp.max(jnp.abs(x)) / qmax, 1e-12)
            return jnp.clip(jnp.round(x / scale), -qmax - 1.0, qmax) * scale

        def fixed_qdq_u16(x):
            scale = 1.0 / 65536.0
            return jnp.clip(jnp.round(x / scale), 0.0, 65535.0) * scale

        def lpbq_dequant(w):
            O, I = w.shape
            qmax = 2.0 ** (W_BITS - 1) - 1.0
            wb = w.reshape(O, I // BLOCK, BLOCK)
            s = jnp.maximum(jnp.max(jnp.abs(wb), axis=-1, keepdims=True) / qmax, 1e-12)
            wq = jnp.clip(jnp.round(wb / s), -qmax - 1.0, qmax) * s
            return wq.reshape(O, I)
        key = jax.random.key(seed)
        k1, k2, k3, k4 = jax.random.split(key, 4)
        B, S, H, I = (2, 1024, 256, 768)
        x = jax.random.normal(k1, (B, S, H), jnp.float32)
        w_gate = jax.random.normal(k2, (I, H), jnp.float32) * 0.02
        w_up = jax.random.normal(k3, (I, H), jnp.float32) * 0.02
        w_down = jax.random.normal(k4, (H, I), jnp.float32) * 0.02
        return {'x': x, 'w_gate': w_gate, 'w_up': w_up, 'w_down': w_down}
    _L0_ffn_all = _L0_ffn_setup()
    _L0_ffn_in = {k: v for k, v in _L0_ffn_all.items() if k in ('w_gate', 'w_up', 'w_down')}
    del _L0_ffn_all
    return {'x': x, 'L0_tok_W1': _L0_tok_in['W1'], 'L0_tok_b1': _L0_tok_in['b1'], 'L0_tok_W2': _L0_tok_in['W2'], 'L0_tok_b2': _L0_tok_in['b2'], 'L0_tok_gamma': _L0_tok_in['gamma'], 'L0_tok_beta': _L0_tok_in['beta'], 'L0_tok_adpfactor': _L0_tok_in['adpfactor'], 'L0_attn_Wq': _L0_attn_in['Wq'], 'L0_attn_bq': _L0_attn_in['bq'], 'L0_attn_Wk': _L0_attn_in['Wk'], 'L0_attn_bk': _L0_attn_in['bk'], 'L0_attn_Wv': _L0_attn_in['Wv'], 'L0_attn_bv': _L0_attn_in['bv'], 'L0_attn_Wo': _L0_attn_in['Wo'], 'L0_attn_bo': _L0_attn_in['bo'], 'L0_attn_m': _L0_attn_in['m'], 'L0_ffn_w_gate': _L0_ffn_in['w_gate'], 'L0_ffn_w_up': _L0_ffn_in['w_up'], 'L0_ffn_w_down': _L0_ffn_in['w_down']}

def reference(x, L0_tok_W1, L0_tok_b1, L0_tok_W2, L0_tok_b2, L0_tok_gamma, L0_tok_beta, L0_tok_adpfactor, L0_attn_Wq, L0_attn_bq, L0_attn_Wk, L0_attn_bk, L0_attn_Wv, L0_attn_bv, L0_attn_Wo, L0_attn_bo, L0_attn_m, L0_ffn_w_gate, L0_ffn_w_up, L0_ffn_w_down):
    import jax
    import jax.numpy as jnp

    def _L0_tok_ref(h, W1, b1, W2, b2, gamma, beta, adpfactor):
        import jax, jax.numpy as jnp
        from jax import lax
        import numpy as np
        B, L, D, J = (8, 1024, 256, 6)
        K = 2 * J
        PAD = (K - 2) // 2
        EPS = 1e-05

        def _conv1d(x, W, b):
            y = lax.conv_general_dilated(x, W, window_strides=(2,), padding=((PAD, PAD),), dimension_numbers=('NCH', 'OIH', 'NCH'))
            return y + b[None, :, None]
        x = jnp.transpose(h, (0, 2, 1))
        y1 = jnp.transpose(_conv1d(x, W1, b1), (0, 2, 1))
        y2 = jnp.transpose(_conv1d(x, W2, b2), (0, 2, 1))
        gate = jax.nn.sigmoid(adpfactor * y2)
        x_out = y1 * gate
        mu = jnp.mean(x_out, axis=-1, keepdims=True)
        var = jnp.var(x_out, axis=-1, keepdims=True)
        x_out = (x_out - mu) * lax.rsqrt(var + EPS) * gamma + beta
        return jax.nn.silu(x_out)

    def _L0_attn_ref(x, Wq, bq, Wk, bk, Wv, bv, Wo, bo, m):
        import jax, jax.numpy as jnp
        import numpy as np
        FEATS = 256
        HEAD = 16
        HEAD_DIM = FEATS // HEAD
        EPS = 1e-12

        def _l2norm(t):
            n = jnp.sqrt(jnp.sum(t * t, axis=-1, keepdims=True))
            return t / jnp.maximum(n, EPS)
        b, n, f = x.shape

        def proj(W, bias):
            y = x @ W + bias
            return y.reshape(b, n, HEAD, HEAD_DIM).transpose(0, 2, 1, 3)
        q = _l2norm(proj(Wq, bq))
        k = _l2norm(proj(Wk, bk))
        v = proj(Wv, bv)
        sim = jnp.einsum('bhid,bhjd->bhij', q, k)
        sigma_m = jax.nn.sigmoid(m).reshape(1, HEAD, 1, 1)
        scaling = jnp.asarray(n, dtype=x.dtype) ** sigma_m
        attn = sim / scaling
        out = jnp.einsum('bhij,bhjd->bhid', attn, v)
        out = out.transpose(0, 2, 1, 3).reshape(b, n, f)
        return out @ Wo + bo

    def _L0_ffn_ref(x, w_gate, w_up, w_down):
        import jax, jax.numpy as jnp
        import numpy as np
        BLOCK = 32
        W_BITS = 4
        ACT_BITS = 16

        def act_qdq(x):
            qmax = 2.0 ** (ACT_BITS - 1) - 1.0
            scale = jnp.maximum(jnp.max(jnp.abs(x)) / qmax, 1e-12)
            return jnp.clip(jnp.round(x / scale), -qmax - 1.0, qmax) * scale

        def fixed_qdq_u16(x):
            scale = 1.0 / 65536.0
            return jnp.clip(jnp.round(x / scale), 0.0, 65535.0) * scale

        def lpbq_dequant(w):
            O, I = w.shape
            qmax = 2.0 ** (W_BITS - 1) - 1.0
            wb = w.reshape(O, I // BLOCK, BLOCK)
            s = jnp.maximum(jnp.max(jnp.abs(wb), axis=-1, keepdims=True) / qmax, 1e-12)
            wq = jnp.clip(jnp.round(wb / s), -qmax - 1.0, qmax) * s
            return wq.reshape(O, I)
        x = act_qdq(x)
        up = act_qdq(x @ lpbq_dequant(w_up).T)
        gate = act_qdq(x @ lpbq_dequant(w_gate).T)
        sig = fixed_qdq_u16(jax.nn.sigmoid(gate))
        gate = act_qdq(gate * sig)
        o = act_qdq(gate * up)
        return o @ lpbq_dequant(w_down).T
    h = _L0_tok_ref(x, L0_tok_W1, L0_tok_b1, L0_tok_W2, L0_tok_b2, L0_tok_gamma, L0_tok_beta, L0_tok_adpfactor)
    h = h + _L0_attn_ref(_layernorm(h, axis=-1), L0_attn_Wq, L0_attn_bq, L0_attn_Wk, L0_attn_bk, L0_attn_Wv, L0_attn_bv, L0_attn_Wo, L0_attn_bo, L0_attn_m)
    h = h + _L0_ffn_ref(_layernorm(h, axis=-1), L0_ffn_w_gate, L0_ffn_w_up, L0_ffn_w_down)
    return h

_drawn_inputs = setup_inputs


def setup_inputs(seed=0):
    import zlib

    import numpy as np

    out = dict(_drawn_inputs(seed))
    spreads = {'L0_tok_gamma': (1.0, 0.2),
     'L0_tok_beta': (0.0, 0.1),
     'L0_attn_bq': (0.0, 0.536),
     'L0_attn_bk': (0.0, 0.1),
     'L0_attn_bv': (0.0, 0.1),
     'L0_attn_bo': (0.0, 0.1),
     'L0_attn_m': (0.5, 0.6)}
    factors = {'L0_tok_b1': 2.877, 'L0_tok_b2': 8.0}
    for name, (base, spread) in spreads.items():
        noise = np.random.default_rng([zlib.crc32(name.encode()), seed]).standard_normal(out[name].shape)
        drawn = base * np.exp(spread * noise) if base else spread * noise
        out[name] = jnp.asarray(drawn.astype(out[name].dtype))
    for name, factor in factors.items():
        out[name] = (out[name] * factor).astype(out[name].dtype)
    return out
```

```python
import math
from contextlib import ExitStack

import concourse.bass as bass
from concourse import mybir

F32, F32R = mybir.dt.float32, mybir.dt.float32r
I16, U16 = mybir.dt.int16, mybir.dt.uint16
ACT = mybir.ActivationFunctionType
ALU = mybir.AluOpType
RMAX = bass.bass_isa.ReduceOp.max
AXX = mybir.AxisListType.X
PASSES = ((0, 0), (0, 1), (1, 0))

B, L, D, KC = 32, 750, 256, 12
PAD = (KC - 2) // 2
N = (L + 2 * PAD - KC) // 2 + 1
CH = D // 128
J = KC // 2
PHL = N + J - 1
OFF = (PAD + 1) // 2, PAD // 2
T, TOK = 3, N // 3
HEADS, HD = 16, 16
LN_EPS = 1e-5
NI = 768
BLK = 32
NTOK = B * N
FT = 500
NFT = NTOK // FT
DT = FT // 2
HT = NI // 128
MT = 2 * HT
QMAX = 32767.0


def wait(eng, sem, count):
    if not isinstance(count, int) or count > 0:
        eng.wait_ge(sem, count)


def wait_alone(eng, sem, count, seen):
    if not isinstance(count, int) or count > 0:
        eng.wait_ge(sem, count)
        eng.sem_inc(seen, 1)


def tower(nc, a, dram, x_max):
    ctx = ExitStack()

    def sb(name, shape, dt=F32):
        return ctx.enter_context(nc.sbuf_tensor(name, shape, dt))

    def sem(name):
        return ctx.enter_context(nc.semaphore(name))

    with ctx:
        conv_w = [sb(f"conv_w{p}", [128, J * 2 * CH, 2 * D], F32R) for p in range(2)]
        x_raw = sb("x_raw", [128, CH, 2, N])
        x_part = [sb(f"x_part{p}", [128, 2, CH, 2, PHL], F32R) for p in range(2)]
        qkv_w = [sb(f"qkv_w{p}", [128, CH, 3 * D], F32R) for p in range(2)]
        wo = sb("wo", [128, CH, D])
        bias12 = sb("bias12", [128, 2 * D])
        gamma, beta = sb("gamma", [128, D]), sb("beta", [128, D])
        bias_qkv = sb("bias_qkv", [128, 3 * D])
        bias_o = sb("bias_o", [128, D])
        adp = sb("adp", [128, 1])
        m_rep = sb("m_rep", [128, CH])
        m_exp = sb("m_exp", [128, CH])
        n_base = sb("n_base", [128, CH])
        inv_scaling = sb("inv_scaling", [128, CH])
        neg_half = sb("neg_half", [128, T * 2 * HEADS])
        eps = sb("eps", [128, T])
        ident = sb("ident", [128, 128])
        block_ones = sb("block_ones", [128, 128])
        head_mask = sb("head_mask", [128, CH, 128])

        y = sb("y", [TOK, T, 2 * D])
        xo, gate = y[:, :, 0:D], y[:, :, D:2 * D]
        z, sig_z = xo, gate
        h = sb("h", [TOK, T, D])
        h_bo = sb("h_bo", [TOK, 2, T, D])
        xn = sb("xn", [TOK, T, D])
        stats = [sb(f"stats{i}", [TOK, T, 6]) for i in range(3)]
        mv = [sb(f"mv{i}", [TOK, T, 2]) for i in range(3)]
        var_eps = [sb(f"var_eps{i}", [TOK, T]) for i in range(3)]
        rstd = [sb(f"rstd{i}", [TOK, T]) for i in range(3)]
        xnT = [sb(f"xnT{p}", [128, CH, N], F32R) for p in range(2)]
        qk_rows = sb("qk", [128, T, 2 * D])
        qk = qk_rows[0:TOK]
        v = sb("v", [TOK, T, D])
        sq_rows = sb("qk_sq", [128, T, 2 * D])
        qk_sq = sq_rows[0:TOK]
        conv_w_raw = sq_rows
        qkv_w_raw = qk_rows[:].rearrange("p t d -> p (t d)").rearrange("p (c d) -> p c d", c=CH)
        norm2 = sb("norm2", [TOK, T * 2 * HEADS])
        norm2_c = sb("norm2_c", [TOK, T * 2 * HEADS])
        inv_norm = sb("inv_norm", [TOK, T * 2 * HEADS])
        qT = sb("qT", [128, CH, N])
        head_m = sb("head_m", [128, CH, 128])
        m_wo = sb("m_wo", [128, CH, D])
        h2 = sb("h2", [TOK, T, D])
        xn3 = sb("xn3", [TOK, T, D])
        xn3T = sb("xn3T", [128, CH, N])
        x_amax = sb("x_amax", [128, B])
        x_amax1 = sb("x_amax1", [128, 1])

        bank = [ctx.enter_context(nc.psum_tensor(f"tower_bank{i}", [128, 512], F32)) for i in range(8)]
        CONV = bank[0], bank[1], bank[0]
        QK = bank[2], bank[3], bank[2]
        V01, V2 = bank[4], bank[5]
        HEADM, MWO = bank[4], bank[5]
        TR = bank[6], bank[7]
        ATT = bank[6], bank[7]
        TR3 = bank[2], bank[3]

        consts_in = sem("consts_in")
        w_slice_in = [sem(f"w_slice_in{i}") for i in range(T)]
        w_hi, w_lo = sem("w_hi"), sem("w_lo")
        qkv_w_hi, qkv_w_lo = sem("qkv_w_hi"), sem("qkv_w_lo")
        memset_done, built, m_sig, m_scaled = sem("memset_done"), sem("built"), sem("m_sig"), sem("m_scaled")
        pads_zero = sem("pads_zero")
        x_in = sem("x_in")
        x_hi, x_lo = sem("x_hi"), sem("x_lo")
        conv_done, y_ready, gate_ready, gated = sem("conv_done"), sem("y_ready"), sem("gate_ready"), sem("gated")
        stats_ready = [sem(f"stats_ready{i}") for i in range(3)]
        stats_seen = sem("stats_seen")
        mv_ready = [sem(f"mv_ready{i}") for i in range(3)]
        veps_ready = [sem(f"veps_ready{i}") for i in range(3)]
        rstd_ready = [sem(f"rstd_ready{i}") for i in range(3)]
        z_norm, z_gamma, z_beta, sigz_ready = sem("z_norm"), sem("z_gamma"), sem("z_beta"), sem("sigz_ready")
        h_ready, h_bo_ready, xn_ready = sem("h_ready"), sem("h_bo_ready"), sem("xn_ready")
        xnT_done, xnT_hi, xnT_lo = sem("xnT_done"), sem("xnT_hi"), sem("xnT_lo")
        qk_done, v_done, qk_ready, v_ready = sem("qk_done"), sem("v_done"), sem("qk_ready"), sem("v_ready")
        sq_ready, norm2_ready, norm2_c_ready, inv_ready = sem("sq_ready"), sem("norm2_ready"), sem("norm2_c_ready"), sem("inv_ready")
        qkn_ready, qT_done, qT_ready = sem("qkn_ready"), sem("qT_done"), sem("qT_ready")
        headm_done, headm_ready, mwo_done, mwo_ready = sem("headm_done"), sem("headm_ready"), sem("mwo_done"), sem("mwo_ready")
        att_done, h2_ready, xn3_ready = sem("att_done"), sem("h2_ready"), sem("xn3_ready")
        xn3T_done, xn3T_ready, x_amax_ready = sem("xn3T_done"), sem("xn3T_ready"), sem("x_amax_ready")
        h2_stored, xn3T_stored = sem("h2_stored"), sem("xn3T_stored")

        N_SLICE = J * 2 * CH

        def steps(run, eng):
            run(0, 0, True, False, False)
            run(1, 1, True, True, False)
            run(2, 0, True, True, True)
            run(3, 1, True, True, True)
            with eng.Fori(4, B - 1, 2) as s:
                for par in range(2):
                    run(s + par, par, True, True, True)
            run(B, 0, False, True, True)
            run(B + 1, 1, False, False, True)

        sp_seen = sem("sp_seen")
        block = ctx.enter_context(nc.Block())

        @block.sync
        def _(sp):
            def load_x(s):
                wait_alone(sp, x_lo, s, sp_seen)
                sp.dma_start(x_raw[:], a["xT"][:, bass.ds(s, 1)].rearrange("p b c h n -> p (b c) h n")
                             ).then_inc(x_in, 16)

            load_x(0)
            for k in range(N_SLICE):
                if k >= T:
                    wait_alone(sp, w_lo, k - T + 1, sp_seen)
                sp.dma_start(conv_w_raw[:, k % T, 0:D], a["W1T"][:, k]).then_inc(w_slice_in[k % T], 16)
                sp.dma_start(conv_w_raw[:, k % T, D:2 * D], a["W2T"][:, k]).then_inc(w_slice_in[k % T], 16)
            load_x(1)

            def store(m):
                wait_alone(sp, h2_ready, 2 * m + 2, sp_seen)
                sp.dma_start(dram["h2"][bass.ds(m, 1)].rearrange("b t p d -> p (b t) d"), h2[:]).then_inc(h2_stored, 16)
                wait_alone(sp, xn3T_ready, 2 * m + 2, sp_seen)
                sp.dma_start(dram["xn3T"][:, :, bass.ds(m * N, N)], xn3T[:]).then_inc(xn3T_stored, 16)

            load_x(2)
            with sp.Fori(0, B - 3) as m:
                load_x(m + 3)
                store(m)
            for m in range(B - 3, B):
                store(m)
            sp.wait_ge(h2_stored, 16 * B)
            sp.wait_ge(xn3T_stored, 16 * B)

        @block.scalar
        def _(act):
            for dst, src in ((bias12[:, 0:D], a["b1"]), (bias12[:, D:2 * D], a["b2"]), (gamma[:], a["gamma"]),
                             (beta[:], a["beta"]), (bias_qkv[:, 0:D], a["bq"]), (bias_qkv[:, D:2 * D], a["bk"]),
                             (bias_qkv[:, 2 * D:3 * D], a["bv"]), (bias_o[:], a["bo"]), (adp[:], a["adp"])):
                act.dma_start(dst, src.rearrange("(o n) -> o n", o=1).broadcast_to([128, src.shape[0]])
                              ).then_inc(consts_in, 16)
            act.dma_start(m_rep[:], a["m_rep"]).then_inc(consts_in, 16)
            for i, name in enumerate(("WqT", "WkT", "WvT")):
                act.dma_start(qkv_w_raw[:, :, i * D:(i + 1) * D], a[name]).then_inc(consts_in, 16)
            act.dma_start(wo[:], a["WoT"]).then_inc(consts_in, 16)
            for k in range(N_SLICE):
                act.wait_ge(w_slice_in[k % T], 32 * (k // T + 1))
                act.activation(conv_w[0][:, k], conv_w_raw[:, k % T], ACT.Copy).then_inc(w_hi, 1)
            act.wait_ge(consts_in, 14 * 16)
            act.activation(m_exp[:], m_rep[:], ACT.Sigmoid).then_inc(m_sig, 1)
            act.activation(qkv_w[0][:], qkv_w_raw[:], ACT.Copy).then_inc(qkv_w_hi, 1)

            def gates(s, t):
                act.wait_ge(y_ready, 3 * s + t + 1)
                act.activation(gate[:, t], y[:, t, D:2 * D], ACT.Sigmoid, scale=adp[0:TOK, 0:1]).then_inc(gate_ready, 1)

            def run(s, par, conv, mid, end):
                n, m = s - 1, s - 2
                if mid:
                    act.wait_ge(z_beta, n + 1)
                    act.activation(sig_z, z, ACT.Sigmoid).then_inc(sigz_ready, 1)
                if conv:
                    gates(s, 0)
                if mid:
                    wait(act, v_done, 3 * n)
                    for c in range(CH):
                        act.wait_ge(xnT_done, 2 * n + c + 1)
                        act.activation(xnT[0][:, c], TR[c][:, 0:N], ACT.Copy).then_inc(xnT_hi, 1)
                if end:
                    act.wait_ge(mwo_done, m + 1)
                    wait(act, att_done, 2 * m)
                    act.activation(m_wo[:].rearrange("p c d -> p (c d)"), MWO[:], ACT.Copy).then_inc(mwo_ready, 1)
                if conv:
                    gates(s, 1)
                if mid:
                    act.wait_ge(qk_ready, 3 * n + 3)
                    act.activation(qk_sq, qk, ACT.Square).then_inc(sq_ready, 1)
                if conv:
                    gates(s, 2)
                if mid:
                    wait(act, att_done, 2 * n)
                    for c in range(CH):
                        act.wait_ge(qT_done, 2 * n + c + 1)
                        act.activation(qT[:, c], TR[c][:, 0:N], ACT.Copy).then_inc(qT_ready, 1)
                if end:
                    wait(act, xn3T_stored, 16 * m)
                    wait(act, x_amax_ready, m)
                    for c in range(CH):
                        act.wait_ge(xn3T_done, 2 * m + c + 1)
                        act.activation(xn3T[:, c], TR3[c][:, 0:N], ACT.Copy).then_inc(xn3T_ready, 1)

            steps(run, act)

        @block.gpsimd
        def _(pool):
            pool.memset(ident[:], 0.0).then_inc(memset_done, 1)
            pool.memset(block_ones[:], 1.0).then_inc(memset_done, 1)
            pool.memset(neg_half[:], -0.5).then_inc(memset_done, 1)
            pool.memset(eps[:], LN_EPS).then_inc(memset_done, 1)
            pool.memset(n_base[:], float(N)).then_inc(memset_done, 1)
            pool.wait_ge(memset_done, 5)
            pool.affine_select(out=ident[:], in_=ident[:], compare_op=ALU.not_equal, fill=1.0, base=0,
                               pattern=[[-1, 128]], channel_multiplier=1).then_inc(built, 1)
            heads = block_ones[:].rearrange("p (j r) -> p j r", r=HD)
            pool.affine_select(out=heads, in_=heads, compare_op=ALU.is_ge, fill=0.0, base=0,
                               pattern=[[-HD, 128 // HD], [0, HD]], channel_multiplier=1).then_inc(built, 1)
            pool.wait_ge(built, 2)
            pool.affine_select(out=heads, in_=heads, compare_op=ALU.is_ge, fill=0.0, base=HD - 1,
                               pattern=[[HD, 128 // HD], [0, HD]], channel_multiplier=-1).then_inc(built, 1)
            pool.wait_ge(m_sig, 1)
            pool.tensor_scalar(m_exp[:], m_exp[:], -1.0, None, ALU.mult).then_inc(m_scaled, 1)
            pool.wait_ge(m_scaled, 1)
            pool.tensor_tensor(inv_scaling[:], n_base[:], m_exp[:], ALU.pow).then_inc(m_scaled, 1)
            pool.wait_ge(m_scaled, 2)
            pool.wait_ge(built, 3)
            for c in range(CH):
                pool.tensor_scalar(head_mask[:, c], block_ones[:], inv_scaling[:, c:c + 1], None, ALU.mult
                                   ).then_inc(m_scaled, 1)
            pool.wait_ge(consts_in, 14 * 16)

            def inv_std(i, k):
                pool.wait_ge(mv_ready[i], 3 * k + 3)
                pool.tensor_tensor(var_eps[i][:], mv[i][:, :, 1], eps[0:TOK], ALU.add).then_inc(veps_ready[i], 1)
                pool.wait_ge(veps_ready[i], k + 1)
                pool.tensor_tensor(rstd[i][:], var_eps[i][:], neg_half[0:TOK, 0:T], ALU.pow).then_inc(rstd_ready[i], 1)

            def run(s, par, conv, mid, end):
                n, m = s - 1, s - 2
                if mid:
                    inv_std(0, n)
                    pool.wait_ge(z_norm, 3 * n + 3)
                    pool.tensor_tensor(z, z, gamma[0:TOK, None, :].broadcast_to([TOK, T, D]), ALU.mult
                                       ).then_inc(z_gamma, 1)
                    pool.wait_ge(z_gamma, n + 1)
                    pool.tensor_tensor(z, z, beta[0:TOK, None, :].broadcast_to([TOK, T, D]), ALU.add
                                       ).then_inc(z_beta, 1)
                    inv_std(1, n)
                    pool.wait_ge(h_ready, n + 1)
                    pool.tensor_tensor(h_bo[:, 1 - par], h[:], bias_o[0:TOK, None, :].broadcast_to([TOK, T, D]),
                                       ALU.add).then_inc(h_bo_ready, 1)
                    pool.wait_ge(norm2_c_ready, n + 1)
                    pool.tensor_tensor(inv_norm[:], norm2_c[:], neg_half[0:TOK], ALU.pow).then_inc(inv_ready, 1)
                if end:
                    inv_std(2, m)

            steps(run, pool)
            pool.wait_ge(x_amax_ready, B + 1)
            pool.partition_all_reduce(x_max[:], x_amax1[:], 128, RMAX).then_inc(built, 1)
            pool.wait_ge(built, 4)

        @block.vector
        def _(dve):
            for p in range(2):
                for ph in range(2):
                    o = OFF[ph]
                    for buf in range(2):
                        dve.memset(x_part[p][:, buf, :, ph, 0:o].bitcast(F32), 0.0).then_inc(pads_zero, 1)
                        dve.memset(x_part[p][:, buf, :, ph, o + N:PHL].bitcast(F32), 0.0).then_inc(pads_zero, 1)

            def split_x(s, par):
                wait(dve, conv_done, 3 * (s - 1))
                dve.wait_ge(x_in, 16 * s + 16)
                for ph in range(2):
                    o = OFF[ph]
                    dve.tensor_copy(x_part[0][:, par, :, ph, o:o + N], x_raw[:, :, ph]).then_inc(x_hi, 1)
                dve.wait_ge(x_hi, 2 * s + 2)
                for ph in range(2):
                    o = OFF[ph]
                    ins = dve.tensor_tensor(x_part[1][:, par, :, ph, o:o + N], x_raw[:, :, ph],
                                            x_part[0][:, par, :, ph, o:o + N].bitcast(F32), ALU.subtract)
                ins.then_inc(x_lo, 1)

            split_x(0, 0)
            for k in range(N_SLICE):
                dve.wait_ge(w_hi, k + 1)
                dve.tensor_tensor(conv_w[1][:, k], conv_w_raw[:, k % T], conv_w[0][:, k].bitcast(F32),
                                  ALU.subtract).then_inc(w_lo, 1)
            dve.wait_ge(qkv_w_hi, 1)
            dve.tensor_tensor(qkv_w[1][:], qkv_w_raw[:], qkv_w[0][:].bitcast(F32), ALU.subtract).then_inc(qkv_w_lo, 1)
            dve.wait_ge(consts_in, 14 * 16)
            dve.wait_ge(m_scaled, 4)

            def layer_stats(i, k, src):
                for t in range(T):
                    dve.bn_stats(stats[i][:, t], src[:, t]).then_inc(stats_ready[i], 1)
                wait_alone(dve, stats_ready[i], 3 * k + 3, stats_seen)
                for t in range(T):
                    dve.bn_aggr(mv[i][:, t], stats[i][:, t]).then_inc(mv_ready[i], 1)

            def layer_norm(i, k, dst, src, ready):
                dve.wait_ge(rstd_ready[i], k + 1)
                for t in range(T):
                    dve.tensor_scalar(dst[:, t], src[:, t], mv[i][:, t, 0:1], rstd[i][:, t:t + 1],
                                      ALU.subtract, ALU.mult).then_inc(ready, 1)

            def conv_out(s, t):
                dve.wait_ge(conv_done, 3 * s + t + 1)
                dve.tensor_tensor(y[:, t], CONV[t][0:TOK], bias12[0:TOK], ALU.add).then_inc(y_ready, 1)

            def apply_gate(s, t):
                dve.wait_ge(gate_ready, 3 * s + t + 1)
                dve.tensor_tensor(xo[:, t], y[:, t, 0:D], gate[:, t], ALU.mult).then_inc(gated, 1)

            def run(s, par, conv, mid, end):
                n, m = s - 1, s - 2
                if mid:
                    dve.wait_ge(gated, 3 * n + 3)
                    layer_stats(0, n, xo)
                    layer_norm(0, n, z, xo, z_norm)
                if conv and not (isinstance(s, int) and s >= B - 1):
                    split_next(s, par)
                if mid:
                    dve.wait_ge(sigz_ready, n + 1)
                    wait(dve, h_bo_ready, n)
                    dve.tensor_tensor(h[:], z, sig_z, ALU.mult).then_inc(h_ready, 1)
                    dve.wait_ge(h_ready, n + 1)
                    layer_stats(1, n, h)
                    wait(dve, xnT_done, 2 * n)
                    layer_norm(1, n, xn, h, xn_ready)
                if conv:
                    conv_out(s, 0)
                if mid:
                    for c in range(CH):
                        dve.wait_ge(xnT_hi, 2 * n + c + 1)
                        dve.tensor_tensor(xnT[1][:, c], TR[c][:, 0:N], xnT[0][:, c].bitcast(F32), ALU.subtract
                                          ).then_inc(xnT_lo, 1)
                if conv:
                    apply_gate(s, 0)
                    conv_out(s, 1)
                if mid:
                    wait(dve, headm_done, n)
                    for t in range(T):
                        dve.wait_ge(qk_done, 3 * n + t + 1)
                        dve.tensor_tensor(qk[:, t], QK[t][0:TOK], bias_qkv[0:TOK, 0:2 * D], ALU.add
                                          ).then_inc(qk_ready, 1)
                    bias_v = bias_qkv[0:TOK, None, 2 * D:3 * D]
                    dve.wait_ge(v_done, 3 * n + 3)
                    dve.tensor_tensor(v[:, 0:2], V01[0:TOK].rearrange("p (t d) -> p t d", t=2),
                                      bias_v.broadcast_to([TOK, 2, D]), ALU.add).then_inc(v_ready, 1)
                    dve.tensor_tensor(v[:, 2], V2[0:TOK, 0:D], bias_qkv[0:TOK, 2 * D:3 * D], ALU.add
                                      ).then_inc(v_ready, 1)
                if end:
                    wait(dve, h2_stored, 16 * m)
                    dve.wait_ge(h_bo_ready, m + 1)
                    dve.wait_ge(att_done, 2 * m + 2)
                    dve.tensor_tensor(h2[:, 0:2], ATT[0][0:TOK].rearrange("p (t d) -> p t d", t=2),
                                      h_bo[:, par, 0:2], ALU.add).then_inc(h2_ready, 1)
                    dve.tensor_tensor(h2[:, 2], ATT[1][0:TOK, 0:D], h_bo[:, par, 2], ALU.add).then_inc(h2_ready, 1)
                if conv:
                    apply_gate(s, 1)
                if mid:
                    dve.wait_ge(sq_ready, n + 1)
                    dve.tensor_reduce(norm2[:], qk_sq.rearrange("p t (h e) -> p (t h) e", e=HD), AXX, ALU.add
                                      ).then_inc(norm2_ready, 1)
                    dve.wait_ge(norm2_ready, n + 1)
                    dve.tensor_scalar(norm2_c[:], norm2[:], 1e-24, None, ALU.max).then_inc(norm2_c_ready, 1)
                if end:
                    dve.wait_ge(h2_ready, 2 * m + 2)
                    layer_stats(2, m, h2)
                if mid:
                    dve.wait_ge(inv_ready, n + 1)
                    heads = qk.rearrange("p t (h e) -> p (t h) e", e=HD)
                    dve.tensor_tensor(heads, heads, inv_norm[:, :, None].broadcast_to([TOK, T * 2 * HEADS, HD]),
                                      ALU.mult).then_inc(qkn_ready, 1)
                if end:
                    wait(dve, xn3T_done, 2 * m)
                    layer_norm(2, m, xn3, h2, xn3_ready)
                if conv:
                    conv_out(s, 2)
                if mid:
                    wait(dve, mwo_done, n)
                    dve.wait_ge(headm_done, n + 1)
                    dve.tensor_tensor(head_m[:].rearrange("p c q -> p (c q)"), HEADM[:, 0:D],
                                      head_mask[:].rearrange("p c q -> p (c q)"), ALU.mult).then_inc(headm_ready, 1)
                if conv:
                    apply_gate(s, 2)
                if end:
                    dve.wait_ge(xn3T_ready, 2 * m + 2)
                    dve.tensor_reduce(x_amax[:, bass.ds(m, 1)], xn3T[:].rearrange("p c n -> p (c n)"), AXX, ALU.max,
                                      apply_absolute_value=True).then_inc(x_amax_ready, 1)

            def split_next(s, par):
                split_x(s + 1, 1 - par)

            run(0, 0, True, False, False)
            run(1, 1, True, True, False)
            run(2, 0, True, True, True)
            run(3, 1, True, True, True)
            with dve.Fori(4, B - 3, 2) as s:
                for par in range(2):
                    run(s + par, par, True, True, True)
            run(B - 2, 0, True, True, True)
            run(B - 1, 1, True, True, True)
            run(B, 0, False, True, True)
            run(B + 1, 1, False, False, True)
            dve.wait_ge(x_amax_ready, B)
            dve.tensor_reduce(x_amax1[:], x_amax[:], AXX, ALU.max).then_inc(x_amax_ready, 1)

        @block.tensor
        def _(pe):
            def conv_tile(s, par, t, first):
                if t == 0:
                    pe.wait_ge(x_lo, s + 1)
                    wait(pe, y_ready, 3 * s)
                if t == 2:
                    pe.wait_ge(y_ready, 3 * s + 1)
                last = N_SLICE - 1
                for k in range(N_SLICE):
                    j, ph, c = k // (2 * CH), k // CH % 2, k % CH
                    if first:
                        pe.wait_ge(w_lo, k + 1)
                    for i, (a_, b_) in enumerate(PASSES):
                        mm = pe.matmul(CONV[t][0:TOK], x_part[a_][:, par, c, ph, t * TOK + j:t * TOK + j + TOK],
                                       conv_w[b_][:, k], start=(k == 0 and i == 0), stop=(k == last and i == 2))
                mm.then_inc(conv_done, 1)

            def transposes(dst, src, done):
                for c in range(CH):
                    for t in range(T):
                        tr = pe.transpose(dst[c][:, t * TOK:(t + 1) * TOK], src[:, t, c * 128:(c + 1) * 128],
                                          ident[0:TOK, 0:TOK])
                    tr.then_inc(done, 1)

            def qkv(n):
                pe.wait_ge(xnT_lo, 2 * n + 2)
                wait(pe, xn3T_ready, 2 * (n - 1))
                for t in range(T):
                    if t == 2:
                        pe.wait_ge(qk_ready, 3 * n + 1)
                    tok = slice(t * TOK, (t + 1) * TOK)
                    groups = ((QK[t][0:TOK], 0, 2 * D, qk_done),
                              (V2[0:TOK, 0:D] if t == 2 else V01[0:TOK, t * D:(t + 1) * D], 2 * D, 3 * D, v_done))
                    for dst, lo, hi, done in groups:
                        for c in range(CH):
                            for i, (a_, b_) in enumerate(PASSES):
                                mm = pe.matmul(dst, xnT[a_][:, c, tok], qkv_w[b_][:, c, lo:hi],
                                               start=(c == 0 and i == 0), stop=(c == CH - 1 and i == 2))
                        mm.then_inc(done, 1)

            def head_matrices(n):
                pe.wait_ge(v_ready, 2 * n + 2)
                for c in range(CH):
                    f = slice(c * 128, (c + 1) * 128)
                    for t in range(T):
                        mm = pe.matmul(HEADM[:, f], v[:, t, f], qk[:, t, D + c * 128:D + (c + 1) * 128],
                                       start=(t == 0), stop=(t == T - 1))
                mm.then_inc(headm_done, 1)

            def heads_times_wo(m):
                pe.wait_ge(headm_ready, m + 1)
                for c in range(CH):
                    mm = pe.matmul(MWO[:, c * D:(c + 1) * D], head_m[:, c], wo[:, c], start=True, stop=True)
                mm.then_inc(mwo_done, 1)

            def attention_out(m):
                pe.wait_ge(mwo_ready, m + 1)
                pe.wait_ge(qT_ready, 2 * m + 2)
                for t in range(T):
                    dst = ATT[1][0:TOK, 0:D] if t == 2 else ATT[0][0:TOK, t * D:(t + 1) * D]
                    for c in range(CH):
                        mm = pe.matmul(dst, qT[:, c, t * TOK:(t + 1) * TOK], m_wo[:, c],
                                       start=(c == 0), stop=(c == CH - 1))
                    if t:
                        mm.then_inc(att_done, 1)

            pe.wait_ge(pads_zero, 16)
            pe.wait_ge(built, 1)
            pe.wait_ge(consts_in, 14 * 16)

            def run(s, par, conv, mid, end):
                n, m = s - 1, s - 2
                first = isinstance(s, int) and s == 0
                if conv:
                    conv_tile(s, par, 0, first)
                if mid:
                    pe.wait_ge(xn_ready, 3 * n + 3)
                    wait(pe, qT_ready, 2 * n)
                    transposes(TR, xn, xnT_done)
                if end:
                    heads_times_wo(m)
                if conv:
                    conv_tile(s, par, 1, False)
                if end:
                    pe.wait_ge(mwo_ready, m + 1)
                if mid:
                    if not conv or isinstance(s, int):
                        pe.wait_ge(qkv_w_lo, 1)
                    qkv(n)
                if end:
                    attention_out(m)
                if conv:
                    conv_tile(s, par, 2, False)
                if mid:
                    pe.wait_ge(qkn_ready, n + 1)
                    if end:
                        pe.wait_ge(h2_ready, 2 * m + 2)
                    transposes(TR, qk, qT_done)
                    head_matrices(n)
                if end:
                    pe.wait_ge(xn3_ready, 3 * m + 3)
                    transposes(TR3, xn3, xn3T_done)

            steps(run, pe)


class Chain:

    def __init__(self, eng, sem):
        self.eng, self.sem, self.n = eng, sem, 0

    def step(self, ins):
        self.n += 1
        ins.then_inc(self.sem, 1)
        self.eng.wait_ge(self.sem, self.n)


def all_reduce_max(nc, name, parts):
    with ExitStack() as ctx:
        row = [ctx.enter_context(nc.sbuf_tensor(f"{name}_row{i}", [128, 1], F32)) for i in range(len(parts))]
        row_max, all_max = (ctx.enter_context(nc.semaphore(f"{name}_{x}")) for x in ("row_max", "all_max"))
        block = ctx.enter_context(nc.Block())

        @block.vector
        def _(dve):
            for i, (_out, tile) in enumerate(parts):
                dve.tensor_reduce(row[i][:], tile, AXX, ALU.max).then_inc(row_max, 1)

        @block.gpsimd
        def _(pool):
            for i, (out, _tile) in enumerate(parts):
                pool.wait_ge(row_max, i + 1)
                pool.partition_all_reduce(out[:], row[i][:], 128, RMAX).then_inc(all_max, 1)
            pool.wait_ge(all_max, len(parts))


def ffn_weights(nc, a, gu_w, down_w):
    mats = (("w_gate", NI // 128, D, lambda p, k, r: gu_w[p][:, k, r * 128:r * 128 + 128]),
            ("w_up", NI // 128, D, lambda p, k, r: gu_w[p][:, k, NI + r * 128:NI + r * 128 + 128]),
            ("w_down", D // 128, NI, lambda p, k, r: down_w[p][:, k, r * 128:r * 128 + 128]))
    with ExitStack() as ctx:
        def sb(name, shape, dt=F32):
            return ctx.enter_context(nc.sbuf_tensor(name, shape, dt))

        def sem(name):
            return ctx.enter_context(nc.semaphore(name))

        raw = [sb(f"{n}_raw", [128, r, i]) for n, r, i, _ in mats]
        scale = [sb(f"{n}_scale", [128, r * i // BLK]) for n, r, i, _ in mats]
        inv = [sb(f"{n}_inv", [128, r * i // BLK]) for n, r, i, _ in mats]
        wq = [sb(f"{n}_q", [128, r, i], I16) for n, r, i, _ in mats]
        ident = sb("w_ident", [128, 128])
        bank = [ctx.enter_context(nc.psum_tensor(f"w_bank{i}", [128, 512], F32)) for i in range(4)]
        raw_in = [sem(f"{n}_in") for n, *_ in mats]
        quant, id_ready, w_ready, w_turned, w_hi, w_lo = (
            sem(x) for x in ("quant", "id_ready", "w_ready", "w_turned", "ffn_w_hi", "ffn_w_lo"))
        groups = []
        for i, (_n, rows, cols, put) in enumerate(mats):
            tiles = [(k, r) for k in range(cols // 128) for r in range(rows)]
            groups += [(i, put, tiles[g:g + 4]) for g in range(0, len(tiles), 4)]
        block = ctx.enter_context(nc.Block())

        @block.sync
        def _(sp):
            for i, (name, rows, cols, _put) in enumerate(mats):
                sp.dma_start(raw[i][:], a[name].rearrange("(r p) i -> p r i", p=128)).then_inc(raw_in[i], 16)

        @block.gpsimd
        def _(pool):
            pool.memset(ident[:], 0.0).then_inc(id_ready, 1)
            pool.wait_ge(id_ready, 1)
            pool.affine_select(out=ident[:], in_=ident[:], compare_op=ALU.not_equal, fill=1.0, base=0,
                               pattern=[[-1, 128]], channel_multiplier=1).then_inc(id_ready, 1)

        @block.vector
        def _(dve):
            chain = Chain(dve, quant)
            for i, (_n, rows, cols, _put) in enumerate(mats):
                nb = rows * cols // BLK
                blocks = raw[i][:].rearrange("p r (b e) -> p (r b) e", e=BLK)
                ints = wq[i][:].rearrange("p r (b e) -> p (r b) e", e=BLK)
                dve.wait_ge(raw_in[i], 16)
                chain.step(dve.tensor_reduce(scale[i][:], blocks, AXX, ALU.max, apply_absolute_value=True))
                chain.step(dve.tensor_scalar(scale[i][:], scale[i][:], 1.0 / 7.0, 1e-12, ALU.mult, ALU.max))
                chain.step(dve.reciprocal(inv[i][:], scale[i][:]))
                chain.step(dve.tensor_tensor(blocks, blocks, inv[i][:, :, None].broadcast_to([128, nb, BLK]), ALU.mult))
                chain.step(dve.tensor_scalar(ints, blocks, 7.0, -8.0, ALU.min, ALU.max))
                dve.tensor_tensor(blocks, ints, scale[i][:, :, None].broadcast_to([128, nb, BLK]), ALU.mult
                                  ).then_inc(w_ready, 1)
            for g, (i, put, tiles) in enumerate(groups):
                dve.wait_ge(w_hi, 4 * g + 4)
                for n, (k, r) in enumerate(tiles):
                    ins = dve.tensor_tensor(put(1, k, r), bank[g % 4][:, n * 128:(n + 1) * 128],
                                            put(0, k, r).bitcast(F32), ALU.subtract)
                    if n == len(tiles) - 1:
                        ins.then_inc(w_lo, 1)

        @block.tensor
        def _(pe):
            pe.wait_ge(id_ready, 2)
            for g, (i, _put, tiles) in enumerate(groups):
                pe.wait_ge(w_ready, i + 1)
                wait(pe, w_lo, g - 3)
                for n, (k, r) in enumerate(tiles):
                    tr = pe.transpose(bank[g % 4][:, n * 128:(n + 1) * 128], raw[i][:, r, k * 128:(k + 1) * 128], ident[:])
                tr.then_inc(w_turned, 1)

        @block.scalar
        def _(act):
            for g, (i, put, tiles) in enumerate(groups):
                act.wait_ge(w_turned, g + 1)
                for n, (k, r) in enumerate(tiles):
                    act.activation(put(0, k, r), bank[g % 4][:, n * 128:(n + 1) * 128], ACT.Copy).then_inc(w_hi, 1)


def gate_up_products(pe, banks, gu_w, x_part, par, tile_no, taken, ready, done):
    ready()
    for mt in range(MT):
        use = par * MT + mt
        count = tile_no * MT + mt + 1 - len(banks)
        wait(pe, taken, count if not isinstance(count, int) else max(count, 0))
        for c in range(CH):
            for i, (a_, b_) in enumerate(PASSES):
                mm = pe.matmul(banks[use % len(banks)][:, 0:FT], gu_w[a_][:, c, mt * 128:(mt + 1) * 128],
                               x_part[b_][:, par, c], start=(c == 0 and i == 0), stop=(c == CH - 1 and i == 2))
        mm.then_inc(done, 1)


def ffn_max(nc, dram, gu_w, x_int, x_max, sx, g_max, u_max):
    with ExitStack() as ctx:
        def sb(name, shape, dt=F32):
            return ctx.enter_context(nc.sbuf_tensor(name, shape, dt))

        def sem(name):
            return ctx.enter_context(nc.semaphore(name))

        inv_x = sb("inv_x", [128, 1])
        x_rows = sb("x_rows", [128, 2, CH, FT])
        x_part = [sb(f"xq_part{p}", [128, 2, CH, FT], F32R) for p in range(2)]
        bank = [ctx.enter_context(nc.psum_tensor(f"max_bank{i}", [128, 512], F32)) for i in range(8)]
        scales, x_in, int_ready = sem("scales"), [sem(f"rows_in{i}") for i in range(2)], sem("int_ready")
        part_hi, part_ready, gu_done, gu_taken = sem("part_hi"), sem("part_ready"), sem("gu_done"), sem("gu_taken")
        sp_seen = sem("sp_seen")
        block = ctx.enter_context(nc.Block())

        @block.sync
        def _(sp):
            def load(n, par):
                wait_alone(sp, int_ready, n - 1, sp_seen)
                sp.dma_start(x_rows[:, par], dram["xn3T"][:, :, bass.ds(n * FT, FT)]).then_inc(x_in[par], 16)

            load(0, 0)
            load(1, 1)
            with sp.Fori(2, NFT - 1, 2) as n:
                for par in range(2):
                    load(n + par, par)

        @block.scalar
        def _(act):
            act.wait_ge(scales, 2)

            def quantise(n, par):
                act.wait_ge(x_in[par], 8 * (n - par) + 16)
                act.activation(x_int[:, :, bass.ds(n * FT, FT)], x_rows[:, par], ACT.Copy, scale=inv_x[:, 0:1]
                               ).then_inc(int_ready, 1)

            with act.Fori(0, NFT - 1, 2) as n:
                for par in range(2):
                    quantise(n + par, par)

        @block.vector
        def _(dve):
            dve.tensor_scalar(sx[:], x_max[:], 1.0 / QMAX, 1e-12, ALU.mult, ALU.max).then_inc(scales, 1)
            dve.wait_ge(scales, 1)
            dve.reciprocal(inv_x[:], sx[:]).then_inc(scales, 1)

            def split(n, par):
                dve.wait_ge(int_ready, n + 1)
                wait(dve, gu_done, MT * (n - 1))
                split_ints(dve, x_part, x_int, n, par, part_hi, part_ready)

            def maxima(n, par):
                for mt in range(MT):
                    dve.wait_ge(gu_done, MT * n + mt + 1)
                    out, col = (g_max, mt) if mt < MT // 2 else (u_max, mt - MT // 2)
                    dve.tensor_reduce(out[:, bass.ds(n * (MT // 2) + col, 1)], bank[(par * MT + mt) % 8][:, 0:FT],
                                      AXX, ALU.max, apply_absolute_value=True).then_inc(gu_taken, 1)

            split(0, 0)
            with dve.Fori(0, NFT - 3, 2) as n:
                for par in range(2):
                    split(n + par + 1, 1 - par)
                    maxima(n + par, par)
            split(NFT - 1, 1)
            maxima(NFT - 2, 0)
            maxima(NFT - 1, 1)
            dve.wait_ge(gu_taken, MT * NFT)

        @block.tensor
        def _(pe):
            def products(n, par):
                gate_up_products(pe, bank, gu_w, x_part, par, n, gu_taken,
                                 lambda: pe.wait_ge(part_ready, n + 1), gu_done)

            for n in range(2):
                products(n, n)
            with pe.Fori(2, NFT - 1, 2) as n:
                for par in range(2):
                    products(n + par, par)


def split_ints(eng, x_part, x_int, n, par, part_hi, part_ready):
    ints = x_int[:, :, bass.ds(n * FT, FT)]
    eng.tensor_copy(x_part[0][:, par], ints).then_inc(part_hi, 1)
    eng.wait_ge(part_hi, n + 1)
    eng.tensor_tensor(x_part[1][:, par], ints, x_part[0][:, par].bitcast(F32), ALU.subtract).then_inc(part_ready, 1)


def ffn_gate_up(nc, dram, gu_w, x_int, sx, g_top, u_top, s_g, s_u, p_max):
    with ExitStack() as ctx:
        def sb(name, shape, dt=F32):
            return ctx.enter_context(nc.sbuf_tensor(name, shape, dt))

        def sem(name):
            return ctx.enter_context(nc.semaphore(name))

        tmp = [sb(f"gu_tmp{i}", [128, 1]) for i in range(2)]
        f_g, f_u = sb("f_g", [128, 1]), sb("f_u", [128, 1])
        x_part = [sb(f"gu_part{p}", [128, 2, CH, FT], F32R) for p in range(2)]
        gi, ui = sb("gi", [128, 2, HT, FT], I16), sb("ui", [128, 2, HT, FT], I16)
        sig = sb("sig", [128, HT, FT])
        si = sb("si", [128, HT, FT], U16)
        p = sb("p", [128, 2, HT, FT])
        bank = [ctx.enter_context(nc.psum_tensor(f"gu_bank{i}", [128, 512], F32)) for i in range(8)]
        scales, part_hi, part_ready = sem("gu_scales"), sem("gu_part_hi"), sem("gu_part_ready")
        gu_done, gu_taken = sem("gu2_done"), sem("gu2_taken")
        sig_ready, si_ready, p_ready, p_max_ready = sem("sig_ready"), sem("si_ready"), sem("p_ready"), sem("p_max_ready")
        p_stored = [sem(f"p_stored{i}") for i in range(2)]
        ui_stored = [sem(f"ui_stored{i}") for i in range(2)]
        N_SCALES = 8
        sp_seen = sem("sp_seen")
        block = ctx.enter_context(nc.Block())

        @block.sync
        def _(sp):
            with sp.Fori(0, NFT - 1, 2) as i:
                for par in range(2):
                    n = i + par
                    wait_alone(sp, gu_taken, MT * n + MT, sp_seen)
                    sp.dma_start(dram["ui"][bass.ds(n, 1)].rearrange("b q m t -> q (b m) t"), ui[:, par]
                                 ).then_inc(ui_stored[par], 16)
                    wait_alone(sp, p_ready, n + 1, sp_seen)
                    sp.dma_start(dram["p"][bass.ds(n, 1)].rearrange("b q m t -> q (b m) t"), p[:, par]
                                 ).then_inc(p_stored[par], 16)
            for par in range(2):
                sp.wait_ge(ui_stored[par], 8 * NFT)
                sp.wait_ge(p_stored[par], 8 * NFT)

        @block.scalar
        def _(act):
            act.wait_ge(scales, N_SCALES)

            def tile(n, par):
                wait(act, p_ready, n - 1)
                for mt in range(MT):
                    act.wait_ge(gu_done, MT * n + mt + 1)
                    if mt == HT:
                        wait(act, si_ready, n)
                        act.wait_ge(gu_taken, MT * n + HT)
                        act.activation(sig[:], gi[:, par], ACT.Sigmoid, scale=s_g[:, 0:1]).then_inc(sig_ready, 1)
                        wait(act, ui_stored[par], 8 * (n - par))
                    dst, f = (gi[:, par, mt], f_g) if mt < HT else (ui[:, par, mt - HT], f_u)
                    act.activation(dst, bank[(par * MT + mt) % 8][:, 0:FT], ACT.Copy, scale=f[:, 0:1]
                                   ).then_inc(gu_taken, 1)

            tile(0, 0)
            tile(1, 1)
            with act.Fori(2, NFT - 1, 2) as n:
                for par in range(2):
                    tile(n + par, par)

        @block.vector
        def _(dve):
            chain = Chain(dve, scales)
            for top, s, f, t in ((g_top, s_g, f_g, tmp[0]), (u_top, s_u, f_u, tmp[1])):
                chain.step(dve.tensor_scalar(t[:], top[:], sx[:, 0:1], 1.0 / QMAX, ALU.mult, ALU.mult))
                chain.step(dve.tensor_scalar(s[:], t[:], 1e-12, None, ALU.max))
                chain.step(dve.reciprocal(t[:], s[:]))
                chain.step(dve.tensor_scalar(f[:], t[:], sx[:, 0:1], None, ALU.mult))

            def split(n, par):
                wait(dve, gu_done, MT * (n - 1))
                split_ints(dve, x_part, x_int, n, par, part_hi, part_ready)

            def tile(n, par):
                dve.wait_ge(sig_ready, n + 1)
                dve.tensor_scalar(si[:], sig[:], 65536.0, 65535.0, ALU.mult, ALU.min).then_inc(si_ready, 1)
                dve.wait_ge(si_ready, n + 1)
                wait(dve, p_stored[par], 8 * (n - par))
                dve.tensor_tensor(p[:, par], gi[:, par], si[:], ALU.mult).then_inc(p_ready, 1)
                dve.wait_ge(p_ready, n + 1)
                dve.tensor_reduce(p_max[:, bass.ds(n, 1)], p[:, par].rearrange("q m t -> q (m t)"), AXX, ALU.max,
                                  apply_absolute_value=True).then_inc(p_max_ready, 1)

            split(0, 0)
            split(1, 1)
            tile(0, 0)
            split(2, 0)
            tile(1, 1)
            with dve.Fori(2, NFT - 3, 2) as n:
                for par in range(2):
                    split(n + par + 1, 1 - par)
                    tile(n + par, par)
            split(NFT - 1, 1)
            tile(NFT - 2, 0)
            tile(NFT - 1, 1)
            dve.wait_ge(p_max_ready, NFT)

        @block.tensor
        def _(pe):
            def products(n, par):
                gate_up_products(pe, bank, gu_w, x_part, par, n, gu_taken,
                                 lambda: pe.wait_ge(part_ready, n + 1), gu_done)

            for n in range(2):
                products(n, n)
            with pe.Fori(2, NFT - 1, 2) as n:
                for par in range(2):
                    products(n + par, par)


def ffn_product_max(nc, dram, gs, p_top, s_g, s_3, o_max):
    with ExitStack() as ctx:
        def sb(name, shape, dt=F32):
            return ctx.enter_context(nc.sbuf_tensor(name, shape, dt))

        def sem(name):
            return ctx.enter_context(nc.semaphore(name))

        tmp, f_3 = sb("p_tmp", [128, 1]), sb("f_3", [128, 1])
        p, ui = sb("p_rows", [128, 2, HT, FT]), sb("ui_rows", [128, 2, HT, FT], I16)
        o = sb("o_prod", [128, HT, FT])
        scales, gs_ready, o_ready, o_max_ready = sem("p_scales"), sem("gs_ready"), sem("o_ready"), sem("o_max_ready")
        p_in, ui_in = [sem(f"p_in{i}") for i in range(2)], [sem(f"ui_in{i}") for i in range(2)]
        sp_seen = sem("sp_seen")
        block = ctx.enter_context(nc.Block())

        @block.sync
        def _(sp):
            def load(n, par):
                wait_alone(sp, gs_ready, n - 1, sp_seen)
                sp.dma_start(p[:, par], dram["p"][bass.ds(n, 1)].rearrange("b q m t -> q (b m) t")).then_inc(p_in[par], 16)
                wait_alone(sp, o_ready, 2 * (n - 1), sp_seen)
                sp.dma_start(ui[:, par], dram["ui"][bass.ds(n, 1)].rearrange("b q m t -> q (b m) t")).then_inc(ui_in[par], 16)

            load(0, 0)
            load(1, 1)
            with sp.Fori(2, NFT - 1, 2) as n:
                for par in range(2):
                    load(n + par, par)

        @block.scalar
        def _(act):
            act.wait_ge(scales, 5)
            with act.Fori(0, NFT - 1, 2) as i:
                for par in range(2):
                    n = i + par
                    act.wait_ge(p_in[par], 8 * i + 16)
                    act.activation(gs[:, bass.ds(n, 1)].rearrange("q b m t -> q (b m) t"), p[:, par], ACT.Copy,
                                   scale=f_3[:, 0:1]).then_inc(gs_ready, 1)

        @block.vector
        def _(dve):
            chain = Chain(dve, scales)
            chain.step(dve.tensor_scalar(tmp[:], p_top[:], s_g[:, 0:1], 1.0 / 65536.0, ALU.mult, ALU.mult))
            chain.step(dve.tensor_scalar(s_3[:], tmp[:], 1.0 / QMAX, 1e-12, ALU.mult, ALU.max))
            chain.step(dve.reciprocal(tmp[:], s_3[:]))
            chain.step(dve.tensor_scalar(f_3[:], tmp[:], s_g[:, 0:1], 1.0 / 65536.0, ALU.mult, ALU.mult))
            chain.step(dve.tensor_copy(tmp[:], f_3[:]))

            def tile(n, par):
                dve.wait_ge(gs_ready, n + 1)
                dve.wait_ge(ui_in[par], 8 * (n - par) + 16)
                for half in range(2):
                    m = slice(half * HT // 2, (half + 1) * HT // 2)
                    wait(dve, o_max_ready, 2 * n + half - 1)
                    dve.tensor_tensor(o[:, m], gs[:, bass.ds(n, 1), m].rearrange("q b m t -> q (b m) t"),
                                      ui[:, par, m], ALU.mult).then_inc(o_ready, 1)
                for half in range(2):
                    m = slice(half * HT // 2, (half + 1) * HT // 2)
                    dve.wait_ge(o_ready, 2 * n + half + 1)
                    dve.tensor_reduce(o_max[:, bass.ds(2 * n + half, 1)], o[:, m].rearrange("q m t -> q (m t)"),
                                      AXX, ALU.max, apply_absolute_value=True).then_inc(o_max_ready, 1)

            tile(0, 0)
            tile(1, 1)
            with dve.Fori(2, NFT - 1, 2) as n:
                for par in range(2):
                    tile(n + par, par)
            dve.wait_ge(o_max_ready, 2 * NFT)


def ffn_down(nc, dram, down_w, gs, o_top, s_3, s_u, out):
    with ExitStack() as ctx:
        def sb(name, shape, dt=F32):
            return ctx.enter_context(nc.sbuf_tensor(name, shape, dt))

        def sem(name):
            return ctx.enter_context(nc.semaphore(name))

        tmp, s_4, f_4 = sb("o_tmp", [128, 1]), sb("s_4", [128, 1]), sb("f_4", [128, 1])
        ui, oi = sb("ui_down", [128, 2, HT, DT], I16), sb("oi", [128, 2, HT, DT], I16)
        o_part = [sb(f"o_part{i}", [128, 2, HT, DT], F32R) for i in range(2)]
        h2 = sb("h2_rows", [TOK, 2, 2, D])
        ffn = sb("ffn", [TOK, 2, 2, D])
        res = sb("res", [TOK, 2, 2, D])
        bank = [ctx.enter_context(nc.psum_tensor(f"down_bank{i}", [128, 512], F32)) for i in range(2)]
        scales, oi_ready, hi_ready, lo_ready = sem("o_scales"), sem("oi_ready"), sem("o_hi_ready"), sem("o_lo_ready")
        down_done, ffn_ready, res_ready = sem("down_done"), sem("ffn_ready"), sem("res_ready")
        ui_in, h2_in = [sem(f"uid_in{i}") for i in range(2)], [sem(f"h2_in{i}") for i in range(2)]
        stored = [sem(f"stored{i}") for i in range(2)]
        h2_rows = dram["h2"].rearrange("b t p d -> (b t) p d")
        out_rows = out.rearrange("(g p) d -> g p d", p=TOK)
        sp_seen = sem("sp_seen")
        block = ctx.enter_context(nc.Block())

        @block.sync
        def _(sp):
            def load(n, half):
                k = 2 * n + half
                wait_alone(sp, oi_ready, k - 1, sp_seen)
                sp.dma_start(ui[:, half], dram["ui"][bass.ds(n, 1), :, :, half * DT:(half + 1) * DT].rearrange(
                    "b q m t -> q (b m) t")).then_inc(ui_in[half], 16)
                wait_alone(sp, res_ready, k - 1, sp_seen)
                sp.dma_start(h2[:, half], h2_rows[bass.ds(2 * k, 2)].rearrange("g p d -> p g d")).then_inc(h2_in[half], 16)

            load(0, 0)
            load(0, 1)
            with sp.Fori(1, NFT) as n:
                for half in range(2):
                    load(n, half)

        @block.gpsimd
        def _(pool):
            def tile(n, half):
                k = 2 * n + half
                pool.wait_ge(ffn_ready, k + 1)
                pool.wait_ge(h2_in[half], 16 * n + 16)
                wait(pool, stored[half], 16 * n)
                pool.tensor_tensor(res[:, half], ffn[:, half], h2[:, half], ALU.add).then_inc(res_ready, 1)

            tile(0, 0)
            tile(0, 1)
            with pool.Fori(1, NFT) as n:
                for half in range(2):
                    tile(n, half)

        @block.scalar
        def _(act):
            act.wait_ge(scales, 6)

            def hi(k, half):
                act.wait_ge(oi_ready, k + 1)
                wait(act, down_done, k - 1)
                act.activation(o_part[0][:, half], oi[:, half], ACT.Copy).then_inc(hi_ready, 1)

            def take(k, half):
                act.wait_ge(down_done, k + 1)
                wait(act, res_ready, k - 1)
                act.activation(ffn[:, half].rearrange("p g d -> p (g d)"), bank[half][0:TOK], ACT.Copy,
                               scale=s_4[0:TOK, 0:1]).then_inc(ffn_ready, 1)

            def store(k, half):
                act.wait_ge(res_ready, k + 1)
                act.dma_start(out_rows[bass.ds(2 * k, 2)].rearrange("g p d -> p g d"), res[:, half]).then_inc(stored[half], 16)

            hi(0, 0)
            hi(1, 1)
            take(0, 0)
            hi(2, 0)
            take(1, 1)
            store(0, 0)
            hi(3, 1)
            with act.Fori(2, 2 * NFT - 3, 2) as i:
                for half in range(2):
                    take(i + half, half)
                    store(i + half - 1, 1 - half)
                    hi(i + half + 2, half)
            take(2 * NFT - 2, 0)
            store(2 * NFT - 3, 1)
            take(2 * NFT - 1, 1)
            store(2 * NFT - 2, 0)
            store(2 * NFT - 1, 1)
            for half in range(2):
                act.wait_ge(stored[half], 16 * NFT)

        @block.vector
        def _(dve):
            chain = Chain(dve, scales)
            chain.step(dve.tensor_scalar(tmp[:], o_top[:], s_3[:, 0:1], s_u[:, 0:1], ALU.mult, ALU.mult))
            chain.step(dve.tensor_scalar(s_4[:], tmp[:], 1.0 / QMAX, 1e-12, ALU.mult, ALU.max))
            chain.step(dve.reciprocal(tmp[:], s_4[:]))
            chain.step(dve.tensor_scalar(f_4[:], tmp[:], s_3[:, 0:1], s_u[:, 0:1], ALU.mult, ALU.mult))
            chain.step(dve.tensor_copy(tmp[:], f_4[:]))
            chain.step(dve.tensor_copy(tmp[:], s_4[:]))

            def quantise(n, half):
                k = 2 * n + half
                dve.wait_ge(ui_in[half], 16 * n + 16)
                wait(dve, lo_ready, k - 1)
                dve.scalar_tensor_tensor(oi[:, half], gs[:, bass.ds(n, 1), :, half * DT:(half + 1) * DT].rearrange(
                    "q b m t -> q (b m) t"), f_4[:, 0:1], ui[:, half], ALU.mult, ALU.mult).then_inc(oi_ready, 1)

            def lo(n, half):
                k = 2 * n + half
                dve.wait_ge(hi_ready, k + 1)
                dve.tensor_tensor(o_part[1][:, half], oi[:, half], o_part[0][:, half].bitcast(F32), ALU.subtract
                                  ).then_inc(lo_ready, 1)

            quantise(0, 0)
            with dve.Fori(0, NFT - 1) as n:
                quantise(n, 1)
                lo(n, 0)
                quantise(n + 1, 0)
                lo(n, 1)
            quantise(NFT - 1, 1)
            lo(NFT - 1, 0)
            lo(NFT - 1, 1)

        @block.tensor
        def _(pe):
            def tile(k, half):
                pe.wait_ge(lo_ready, k + 1)
                wait(pe, ffn_ready, k - 1)
                for g in range(2):
                    tok = slice(g * TOK, (g + 1) * TOK)
                    for c in range(HT):
                        for i, (a_, b_) in enumerate(PASSES):
                            mm = pe.matmul(bank[half][0:TOK, g * D:(g + 1) * D], o_part[a_][:, half, c, tok],
                                           down_w[b_][:, c], start=(c == 0 and i == 0), stop=(c == HT - 1 and i == 2))
                mm.then_inc(down_done, 1)

            tile(0, 0)
            tile(1, 1)
            with pe.Fori(2, 2 * NFT - 1, 2) as k:
                for half in range(2):
                    tile(k + half, half)


def build(nc, a, out):
    with ExitStack() as ctx:
        def scalar(name):
            return ctx.enter_context(nc.sbuf_tensor(name, [128, 1], F32))

        x_max, sx, g_top, u_top, s_g, s_u, p_top, s_3, o_top = (
            scalar(x) for x in ("x_max", "sx", "g_top", "u_top", "s_g", "s_u", "p_top", "s_3", "o_top"))
        dram = {"h2": nc.dram_tensor("h2_dram", (B, T, TOK, D), F32, kind="Internal").ap(),
                "xn3T": nc.dram_tensor("xn3T_dram", (128, CH, NTOK), F32, kind="Internal").ap(),
                "ui": nc.dram_tensor("ui_dram", (NFT, 128, HT, FT), I16, kind="Internal").ap(),
                "p": nc.dram_tensor("p_dram", (NFT, 128, HT, FT), F32, kind="Internal").ap()}
        tower(nc, a, dram, x_max)
        with ExitStack() as c1:
            def sb(name, shape, dt=F32):
                return c1.enter_context(nc.sbuf_tensor(name, shape, dt))

            down_w = [sb(f"down_w{p}", [128, NI // 128, D], F32R) for p in range(2)]
            p_max, o_max = sb("p_max", [128, NFT]), sb("o_max", [128, 2 * NFT])
            with ExitStack() as c2:
                gu_w = [c2.enter_context(nc.sbuf_tensor(f"gu_w{p}", [128, CH, 2 * NI], F32R)) for p in range(2)]
                x_int = c2.enter_context(nc.sbuf_tensor("x_int", [128, CH, NTOK], I16))
                g_max = c2.enter_context(nc.sbuf_tensor("g_max", [128, NFT * HT], F32))
                u_max = c2.enter_context(nc.sbuf_tensor("u_max", [128, NFT * HT], F32))
                ffn_weights(nc, a, gu_w, down_w)
                ffn_max(nc, dram, gu_w, x_int, x_max, sx, g_max, u_max)
                all_reduce_max(nc, "gu", ((g_top, g_max[:]), (u_top, u_max[:])))
                ffn_gate_up(nc, dram, gu_w, x_int, sx, g_top, u_top, s_g, s_u, p_max)
            all_reduce_max(nc, "pm", ((p_top, p_max[:]),))
            gs = c1.enter_context(nc.sbuf_tensor("gs", [128, NFT, HT, FT], I16))
            ffn_product_max(nc, dram, gs, p_top, s_g, s_3, o_max)
            all_reduce_max(nc, "om", ((o_top, o_max[:]),))
            ffn_down(nc, dram, down_w, gs, o_top, s_3, s_u, out)


def kernel(x, L0_tok_W1, L0_tok_b1, L0_tok_W2, L0_tok_b2, L0_tok_gamma, L0_tok_beta, L0_tok_adpfactor,
           L0_attn_Wq, L0_attn_bq, L0_attn_Wk, L0_attn_bk, L0_attn_Wv, L0_attn_bv, L0_attn_Wo, L0_attn_bo,
           L0_attn_m, L0_ffn_w_gate, L0_ffn_w_up, L0_ffn_w_down):
    import numpy as np
    import concourse.bacc as bacc
    from concourse.bass_utils import run_bass_kernel_spmd

    def conv_rows(w):
        w = np.asarray(w).reshape(D, CH, 128, J, 2)
        return np.ascontiguousarray(w.transpose(2, 3, 4, 1, 0).reshape(128, J * 2 * CH, D))

    def chunk_rows(w):
        return np.ascontiguousarray(np.asarray(w).reshape(CH, 128, D).transpose(1, 0, 2))

    xT = np.ascontiguousarray(np.asarray(x).reshape(B, N, 2, CH, 128)[:, :, ::-1].transpose(4, 0, 3, 2, 1))
    arrays = {
        "xT": xT, "W1T": conv_rows(L0_tok_W1), "W2T": conv_rows(L0_tok_W2),
        "b1": L0_tok_b1, "b2": L0_tok_b2, "gamma": L0_tok_gamma, "beta": L0_tok_beta,
        "adp": np.asarray(L0_tok_adpfactor).reshape(1),
        "WqT": chunk_rows(L0_attn_Wq), "WkT": chunk_rows(L0_attn_Wk), "WvT": chunk_rows(L0_attn_Wv),
        "WoT": chunk_rows(L0_attn_Wo), "bq": L0_attn_bq, "bk": L0_attn_bk, "bv": L0_attn_bv, "bo": L0_attn_bo,
        "m_rep": np.ascontiguousarray(np.repeat(np.asarray(L0_attn_m), HD).reshape(CH, 128).T),
        "w_gate": L0_ffn_w_gate, "w_up": L0_ffn_w_up, "w_down": L0_ffn_w_down,
    }
    arrays = {k: np.ascontiguousarray(v) for k, v in arrays.items()}
    nc = bacc.Bacc("TRN2", target_bir_lowering=False, num_devices=1)
    a = {k: nc.dram_tensor(f"in_{k}", v.shape, mybir.dt.from_np(v.dtype), kind="ExternalInput").ap()
         for k, v in arrays.items()}
    out = nc.dram_tensor("out", (NTOK, D), F32, kind="ExternalOutput").ap()
    build(nc, a, out)
    r = run_bass_kernel_spmd(nc, [{f"in_{k}": v for k, v in arrays.items()}], core_ids=[0])
    return r.results[0]["out"].reshape(B, N, D)
```

```python
import math
from contextlib import ExitStack

import concourse.bass as bass
from concourse import mybir

F32, F32R = mybir.dt.float32, mybir.dt.float32r
I16, U16, I32 = mybir.dt.int16, mybir.dt.uint16, mybir.dt.int32
ACT = mybir.ActivationFunctionType
ALU = mybir.AluOpType
RMAX = bass.bass_isa.ReduceOp.max
AXX = mybir.AxisListType.X
PASSES = ((0, 0), (0, 1), (1, 0))

B, L, D, KC = 32, 750, 256, 12
PAD = (KC - 2) // 2
N = (L + 2 * PAD - KC) // 2 + 1
CH = D // 128
J = KC // 2
TAPS = 3
GRP = J // TAPS
NW = 2 * CH * GRP
UT = 128
ROWS = 384
KINDS = 3
NPAIR = B // 2
NCT = NPAIR * KINDS
XL = 2 * UT + J
SL = UT + 2
OFF = (PAD + 1) // 2, PAD // 2
T, TOK = 3, N // 3
HEADS, HD = 16, 16
LN_EPS = 1e-5
STREAMS = ((0, 2, ALU.subtract, SL), (1, 3, ALU.subtract, SL - 1), (1, 2, ALU.add, UT),
           (2, 1, ALU.subtract, UT), (4, 5, ALU.add, UT), (5, 4, ALU.subtract, UT))
NS = len(STREAMS)
USES = ((0, 0), (2, 0), (3, 0), (1, 0)), ((1, 1), (4, 0), (5, 0), (0, 2))
NI = 768
BLK = 32
NTOK = B * N
FT = 500
NFT = NTOK // FT
DT = FT // 2
HT = NI // 128
MT = 2 * HT
QMAX = 32767.0


def wait(eng, sem, count):
    if not isinstance(count, int) or count > 0:
        eng.wait_ge(sem, count)


def wait_alone(eng, sem, count, seen):
    if not isinstance(count, int) or count > 0:
        eng.wait_ge(sem, count)
        eng.sem_inc(seen, 1)


def conv_tower(nc, a, dram):
    ctx = ExitStack()

    def sb(name, shape, dt=F32):
        return ctx.enter_context(nc.sbuf_tensor(name, shape, dt))

    def sem(name):
        return ctx.enter_context(nc.semaphore(name))

    RING = 3

    with ctx:
        conv_w = [sb(f"conv_w{p}", [128, NW, 4, 2 * D], F32R) for p in range(2)]
        x_raw = [sb(f"x_raw{i}", [128, 2 * CH, XL]) for i in range(KINDS)]
        stream = sb("stream", [128, 2 * CH, NS, SL])
        s_part = [[sb(f"s_part{p}_{buf}", [128, 2, NS, SL], F32R) for buf in range(RING)] for p in range(2)]
        bias12 = sb("bias12", [128, 2 * D])
        gamma, beta, bias_o = sb("gamma", [128, D]), sb("beta", [128, D]), sb("bias_o", [128, D])
        adp = sb("adp", [128, 1])
        neg_half, eps = sb("neg_half", [128, 2]), sb("eps", [128, 2])
        y = sb("y", [128, 2, 2 * D])
        z, gate = y[:, :, 0:D], y[:, :, D:2 * D]
        hx = sb("hx", [128, 2, 2, 2, D])
        stats = [sb(f"c_stats{i}", [128, 2, 6]) for i in range(2)]
        mv = [sb(f"c_mv{i}", [128, 2, 2]) for i in range(2)]
        var_eps = [sb(f"c_var_eps{i}", [128, 2]) for i in range(2)]
        rstd = [sb(f"c_rstd{i}", [128, 2]) for i in range(2)]
        bank = [ctx.enter_context(nc.psum_tensor(f"conv_bank{i}", [128, 512], F32)) for i in range(8)]

        w_raw = stream[:].rearrange("p c s v -> p (c s v)")[:, 0:2 * 3 * 2 * D].rearrange(
            "p (b t d) -> p b t d", b=2, t=3)
        w_sum = hx[:].rearrange("p b e k d -> p (b e k d)").rearrange("p (k d) -> p k d", k=4)[:, 0:3]

        consts_in, ones_set = sem("c_consts_in"), sem("c_ones_set")
        w_in = [sem(f"w_in{i}") for i in range(2)]
        w_sums, w_hi, w_lo = sem("w_sums"), sem("w_hi"), sem("w_lo")
        zeros_set, tails_set = sem("zeros_set"), sem("tails_set")
        x_in = [sem(f"x_in{i}") for i in range(KINDS)]
        stream_ready, s_hi, s_lo = sem("stream_ready"), sem("s_hi"), sem("s_lo")
        half_done, out_sum, gate_ready, gated = sem("half_done"), sem("out_sum"), sem("gate_ready"), sem("gated")
        stats_ready = [sem(f"c_stats_ready{i}") for i in range(2)]
        mv_ready = [sem(f"c_mv_ready{i}") for i in range(2)]
        veps_ready = [sem(f"c_veps_ready{i}") for i in range(2)]
        rstd_ready = [sem(f"c_rstd_ready{i}") for i in range(2)]
        z_norm, z_gamma, z_beta, sigz_ready = sem("z_norm"), sem("z_gamma"), sem("z_beta"), sem("sigz_ready")
        h_ready, xn_ready, h_bo_ready = sem("h_ready"), sem("c_xn_ready"), sem("h_bo_ready")
        hx_stored = [sem(f"hx_stored{i}") for i in range(2)]
        sp_seen, dve_seen = sem("c_sp_seen"), sem("c_dve_seen")

        def steps(run, eng, lag):
            for s in range(2 * KINDS):
                run(s, s // KINDS, s, True, s >= lag)
            with eng.Fori(2, NPAIR - 1, 2) as pair:
                for k in range(2 * KINDS):
                    run(pair * KINDS + k, pair + k // KINDS, k, True, True)
            for s in range(NCT, NCT + lag):
                run(s, None, s % (2 * KINDS), False, True)

        def ring(k, c):
            return (CH * k + c) % RING

        def x_pieces(pair, kind):
            first = 2 * UT * kind
            for ph in range(2):
                for b in range(2):
                    lo = max(first, b * ROWS + OFF[ph])
                    hi = min(first + XL, b * ROWS + OFF[ph] + N)
                    if lo < hi:
                        yield lo - first, ph, 2 * pair + b, lo - b * ROWS - OFF[ph], hi - lo

        N_PIECES = [len(list(x_pieces(0, kind))) for kind in range(KINDS)]
        block = ctx.enter_context(nc.Block())

        @block.sync
        def _(sp):
            def load_w(g):
                if g >= 2:
                    sp.wait_ge(w_lo, 4 * (g - 1))
                for i, name in enumerate(("W1T", "W2T")):
                    sp.dma_start(w_raw[:, g % 2, :, i * D:(i + 1) * D], a[name][:, g]).then_inc(w_in[g % 2], 16)

            def load_x(pair, kind):
                for col, ph, batch, n0, n in x_pieces(pair, kind):
                    sp.dma_start(x_raw[kind][:, ph:2 * CH:2, col:col + n],
                                 a["xT"][:, bass.ds(batch, 1), :, ph, n0:n0 + n].rearrange("p b c n -> p (b c) n")
                                 ).then_inc(x_in[kind], 16)

            load_w(0)
            load_w(1)
            sp.wait_ge(zeros_set, KINDS)
            for kind in range(KINDS):
                load_x(0, kind)
            for g in range(2, NW):
                load_w(g)

            def reload(pair, kind):
                wait_alone(sp, stream_ready, CH * (KINDS * (pair - 1) + kind + 1), sp_seen)
                load_x(pair, kind)

            def store(s, par):
                wait_alone(sp, xn_ready, 2 * s + 2, sp_seen)
                wait_alone(sp, h_bo_ready, s + 1, sp_seen)
                sp.dma_start(dram["hx"][bass.ds(s, 1)].rearrange("s p e k d -> p (s e) k d"), hx[:, par]
                             ).then_inc(hx_stored[par], 16)

            for kind in range(KINDS):
                reload(1, kind)
            with sp.Fori(2, NPAIR - 1, 2) as pair:
                for k in range(2 * KINDS):
                    reload(pair + k // KINDS, k % KINDS)
                    store((pair - 2) * KINDS + k, k % 2)
            for s in range(NCT - 2 * KINDS, NCT):
                store(s, s % 2)
            for par in range(2):
                sp.wait_ge(hx_stored[par], 16 * NCT // 2)

        @block.scalar
        def _(act):
            for dst, src in ((bias12[:, 0:D], a["b1"]), (bias12[:, D:2 * D], a["b2"]), (gamma[:], a["gamma"]),
                             (beta[:], a["beta"]), (bias_o[:], a["bo"]), (adp[:], a["adp"])):
                act.dma_start(dst, src.rearrange("(o n) -> o n", o=1).broadcast_to([128, src.shape[0]])
                              ).then_inc(consts_in, 16)
            for g in range(NW):
                raw = w_raw[:, g % 2]
                for k, (src, scale) in enumerate(((raw[:, 0], 1.0), (raw[:, 2], 1.0), (w_sum[:, 1], 0.5), (w_sum[:, 2], 0.5))):
                    if k == 0:
                        act.wait_ge(w_in[g % 2], 32 * (g // 2 + 1))
                    if k == 2:
                        act.wait_ge(w_sums, 3 * g + 3)
                    act.activation(conv_w[0][:, g, (0, 3, 1, 2)[k]], src, ACT.Copy, scale=scale).then_inc(w_hi, 1)
            act.wait_ge(consts_in, 6 * 16)

            def high(s, k, c):
                act.wait_ge(stream_ready, CH * s + c + 1)
                wait(act, half_done, CH * s + c - RING + 1)
                act.activation(s_part[0][ring(k, c)][:], stream[:, 2 * c:2 * c + 2], ACT.Copy).then_inc(s_hi, 1)

            def run(s, pair, k, start, end):
                f = s - 2
                if start:
                    high(s, k, 0)
                if end:
                    act.wait_ge(out_sum, 5 * f + 5)
                    act.activation(gate, gate, ACT.Sigmoid, scale=adp[:, 0:1]).then_inc(gate_ready, 1)
                if start:
                    high(s, k, 1)
                if end:
                    act.wait_ge(z_beta, f + 1)
                    act.activation(gate, z, ACT.Sigmoid).then_inc(sigz_ready, 1)

            steps(run, act, 2)

        @block.gpsimd
        def _(pool):
            pool.memset(neg_half[:], -0.5).then_inc(ones_set, 1)
            pool.memset(eps[:], LN_EPS).then_inc(ones_set, 1)
            pool.wait_ge(ones_set, 2)
            for g in range(NW):
                raw = w_raw[:, g % 2]
                pool.wait_ge(w_in[g % 2], 32 * (g // 2 + 1))
                if g:
                    pool.wait_ge(w_lo, 4 * g)
                pool.tensor_tensor(w_sum[:, 0], raw[:, 0], raw[:, 2], ALU.add).then_inc(w_sums, 1)
                pool.wait_ge(w_sums, 3 * g + 1)
                pool.tensor_tensor(w_sum[:, 1], w_sum[:, 0], raw[:, 1], ALU.add).then_inc(w_sums, 1)
                pool.tensor_tensor(w_sum[:, 2], w_sum[:, 0], raw[:, 1], ALU.subtract).then_inc(w_sums, 1)
            pool.wait_ge(w_lo, 4 * NW)
            pool.memset(stream[:, :, :, UT:SL], 0.0).then_inc(tails_set, 1)
            pool.wait_ge(tails_set, 1)
            pool.wait_ge(consts_in, 6 * 16)

            def streams(s, pair, k, c):
                if c == 0:
                    pool.wait_ge(x_in[k % KINDS], (pair + 1) * (16 * N_PIECES[k % KINDS]))
                wait(pool, s_lo, CH * (s - 1) + c + 1)
                for i, (p, q, op, n) in enumerate(STREAMS):
                    ins = pool.tensor_tensor(stream[:, 2 * c:2 * c + 2, i, 0:n],
                                             x_raw[k % KINDS][:, 2 * c:2 * c + 2, p:p + 2 * n - 1:2],
                                             x_raw[k % KINDS][:, 2 * c:2 * c + 2, q:q + 2 * n - 1:2], op)
                ins.then_inc(stream_ready, 1)

            def inv_std(i, s):
                pool.wait_ge(mv_ready[i], 2 * s + 2)
                pool.tensor_tensor(var_eps[i][:], mv[i][:, :, 1], eps[:], ALU.add).then_inc(veps_ready[i], 1)
                pool.wait_ge(veps_ready[i], s + 1)
                pool.tensor_tensor(rstd[i][:], var_eps[i][:], neg_half[:], ALU.pow).then_inc(rstd_ready[i], 1)

            def finish(s, par):
                inv_std(0, s)
                pool.wait_ge(z_norm, 2 * s + 2)
                pool.tensor_tensor(z, z, gamma[:, None, :].broadcast_to([128, 2, D]), ALU.mult).then_inc(z_gamma, 1)
                pool.wait_ge(z_gamma, s + 1)
                pool.tensor_tensor(z, z, beta[:, None, :].broadcast_to([128, 2, D]), ALU.add).then_inc(z_beta, 1)
                inv_std(1, s)
                pool.wait_ge(xn_ready, 2 * s + 2)
                pool.tensor_tensor(hx[:, par, :, 0], hx[:, par, :, 0], bias_o[:, None, :].broadcast_to([128, 2, D]),
                                   ALU.add).then_inc(h_bo_ready, 1)

            def run(s, pair, k, start, end):
                if start:
                    streams(s, pair, k, 0)
                if end:
                    finish(s - 3, (k - 3) % 2)
                if start:
                    streams(s, pair, k, 1)

            steps(run, pool, 3)

        @block.vector
        def _(dve):
            for kind in range(KINDS):
                dve.memset(x_raw[kind][:], 0.0).then_inc(zeros_set, 1)
            for g in range(NW):
                raw = w_raw[:, g % 2]
                for k, (src, scale) in enumerate(((raw[:, 0], 1.0), (raw[:, 2], 1.0), (w_sum[:, 1], 0.5), (w_sum[:, 2], 0.5))):
                    f = (0, 3, 1, 2)[k]
                    dve.wait_ge(w_hi, 4 * g + k + 1)
                    dve.scalar_tensor_tensor(conv_w[1][:, g, f], src, scale, conv_w[0][:, g, f].bitcast(F32),
                                             ALU.mult, ALU.subtract).then_inc(w_lo, 1)
            dve.wait_ge(consts_in, 6 * 16)

            def low(s, k, c):
                dve.wait_ge(s_hi, CH * s + c + 1)
                dve.tensor_tensor(s_part[1][ring(k, c)][:], stream[:, 2 * c:2 * c + 2],
                                  s_part[0][ring(k, c)][:].bitcast(F32), ALU.subtract).then_inc(s_lo, 1)

            def layer_stats(i, s, src):
                for e in range(2):
                    dve.bn_stats(stats[i][:, e], src[:, e]).then_inc(stats_ready[i], 1)
                wait_alone(dve, stats_ready[i], 2 * s + 2, dve_seen)
                for e in range(2):
                    dve.bn_aggr(mv[i][:, e], stats[i][:, e]).then_inc(mv_ready[i], 1)

            def layer_norm(i, s, dst, src, ready):
                dve.wait_ge(rstd_ready[i], s + 1)
                for e in range(2):
                    dve.tensor_scalar(dst[:, e], src[:, e], mv[i][:, e, 0:1], rstd[i][:, e:e + 1],
                                      ALU.subtract, ALU.mult).then_inc(ready, 1)

            def take(s, par):
                m = bank[4 * par:4 * par + 4]
                dve.wait_ge(half_done, CH * s + CH)
                dve.tensor_tensor(y[:, 0], m[1][:], bias12[:], ALU.add).then_inc(out_sum, 1)
                dve.wait_ge(out_sum, 5 * s + 1)
                dve.tensor_tensor(y[:, 1], y[:, 0], m[2][:], ALU.subtract).then_inc(out_sum, 1)
                dve.wait_ge(out_sum, 5 * s + 2)
                dve.tensor_tensor(y[:, 0], m[2][:], y[:, 0], ALU.add).then_inc(out_sum, 1)
                dve.tensor_tensor(y[:, 1], y[:, 1], m[3][:], ALU.subtract).then_inc(out_sum, 1)
                dve.wait_ge(out_sum, 5 * s + 3)
                dve.tensor_tensor(y[:, 0], m[0][:], y[:, 0], ALU.add).then_inc(out_sum, 1)
                dve.wait_ge(gate_ready, s + 1)
                dve.tensor_tensor(z, z, gate, ALU.mult).then_inc(gated, 1)
                dve.wait_ge(gated, s + 1)
                layer_stats(0, s, z)
                layer_norm(0, s, z, z, z_norm)

            def finish(s, par):
                dve.wait_ge(sigz_ready, s + 1)
                wait(dve, hx_stored[par], 8 * (s - par))
                h = hx[:, par, :, 0]
                dve.tensor_tensor(h, z, gate, ALU.mult).then_inc(h_ready, 1)
                dve.wait_ge(h_ready, s + 1)
                layer_stats(1, s, h)
                layer_norm(1, s, hx[:, par, :, 1], h, xn_ready)

            def run(s, pair, k, start, end):
                if start:
                    low(s, k, 0)
                if end:
                    take(s - 2, k % 2)
                if start:
                    low(s, k, 1)
                if end:
                    finish(s - 2, k % 2)

            steps(run, dve, 2)

        @block.tensor
        def _(pe):
            def conv(s, k):
                m = bank[4 * (k % 2):4 * (k % 2) + 4]
                wait(pe, out_sum, 5 * (s - 1))
                for c in range(CH):
                    pe.wait_ge(s_lo, CH * s + c + 1)
                    for w in range(2 * GRP * c, 2 * GRP * (c + 1)):
                        if isinstance(s, int) and s == 0:
                            pe.wait_ge(w_lo, 4 * (w + 1))
                        ph, grp = w // GRP % 2, w % GRP
                        for f, (st, shift) in enumerate(USES[grp]):
                            for i, (a_, b_) in enumerate(PASSES):
                                mm = pe.matmul(m[f][:], s_part[a_][ring(k, c)][:, ph, st, shift:shift + UT],
                                               conv_w[b_][:, w, f], start=(w == 0 and i == 0),
                                               stop=(w == NW - 1 and i == 2))
                    mm.then_inc(half_done, 1)

            for s in range(2 * KINDS):
                conv(s, s)
            with pe.Fori(2, NPAIR - 1, 2) as pair:
                for k in range(2 * KINDS):
                    conv(pair * KINDS + k, k)


def attention(nc, a, dram, x_max):
    ctx = ExitStack()

    def sb(name, shape, dt=F32):
        return ctx.enter_context(nc.sbuf_tensor(name, shape, dt))

    def sem(name):
        return ctx.enter_context(nc.semaphore(name))

    with ctx:
        NH3 = T * 2 * HEADS
        qkv_w_raw = sb("qkv_w_raw", [128, CH, 3 * D])
        qkv_w = [sb(f"qkv_w{p}", [128, CH, 3 * D], F32R) for p in range(2)]
        wo = sb("wo", [128, CH, D])
        bias_qkv = sb("bias_qkv", [128, 3 * D])
        m_rep, m_exp, n_base, inv_scaling = (sb(x, [128, CH]) for x in ("m_rep", "m_exp", "n_base", "inv_scaling"))
        neg_half, eps = sb("a_neg_half", [128, T]), sb("a_eps", [128, T])
        ident, block_ones = sb("ident", [128, 128]), sb("block_ones", [128, 128])
        head_mask = sb("head_mask", [128, CH, 128])
        xn = sb("xn", [TOK, 2, T, D])
        h_bo = sb("h_bo", [TOK, 2, T, D])
        xnT = [[sb(f"xnT{p}_{i}", [128, CH, N], F32R) for i in range(2)] for p in range(2)]
        qk = sb("qk", [TOK, 2, T, 2 * D])
        v = sb("v", [TOK, 2, T, D])
        qk_sq = sb("qk_sq", [TOK, T, 2 * D])
        norm2, inv_norm, nr = sb("norm2", [TOK, NH3]), sb("inv_norm", [TOK, 2, NH3]), sb("nr", [TOK, NH3])
        qT = sb("qT", [128, 2, CH, N])
        head_m = sb("head_m", [128, 2, CH, 128])
        m_wo = sb("m_wo", [128, CH, D])
        h2 = sb("h2", [TOK, 2, T, D])
        xn3 = sb("xn3", [TOK, 2, T, D])
        xn3T = sb("xn3T", [128, 2, CH, N])
        stats, mv = sb("a_stats", [TOK, T, 6]), sb("a_mv", [TOK, T, 2])
        var_eps, rstd, shift = sb("a_var_eps", [TOK, T]), sb("a_rstd", [TOK, 2, T]), sb("a_shift", [TOK, 2, T])
        x_amax, x_amax1 = sb("x_amax", [128, B]), sb("x_amax1", [128, 1])

        bank = [ctx.enter_context(nc.psum_tensor(f"att_bank{i}", [128, 512], F32)) for i in range(8)]
        XNT, QT = bank[0:2], bank[0:2]
        QK = bank[2], bank[4], bank[5]
        V01, V2, MWO, HEADM = bank[3], bank[6], bank[7], bank[5]
        XN3T = bank[2], bank[4]
        ATT = bank[3], bank[6]

        consts_in, set_, built, m_steps = sem("a_consts_in"), sem("a_set"), sem("a_built"), sem("m_steps")
        qkv_w_hi, qkv_w_lo = sem("qkv_w_hi"), sem("qkv_w_lo")
        xn_in, h_in = [sem(f"xn_in{i}") for i in range(2)], [sem(f"h_in{i}") for i in range(2)]
        xnT_done, xnT_hi, xnT_lo = sem("xnT_done"), sem("xnT_hi"), sem("xnT_lo")
        qk_done, v_done, qk_ready, v_ready = sem("qk_done"), sem("v_done"), sem("qk_ready"), sem("v_ready")
        sq_ready, norm2_ready, newton, inv_ready, root_ready = sem("sq_ready"), sem("norm2_ready"), sem("newton"), sem("inv_ready"), sem("root_ready")
        qkn_ready, qT_done, qT_ready = sem("qkn_ready"), sem("qT_done"), sem("qT_ready")
        headm_done, headm_ready, mwo_done, mwo_ready = (
            sem(x) for x in ("headm_done", "headm_ready", "mwo_done", "mwo_ready"))
        att_done, h2_ready, stats_ready, mv_ready = (sem(x) for x in ("att_done", "h2_ready", "a_stats_ready", "a_mv_ready"))
        veps_ready, rstd_ready, shift_ready, xn3_ready = (
            sem(x) for x in ("a_veps_ready", "a_rstd_ready", "shift_ready", "xn3_ready"))
        xn3T_done, xn3T_ready, x_amax_ready = sem("xn3T_done"), sem("xn3T_ready"), sem("x_amax_ready")
        h2_stored, xn3T_stored = [sem(f"h2_stored{i}") for i in range(2)], [sem(f"xn3T_stored{i}") for i in range(2)]
        sp_seen, dve_seen = sem("a_sp_seen"), sem("a_dve_seen")
        N_CONSTS = 8


        def steps(run, eng, last=4):
            for s in range(6):
                run(s, s % 2, lambda k, s=s: s >= k)
            with eng.Fori(6, B - 1, 2) as i:
                for par in range(2):
                    run(i + par, par, lambda k: True)
            for s in range(B, B + last):
                run(s, s % 2, lambda k, s=s: s - k < B)

        def stored(par, count):
            return 8 * (count - par)

        block = ctx.enter_context(nc.Block())

        @block.sync
        def _(sp):
            rows = dram["hx"].rearrange("s p e k d -> (s p e) k d").rearrange("(b n) k d -> b n k d", n=ROWS)

            def load(dst, n, k, sem_):
                sp.dma_start(dst, rows[bass.ds(n, 1), 0:N, k].rearrange("b (t p) d -> p (b t) d", p=TOK)
                             ).then_inc(sem_, 16)

            def run(s, par, has):
                if has(0):
                    wait_alone(sp, xnT_done, 2 * (s - 1), sp_seen)
                    load(xn[:, par], s, 1, xn_in[par])
                if has(2):
                    wait_alone(sp, h2_ready, 2 * (s - 3), sp_seen)
                    load(h_bo[:, par], s - 2, 0, h_in[par])
                if has(4):
                    m = s - 4
                    wait_alone(sp, h2_ready, 2 * m + 2, sp_seen)
                    sp.dma_start(dram["h2"][bass.ds(m, 1)].rearrange("b t p d -> p (b t) d"), h2[:, par]
                                 ).then_inc(h2_stored[par], 16)
                if has(5):
                    m, mp = s - 5, 1 - par
                    wait_alone(sp, xn3T_ready, 2 * m + 2, sp_seen)
                    sp.dma_start(dram["xn3T"][:, :, bass.ds(m * N, N)], xn3T[:, mp]).then_inc(xn3T_stored[mp], 16)

            steps(run, sp, 5)
            for par in range(2):
                sp.wait_ge(h2_stored[par], 8 * B)
                sp.wait_ge(xn3T_stored[par], 8 * B)

        @block.scalar
        def _(act):
            for i, name in enumerate(("WqT", "WkT", "WvT")):
                act.dma_start(qkv_w_raw[:, :, i * D:(i + 1) * D], a[name]).then_inc(consts_in, 16)
            act.dma_start(wo[:], a["WoT"]).then_inc(consts_in, 16)
            act.dma_start(m_rep[:], a["m_rep"]).then_inc(consts_in, 16)
            for i, name in enumerate(("bq", "bk", "bv")):
                act.dma_start(bias_qkv[:, i * D:(i + 1) * D], a[name].rearrange("(o n) -> o n", o=1).broadcast_to([128, D])
                              ).then_inc(consts_in, 16)
            act.wait_ge(consts_in, 16 * N_CONSTS)
            act.activation(m_exp[:], m_rep[:], ACT.Sigmoid).then_inc(m_steps, 1)
            act.activation(qkv_w[0][:], qkv_w_raw[:], ACT.Copy).then_inc(qkv_w_hi, 1)

            def run(s, par, has):
                if has(0):
                    wait(act, v_done, 3 * (s - 1))
                    for c in range(CH):
                        act.wait_ge(xnT_done, 2 * s + c + 1)
                        act.activation(xnT[0][par][:, c], XNT[c][:, 0:N], ACT.Copy).then_inc(xnT_hi, 1)
                if has(4):
                    m = s - 4
                    act.wait_ge(shift_ready, m + 1)
                    wait(act, xn3T_done, 2 * (m - 1))
                    for t in range(T):
                        act.activation(xn3[:, par, t], h2[:, par, t], ACT.Identity, scale=rstd[:, par, t:t + 1],
                                       bias=shift[:, par, t:t + 1]).then_inc(xn3_ready, 1)
                if has(1):
                    n, np_ = s - 1, 1 - par
                    wait(act, norm2_ready, 4 * n)
                    for t in range(T):
                        act.wait_ge(qk_ready, 3 * n + t + 1)
                        act.activation(qk_sq[:, t], qk[:, np_, t], ACT.Square).then_inc(sq_ready, 1)
                if has(3):
                    m = s - 3
                    act.wait_ge(mwo_done, m + 1)
                    wait(act, att_done, 2 * m)
                    act.activation(m_wo[:].rearrange("p c d -> p (c d)"), MWO[:], ACT.Copy).then_inc(mwo_ready, 1)
                if has(4):
                    m = s - 4
                    wait(act, xn3T_stored[par], stored(par, m))
                    wait(act, x_amax_ready, m - 1)
                    for c in range(CH):
                        act.wait_ge(xn3T_done, 2 * m + c + 1)
                        act.activation(xn3T[:, par, c], XN3T[c][:, 0:N], ACT.Copy).then_inc(xn3T_ready, 1)
                if has(1):
                    n = s - 1
                    act.wait_ge(norm2_ready, 4 * n + 4)
                    act.activation(nr[:], norm2[:], ACT.Sqrt).then_inc(root_ready, 1)
                if has(2):
                    n = s - 2
                    wait(act, att_done, 2 * (n - 1))
                    for c in range(CH):
                        act.wait_ge(qT_done, 2 * n + c + 1)
                        act.activation(qT[:, par, c], QT[c][:, 0:N], ACT.Copy).then_inc(qT_ready, 1)

            steps(run, act)

        @block.gpsimd
        def _(pool):
            for tile, value in ((ident, 0.0), (block_ones, 1.0), (neg_half, -0.5), (eps, LN_EPS), (n_base, float(N))):
                pool.memset(tile[:], value).then_inc(set_, 1)
            pool.wait_ge(set_, 5)
            pool.affine_select(out=ident[:], in_=ident[:], compare_op=ALU.not_equal, fill=1.0, base=0,
                               pattern=[[-1, 128]], channel_multiplier=1).then_inc(built, 1)
            heads = block_ones[:].rearrange("p (j r) -> p j r", r=HD)
            pool.affine_select(out=heads, in_=heads, compare_op=ALU.is_ge, fill=0.0, base=0,
                               pattern=[[-HD, 128 // HD], [0, HD]], channel_multiplier=1).then_inc(built, 1)
            pool.wait_ge(built, 2)
            pool.affine_select(out=heads, in_=heads, compare_op=ALU.is_ge, fill=0.0, base=HD - 1,
                               pattern=[[HD, 128 // HD], [0, HD]], channel_multiplier=-1).then_inc(built, 1)
            pool.wait_ge(m_steps, 1)
            pool.tensor_scalar(m_exp[:], m_exp[:], -1.0, None, ALU.mult).then_inc(m_steps, 1)
            pool.wait_ge(m_steps, 2)
            pool.tensor_tensor(inv_scaling[:], n_base[:], m_exp[:], ALU.pow).then_inc(m_steps, 1)
            pool.wait_ge(m_steps, 3)
            pool.wait_ge(built, 3)
            for c in range(CH):
                pool.tensor_scalar(head_mask[:, c], block_ones[:], inv_scaling[:, c:c + 1], None, ALU.mult
                                   ).then_inc(m_steps, 1)

            def run(s, par, has):
                if has(1):
                    n, np_ = s - 1, 1 - par
                    pool.wait_ge(inv_ready, n + 1)
                    rows = qk[:, np_].rearrange("p t (h e) -> p (t h) e", e=HD)
                    pool.tensor_tensor(rows, rows, inv_norm[:, np_, :, None].broadcast_to([TOK, NH3, HD]), ALU.mult
                                       ).then_inc(qkn_ready, 1)
                if has(3):
                    m, mp = s - 3, 1 - par
                    pool.wait_ge(mv_ready, 3 * m + 3)
                    pool.tensor_tensor(var_eps[:], mv[:, :, 1], eps[0:TOK], ALU.add).then_inc(veps_ready, 1)
                    pool.wait_ge(veps_ready, m + 1)
                    wait(pool, xn3_ready, 3 * (m - 1))
                    pool.tensor_tensor(rstd[:, mp], var_eps[:], neg_half[0:TOK], ALU.pow).then_inc(rstd_ready, 1)

            steps(run, pool)
            pool.wait_ge(x_amax_ready, B + 1)
            pool.partition_all_reduce(x_max[:], x_amax1[:], 128, RMAX).then_inc(built, 1)
            pool.wait_ge(built, 4)

        @block.vector
        def _(dve):
            dve.wait_ge(qkv_w_hi, 1)
            dve.tensor_tensor(qkv_w[1][:], qkv_w_raw[:], qkv_w[0][:].bitcast(F32), ALU.subtract).then_inc(qkv_w_lo, 1)
            dve.wait_ge(consts_in, 16 * N_CONSTS)
            dve.wait_ge(m_steps, 5)

            def run(s, par, has):
                if has(0):
                    for c in range(CH):
                        dve.wait_ge(xnT_hi, 2 * s + c + 1)
                        dve.tensor_tensor(xnT[1][par][:, c], XNT[c][:, 0:N], xnT[0][par][:, c].bitcast(F32),
                                          ALU.subtract).then_inc(xnT_lo, 1)
                if has(4):
                    dve.wait_ge(rstd_ready, s - 3)
                    dve.scalar_tensor_tensor(shift[:, par], mv[:, :, 0], -1.0, rstd[:, par], ALU.mult, ALU.mult
                                             ).then_inc(shift_ready, 1)
                if has(1):
                    n, np_ = s - 1, 1 - par
                    wait(dve, headm_done, n - 1)
                    for t in range(T):
                        dve.wait_ge(qk_done, 3 * n + t + 1)
                        dve.tensor_tensor(qk[:, np_, t], QK[t][0:TOK], bias_qkv[0:TOK, 0:2 * D], ALU.add
                                          ).then_inc(qk_ready, 1)
                    dve.wait_ge(v_done, 3 * n + 2)
                    dve.tensor_tensor(v[:, np_, 0:2], V01[0:TOK].rearrange("p (t d) -> p t d", t=2),
                                      bias_qkv[0:TOK, None, 2 * D:3 * D].broadcast_to([TOK, 2, D]), ALU.add
                                      ).then_inc(v_ready, 1)
                    wait(dve, inv_ready, n)
                    for t in range(T):
                        half = slice(t * 2 * HEADS, (t + 1) * 2 * HEADS)
                        dve.wait_ge(sq_ready, 3 * n + t + 1)
                        dve.tensor_reduce(norm2[:, half], qk_sq[:, t].rearrange("p (h e) -> p h e", e=HD), AXX, ALU.add
                                          ).then_inc(norm2_ready, 1)
                    dve.wait_ge(norm2_ready, 4 * n + 3)
                    dve.tensor_scalar(norm2[:], norm2[:], 1e-24, None, ALU.max).then_inc(norm2_ready, 1)
                    dve.wait_ge(v_done, 3 * n + 3)
                    dve.tensor_tensor(v[:, np_, 2], V2[0:TOK, 0:D], bias_qkv[0:TOK, 2 * D:3 * D], ALU.add
                                      ).then_inc(v_ready, 1)
                    inv = inv_norm[:, np_]
                    dve.wait_ge(root_ready, n + 1)
                    dve.reciprocal(inv, nr[:]).then_inc(newton, 1)
                    dve.wait_ge(newton, 3 * n + 1)
                    dve.tensor_tensor(nr[:], inv, inv, ALU.mult).then_inc(newton, 1)
                    dve.wait_ge(newton, 3 * n + 2)
                    dve.scalar_tensor_tensor(nr[:], nr[:], -0.5, norm2[:], ALU.mult, ALU.mult).then_inc(newton, 1)
                    dve.wait_ge(newton, 3 * n + 3)
                    dve.scalar_tensor_tensor(inv, nr[:], 1.5, inv, ALU.add, ALU.mult).then_inc(inv_ready, 1)
                if has(4):
                    m = s - 4
                    dve.wait_ge(xn3T_ready, 2 * m + 2)
                    dve.tensor_reduce(x_amax[:, bass.ds(m, 1)], xn3T[:, par].rearrange("p c n -> p (c n)"), AXX, ALU.max,
                                      apply_absolute_value=True).then_inc(x_amax_ready, 1)
                if has(2):
                    n = s - 2
                    wait(dve, mwo_done, n - 1)
                    dve.wait_ge(headm_done, n + 1)
                    dve.tensor_tensor(head_m[:, par].rearrange("p c q -> p (c q)"), HEADM[:, 0:D],
                                      head_mask[:].rearrange("p c q -> p (c q)"), ALU.mult).then_inc(headm_ready, 1)
                if has(3):
                    m, mp = s - 3, 1 - par
                    wait(dve, h2_stored[mp], stored(mp, m))
                    wait(dve, xn3_ready, 3 * (m - 1))
                    dve.wait_ge(h_in[mp], stored(mp, m) + 16)
                    dve.wait_ge(att_done, 2 * m + 2)
                    dve.tensor_tensor(h2[:, mp, 0:2], ATT[0][0:TOK].rearrange("p (t d) -> p t d", t=2),
                                      h_bo[:, mp, 0:2], ALU.add).then_inc(h2_ready, 1)
                    dve.tensor_tensor(h2[:, mp, 2], ATT[1][0:TOK, 0:D], h_bo[:, mp, 2], ALU.add).then_inc(h2_ready, 1)
                    dve.wait_ge(h2_ready, 2 * m + 2)
                    for t in range(T):
                        dve.bn_stats(stats[:, t], h2[:, mp, t]).then_inc(stats_ready, 1)
                    wait_alone(dve, stats_ready, 3 * m + 3, dve_seen)
                    for t in range(T):
                        dve.bn_aggr(mv[:, t], stats[:, t]).then_inc(mv_ready, 1)

            steps(run, dve)
            dve.wait_ge(x_amax_ready, B)
            dve.tensor_reduce(x_amax1[:], x_amax[:], AXX, ALU.max).then_inc(x_amax_ready, 1)

        @block.tensor
        def _(pe):
            def transposes(dst, src, done):
                for c in range(CH):
                    for t in range(T):
                        tr = pe.transpose(dst[c][:, t * TOK:(t + 1) * TOK], src[:, t, c * 128:(c + 1) * 128],
                                          ident[0:TOK, 0:TOK])
                    tr.then_inc(done, 1)

            def qkv(n, par):
                pe.wait_ge(xnT_lo, 2 * n + 2)
                wait(pe, xn3T_ready, 2 * (n - 3))
                wait(pe, headm_ready, n - 1)

                def product(dst, t, lo, hi, done):
                    for c in range(CH):
                        for i, (a_, b_) in enumerate(PASSES):
                            mm = pe.matmul(dst, xnT[a_][par][:, c, t * TOK:(t + 1) * TOK], qkv_w[b_][:, c, lo:hi],
                                           start=(c == 0 and i == 0), stop=(c == CH - 1 and i == 2))
                    mm.then_inc(done, 1)

                for t in range(T):
                    product(QK[t][0:TOK], t, 0, 2 * D, qk_done)
                wait(pe, h2_ready, 2 * (n - 2))
                for t in range(T):
                    product(V2[0:TOK, 0:D] if t == 2 else V01[0:TOK, t * D:(t + 1) * D], t, 2 * D, 3 * D, v_done)

            pe.wait_ge(built, 1)
            pe.wait_ge(consts_in, 16 * N_CONSTS)
            pe.wait_ge(qkv_w_lo, 1)

            def run(s, par, has):
                if has(0):
                    pe.wait_ge(xn_in[par], stored(par, s) + 16)
                    wait(pe, qT_ready, 2 * (s - 2))
                    if not has(3):
                        wait(pe, xnT_lo, 2 * s)
                    transposes(XNT, xn[:, par], xnT_done)
                if has(1):
                    if not has(4):
                        wait(pe, qk_ready, 3 * (s - 1))
                        wait(pe, v_ready, 2 * (s - 1))
                    qkv(s - 1, 1 - par)
                if has(3):
                    m, mp = s - 3, 1 - par
                    pe.wait_ge(headm_ready, m + 1)
                    wait(pe, mwo_ready, m)
                    for c in range(CH):
                        mm = pe.matmul(MWO[:, c * D:(c + 1) * D], head_m[:, mp, c], wo[:, c], start=True, stop=True)
                    mm.then_inc(mwo_done, 1)
                if has(4):
                    m = s - 4
                    pe.wait_ge(xn3_ready, 3 * m + 3)
                    if has(1):
                        pe.wait_ge(qk_ready, 3 * (s - 1) + 2)
                    transposes(XN3T, xn3[:, par], xn3T_done)
                if has(2):
                    n = s - 2
                    pe.wait_ge(qkn_ready, n + 1)
                    if has(0):
                        pe.wait_ge(xnT_lo, 2 * s + 2)
                    transposes(QT, qk[:, par], qT_done)
                    pe.wait_ge(v_ready, 2 * n + 2)
                    if has(1):
                        pe.wait_ge(qk_ready, 3 * (s - 1) + 3)
                    for c in range(CH):
                        f = slice(c * 128, (c + 1) * 128)
                        for t in range(T):
                            mm = pe.matmul(HEADM[:, f], v[:, par, t, f], qk[:, par, t, D + c * 128:D + (c + 1) * 128],
                                           start=(t == 0), stop=(t == T - 1))
                    mm.then_inc(headm_done, 1)
                if has(3):
                    m, mp = s - 3, 1 - par
                    pe.wait_ge(mwo_ready, m + 1)
                    pe.wait_ge(qT_ready, 2 * m + 2)
                    if has(1):
                        pe.wait_ge(v_ready, 2 * (s - 1) + 2)
                    for t in range(T):
                        dst = ATT[1][0:TOK, 0:D] if t == 2 else ATT[0][0:TOK, t * D:(t + 1) * D]
                        for c in range(CH):
                            mm = pe.matmul(dst, qT[:, mp, c, t * TOK:(t + 1) * TOK], m_wo[:, c],
                                           start=(c == 0), stop=(c == CH - 1))
                        if t:
                            mm.then_inc(att_done, 1)

            steps(run, pe)


class Chain:

    def __init__(self, eng, sem):
        self.eng, self.sem, self.n = eng, sem, 0

    def step(self, ins):
        self.n += 1
        ins.then_inc(self.sem, 1)
        self.eng.wait_ge(self.sem, self.n)


def all_reduce_max(nc, name, parts):
    with ExitStack() as ctx:
        row = [ctx.enter_context(nc.sbuf_tensor(f"{name}_row{i}", [128, 1], F32)) for i in range(len(parts))]
        row_max, all_max = (ctx.enter_context(nc.semaphore(f"{name}_{x}")) for x in ("row_max", "all_max"))
        block = ctx.enter_context(nc.Block())

        @block.vector
        def _(dve):
            for i, (_out, tile) in enumerate(parts):
                dve.tensor_reduce(row[i][:], tile, AXX, ALU.max).then_inc(row_max, 1)

        @block.gpsimd
        def _(pool):
            for i, (out, _tile) in enumerate(parts):
                pool.wait_ge(row_max, i + 1)
                pool.partition_all_reduce(out[:], row[i][:], 128, RMAX).then_inc(all_max, 1)
            pool.wait_ge(all_max, len(parts))


def ffn_weights(nc, a, gu_w, down_w):
    mats = (("w_gate", NI // 128, D, lambda p, k, r: gu_w[p][:, k, r * 128:r * 128 + 128]),
            ("w_up", NI // 128, D, lambda p, k, r: gu_w[p][:, k, NI + r * 128:NI + r * 128 + 128]),
            ("w_down", D // 128, NI, lambda p, k, r: down_w[p][:, k, r * 128:r * 128 + 128]))
    with ExitStack() as ctx:
        def sb(name, shape, dt=F32):
            return ctx.enter_context(nc.sbuf_tensor(name, shape, dt))

        def sem(name):
            return ctx.enter_context(nc.semaphore(name))

        raw = [sb(f"{n}_raw", [128, r, i]) for n, r, i, _ in mats]
        scale = [sb(f"{n}_scale", [128, r * i // BLK]) for n, r, i, _ in mats]
        inv = [sb(f"{n}_inv", [128, r * i // BLK]) for n, r, i, _ in mats]
        wq = [sb(f"{n}_q", [128, r, i], I16) for n, r, i, _ in mats]
        ident = sb("w_ident", [128, 128])
        bank = [ctx.enter_context(nc.psum_tensor(f"w_bank{i}", [128, 512], F32)) for i in range(4)]
        raw_in = [sem(f"{n}_in") for n, *_ in mats]
        quant, id_ready, w_ready, w_turned, w_hi, w_lo = (
            sem(x) for x in ("quant", "id_ready", "w_ready", "w_turned", "ffn_w_hi", "ffn_w_lo"))
        groups = []
        for i, (_n, rows, cols, put) in enumerate(mats):
            tiles = [(k, r) for k in range(cols // 128) for r in range(rows)]
            groups += [(i, put, tiles[g:g + 4]) for g in range(0, len(tiles), 4)]
        block = ctx.enter_context(nc.Block())

        @block.sync
        def _(sp):
            for i, (name, rows, cols, _put) in enumerate(mats):
                sp.dma_start(raw[i][:], a[name].rearrange("(r p) i -> p r i", p=128)).then_inc(raw_in[i], 16)

        @block.gpsimd
        def _(pool):
            pool.memset(ident[:], 0.0).then_inc(id_ready, 1)
            pool.wait_ge(id_ready, 1)
            pool.affine_select(out=ident[:], in_=ident[:], compare_op=ALU.not_equal, fill=1.0, base=0,
                               pattern=[[-1, 128]], channel_multiplier=1).then_inc(id_ready, 1)

        @block.vector
        def _(dve):
            chain = Chain(dve, quant)
            for i, (_n, rows, cols, _put) in enumerate(mats):
                nb = rows * cols // BLK
                blocks = raw[i][:].rearrange("p r (b e) -> p (r b) e", e=BLK)
                ints = wq[i][:].rearrange("p r (b e) -> p (r b) e", e=BLK)
                dve.wait_ge(raw_in[i], 16)
                chain.step(dve.tensor_reduce(scale[i][:], blocks, AXX, ALU.max, apply_absolute_value=True))
                chain.step(dve.tensor_scalar(scale[i][:], scale[i][:], 1.0 / 7.0, 1e-12, ALU.mult, ALU.max))
                chain.step(dve.reciprocal(inv[i][:], scale[i][:]))
                chain.step(dve.tensor_tensor(blocks, blocks, inv[i][:, :, None].broadcast_to([128, nb, BLK]), ALU.mult))
                chain.step(dve.tensor_scalar(ints, blocks, 7.0, -8.0, ALU.min, ALU.max))
                dve.tensor_tensor(blocks, ints, scale[i][:, :, None].broadcast_to([128, nb, BLK]), ALU.mult
                                  ).then_inc(w_ready, 1)
            for g, (i, put, tiles) in enumerate(groups):
                dve.wait_ge(w_hi, 4 * g + 4)
                for n, (k, r) in enumerate(tiles):
                    ins = dve.tensor_tensor(put(1, k, r), bank[g % 4][:, n * 128:(n + 1) * 128],
                                            put(0, k, r).bitcast(F32), ALU.subtract)
                    if n == len(tiles) - 1:
                        ins.then_inc(w_lo, 1)

        @block.tensor
        def _(pe):
            pe.wait_ge(id_ready, 2)
            for g, (i, _put, tiles) in enumerate(groups):
                pe.wait_ge(w_ready, i + 1)
                wait(pe, w_lo, g - 3)
                for n, (k, r) in enumerate(tiles):
                    tr = pe.transpose(bank[g % 4][:, n * 128:(n + 1) * 128], raw[i][:, r, k * 128:(k + 1) * 128], ident[:])
                tr.then_inc(w_turned, 1)

        @block.scalar
        def _(act):
            for g, (i, put, tiles) in enumerate(groups):
                act.wait_ge(w_turned, g + 1)
                for n, (k, r) in enumerate(tiles):
                    act.activation(put(0, k, r), bank[g % 4][:, n * 128:(n + 1) * 128], ACT.Copy).then_inc(w_hi, 1)


def gate_up_products(pe, banks, gu_w, x_part, par, tile_no, taken, ready, done):
    ready()
    for mt in range(MT):
        use = par * MT + mt
        count = tile_no * MT + mt + 1 - len(banks)
        wait(pe, taken, count if not isinstance(count, int) else max(count, 0))
        for c in range(CH):
            for i, (a_, b_) in enumerate(PASSES):
                mm = pe.matmul(banks[use % len(banks)][:, 0:FT], gu_w[a_][:, c, mt * 128:(mt + 1) * 128],
                               x_part[b_][:, par, c], start=(c == 0 and i == 0), stop=(c == CH - 1 and i == 2))
        mm.then_inc(done, 1)


def ffn_max(nc, dram, gu_w, x_int, x_max, sx, g_max, u_max):
    with ExitStack() as ctx:
        def sb(name, shape, dt=F32):
            return ctx.enter_context(nc.sbuf_tensor(name, shape, dt))

        def sem(name):
            return ctx.enter_context(nc.semaphore(name))

        inv_x = sb("inv_x", [128, 1])
        x_rows = sb("x_rows", [128, 2, CH, FT])
        x_part = [sb(f"xq_part{p}", [128, 2, CH, FT], F32R) for p in range(2)]
        bank = [ctx.enter_context(nc.psum_tensor(f"max_bank{i}", [128, 512], F32)) for i in range(8)]
        scales, x_in, int_ready = sem("scales"), [sem(f"rows_in{i}") for i in range(2)], sem("int_ready")
        part_hi, part_ready, gu_done, gu_taken = sem("part_hi"), sem("part_ready"), sem("gu_done"), sem("gu_taken")
        sp_seen = sem("sp_seen")
        block = ctx.enter_context(nc.Block())

        @block.sync
        def _(sp):
            def load(n, par):
                wait_alone(sp, int_ready, n - 1, sp_seen)
                sp.dma_start(x_rows[:, par], dram["xn3T"][:, :, bass.ds(n * FT, FT)]).then_inc(x_in[par], 16)

            load(0, 0)
            load(1, 1)
            with sp.Fori(2, NFT - 1, 2) as n:
                for par in range(2):
                    load(n + par, par)

        @block.scalar
        def _(act):
            act.wait_ge(scales, 2)

            def quantise(n, par):
                act.wait_ge(x_in[par], 8 * (n - par) + 16)
                act.activation(x_int[:, :, bass.ds(n * FT, FT)], x_rows[:, par], ACT.Copy, scale=inv_x[:, 0:1]
                               ).then_inc(int_ready, 1)

            with act.Fori(0, NFT - 1, 2) as n:
                for par in range(2):
                    quantise(n + par, par)

        @block.vector
        def _(dve):
            dve.tensor_scalar(sx[:], x_max[:], 1.0 / QMAX, 1e-12, ALU.mult, ALU.max).then_inc(scales, 1)
            dve.wait_ge(scales, 1)
            dve.reciprocal(inv_x[:], sx[:]).then_inc(scales, 1)

            def split(n, par):
                dve.wait_ge(int_ready, n + 1)
                wait(dve, gu_done, MT * (n - 1))
                split_ints(dve, x_part, x_int, n, par, part_hi, part_ready)

            def maxima(n, par):
                for mt in range(MT):
                    dve.wait_ge(gu_done, MT * n + mt + 1)
                    out, col = (g_max, mt) if mt < MT // 2 else (u_max, mt - MT // 2)
                    dve.tensor_reduce(out[:, bass.ds(n * (MT // 2) + col, 1)], bank[(par * MT + mt) % 8][:, 0:FT],
                                      AXX, ALU.max, apply_absolute_value=True).then_inc(gu_taken, 1)

            split(0, 0)
            with dve.Fori(0, NFT - 3, 2) as n:
                for par in range(2):
                    split(n + par + 1, 1 - par)
                    maxima(n + par, par)
            split(NFT - 1, 1)
            maxima(NFT - 2, 0)
            maxima(NFT - 1, 1)
            dve.wait_ge(gu_taken, MT * NFT)

        @block.tensor
        def _(pe):
            def products(n, par):
                gate_up_products(pe, bank, gu_w, x_part, par, n, gu_taken,
                                 lambda: pe.wait_ge(part_ready, n + 1), gu_done)

            for n in range(2):
                products(n, n)
            with pe.Fori(2, NFT - 1, 2) as n:
                for par in range(2):
                    products(n + par, par)


def split_ints(eng, x_part, x_int, n, par, part_hi, part_ready):
    ints = x_int[:, :, bass.ds(n * FT, FT)]
    eng.tensor_copy(x_part[0][:, par], ints).then_inc(part_hi, 1)
    eng.wait_ge(part_hi, n + 1)
    eng.tensor_tensor(x_part[1][:, par], ints, x_part[0][:, par].bitcast(F32), ALU.subtract).then_inc(part_ready, 1)


def ffn_gate_up(nc, dram, gu_w, x_int, sx, g_top, u_top, s_g, s_u, p_max):
    with ExitStack() as ctx:
        def sb(name, shape, dt=F32):
            return ctx.enter_context(nc.sbuf_tensor(name, shape, dt))

        def sem(name):
            return ctx.enter_context(nc.semaphore(name))

        tmp = [sb(f"gu_tmp{i}", [128, 1]) for i in range(2)]
        f_g, f_u = sb("f_g", [128, 1]), sb("f_u", [128, 1])
        x_part = [sb(f"gu_part{p}", [128, 2, CH, FT], F32R) for p in range(2)]
        gi, ui = sb("gi", [128, 2, HT, FT], I16), sb("ui", [128, 2, HT, FT], I16)
        sig = sb("sig", [128, HT, FT])
        si = sb("si", [128, HT, FT], U16)
        p = sb("p", [128, 2, HT, FT])
        bank = [ctx.enter_context(nc.psum_tensor(f"gu_bank{i}", [128, 512], F32)) for i in range(8)]
        scales, part_hi, part_ready = sem("gu_scales"), sem("gu_part_hi"), sem("gu_part_ready")
        gu_done, gu_taken = sem("gu2_done"), sem("gu2_taken")
        sig_ready, si_ready, p_ready, p_max_ready = sem("sig_ready"), sem("si_ready"), sem("p_ready"), sem("p_max_ready")
        p_stored = [sem(f"p_stored{i}") for i in range(2)]
        ui_stored = [sem(f"ui_stored{i}") for i in range(2)]
        N_SCALES = 8
        sp_seen = sem("sp_seen")
        block = ctx.enter_context(nc.Block())

        @block.sync
        def _(sp):
            with sp.Fori(0, NFT - 1, 2) as i:
                for par in range(2):
                    n = i + par
                    wait_alone(sp, gu_taken, MT * n + MT, sp_seen)
                    sp.dma_start(dram["ui"][bass.ds(n, 1)].rearrange("b q m t -> q (b m) t"), ui[:, par]
                                 ).then_inc(ui_stored[par], 16)
                    wait_alone(sp, p_ready, n + 1, sp_seen)
                    sp.dma_start(dram["p"][bass.ds(n, 1)].rearrange("b q m t -> q (b m) t"), p[:, par]
                                 ).then_inc(p_stored[par], 16)
            for par in range(2):
                sp.wait_ge(ui_stored[par], 8 * NFT)
                sp.wait_ge(p_stored[par], 8 * NFT)

        @block.scalar
        def _(act):
            act.wait_ge(scales, N_SCALES)

            def tile(n, par):
                wait(act, p_ready, n - 1)
                for mt in range(MT):
                    act.wait_ge(gu_done, MT * n + mt + 1)
                    if mt == HT:
                        wait(act, si_ready, n)
                        act.wait_ge(gu_taken, MT * n + HT)
                        act.activation(sig[:], gi[:, par], ACT.Sigmoid, scale=s_g[:, 0:1]).then_inc(sig_ready, 1)
                        wait(act, ui_stored[par], 8 * (n - par))
                    dst, f = (gi[:, par, mt], f_g) if mt < HT else (ui[:, par, mt - HT], f_u)
                    act.activation(dst, bank[(par * MT + mt) % 8][:, 0:FT], ACT.Copy, scale=f[:, 0:1]
                                   ).then_inc(gu_taken, 1)

            tile(0, 0)
            tile(1, 1)
            with act.Fori(2, NFT - 1, 2) as n:
                for par in range(2):
                    tile(n + par, par)

        @block.vector
        def _(dve):
            chain = Chain(dve, scales)
            for top, s, f, t in ((g_top, s_g, f_g, tmp[0]), (u_top, s_u, f_u, tmp[1])):
                chain.step(dve.tensor_scalar(t[:], top[:], sx[:, 0:1], 1.0 / QMAX, ALU.mult, ALU.mult))
                chain.step(dve.tensor_scalar(s[:], t[:], 1e-12, None, ALU.max))
                chain.step(dve.reciprocal(t[:], s[:]))
                chain.step(dve.tensor_scalar(f[:], t[:], sx[:, 0:1], None, ALU.mult))

            def split(n, par):
                wait(dve, gu_done, MT * (n - 1))
                split_ints(dve, x_part, x_int, n, par, part_hi, part_ready)

            def tile(n, par):
                dve.wait_ge(sig_ready, n + 1)
                dve.tensor_scalar(si[:], sig[:], 65536.0, 65535.0, ALU.mult, ALU.min).then_inc(si_ready, 1)
                dve.wait_ge(si_ready, n + 1)
                wait(dve, p_stored[par], 8 * (n - par))
                dve.tensor_tensor(p[:, par], gi[:, par], si[:], ALU.mult).then_inc(p_ready, 1)
                dve.wait_ge(p_ready, n + 1)
                dve.tensor_reduce(p_max[:, bass.ds(n, 1)], p[:, par].rearrange("q m t -> q (m t)"), AXX, ALU.max,
                                  apply_absolute_value=True).then_inc(p_max_ready, 1)

            split(0, 0)
            split(1, 1)
            tile(0, 0)
            split(2, 0)
            tile(1, 1)
            with dve.Fori(2, NFT - 3, 2) as n:
                for par in range(2):
                    split(n + par + 1, 1 - par)
                    tile(n + par, par)
            split(NFT - 1, 1)
            tile(NFT - 2, 0)
            tile(NFT - 1, 1)
            dve.wait_ge(p_max_ready, NFT)

        @block.tensor
        def _(pe):
            def products(n, par):
                gate_up_products(pe, bank, gu_w, x_part, par, n, gu_taken,
                                 lambda: pe.wait_ge(part_ready, n + 1), gu_done)

            for n in range(2):
                products(n, n)
            with pe.Fori(2, NFT - 1, 2) as n:
                for par in range(2):
                    products(n + par, par)


def ffn_product_max(nc, dram, gs, p_top, s_g, s_3, o_max):
    with ExitStack() as ctx:
        def sb(name, shape, dt=F32):
            return ctx.enter_context(nc.sbuf_tensor(name, shape, dt))

        def sem(name):
            return ctx.enter_context(nc.semaphore(name))

        tmp, f_3 = sb("p_tmp", [128, 1]), sb("f_3", [128, 1])
        p, ui = sb("p_rows", [128, 2, HT, FT]), sb("ui_rows", [128, 2, HT, FT], I16)
        o = sb("o_prod", [128, HT, FT])
        scales, gs_ready, o_ready, o_max_ready = sem("p_scales"), sem("gs_ready"), sem("o_ready"), sem("o_max_ready")
        p_in, ui_in = [sem(f"p_in{i}") for i in range(2)], [sem(f"ui_in{i}") for i in range(2)]
        sp_seen = sem("sp_seen")
        block = ctx.enter_context(nc.Block())

        @block.sync
        def _(sp):
            def load(n, par):
                wait_alone(sp, gs_ready, n - 1, sp_seen)
                sp.dma_start(p[:, par], dram["p"][bass.ds(n, 1)].rearrange("b q m t -> q (b m) t")).then_inc(p_in[par], 16)
                wait_alone(sp, o_ready, 2 * (n - 1), sp_seen)
                sp.dma_start(ui[:, par], dram["ui"][bass.ds(n, 1)].rearrange("b q m t -> q (b m) t")).then_inc(ui_in[par], 16)

            load(0, 0)
            load(1, 1)
            with sp.Fori(2, NFT - 1, 2) as n:
                for par in range(2):
                    load(n + par, par)

        @block.scalar
        def _(act):
            act.wait_ge(scales, 5)
            with act.Fori(0, NFT - 1, 2) as i:
                for par in range(2):
                    n = i + par
                    act.wait_ge(p_in[par], 8 * i + 16)
                    act.activation(gs[:, bass.ds(n, 1)].rearrange("q b m t -> q (b m) t"), p[:, par], ACT.Copy,
                                   scale=f_3[:, 0:1]).then_inc(gs_ready, 1)

        @block.vector
        def _(dve):
            chain = Chain(dve, scales)
            chain.step(dve.tensor_scalar(tmp[:], p_top[:], s_g[:, 0:1], 1.0 / 65536.0, ALU.mult, ALU.mult))
            chain.step(dve.tensor_scalar(s_3[:], tmp[:], 1.0 / QMAX, 1e-12, ALU.mult, ALU.max))
            chain.step(dve.reciprocal(tmp[:], s_3[:]))
            chain.step(dve.tensor_scalar(f_3[:], tmp[:], s_g[:, 0:1], 1.0 / 65536.0, ALU.mult, ALU.mult))
            chain.step(dve.tensor_copy(tmp[:], f_3[:]))

            def tile(n, par):
                dve.wait_ge(gs_ready, n + 1)
                dve.wait_ge(ui_in[par], 8 * (n - par) + 16)
                for half in range(2):
                    m = slice(half * HT // 2, (half + 1) * HT // 2)
                    wait(dve, o_max_ready, 2 * n + half - 1)
                    dve.tensor_tensor(o[:, m], gs[:, bass.ds(n, 1), m].rearrange("q b m t -> q (b m) t"),
                                      ui[:, par, m], ALU.mult).then_inc(o_ready, 1)
                for half in range(2):
                    m = slice(half * HT // 2, (half + 1) * HT // 2)
                    dve.wait_ge(o_ready, 2 * n + half + 1)
                    dve.tensor_reduce(o_max[:, bass.ds(2 * n + half, 1)], o[:, m].rearrange("q m t -> q (m t)"),
                                      AXX, ALU.max, apply_absolute_value=True).then_inc(o_max_ready, 1)

            tile(0, 0)
            tile(1, 1)
            with dve.Fori(2, NFT - 1, 2) as n:
                for par in range(2):
                    tile(n + par, par)
            dve.wait_ge(o_max_ready, 2 * NFT)


def ffn_down(nc, dram, down_w, gs, o_top, s_3, s_u, out):
    RING = 4
    NU = 4 * NFT
    STEP = 2 * RING
    with ExitStack() as ctx:
        def sb(name, shape, dt=F32):
            return ctx.enter_context(nc.sbuf_tensor(name, shape, dt))

        def sem(name):
            return ctx.enter_context(nc.semaphore(name))

        tmp, s_4, f_4 = sb("o_tmp", [128, 1]), sb("s_4", [128, 1]), sb("f_4", [128, 1])
        ui, oi = sb("ui_down", [128, RING, HT, DT], I16), sb("oi", [128, RING, HT, TOK], I16)
        o_part = [sb(f"o_part{i}", [128, RING, HT, TOK], F32R) for i in range(2)]
        h2 = sb("h2_rows", [TOK, 2, 2, D])
        res = sb("res", [TOK, RING, 2, D])
        bank = [ctx.enter_context(nc.psum_tensor(f"down_bank{i}", [128, 512], F32)) for i in range(RING)]
        scales, oi_ready, hi_ready, lo_ready = sem("o_scales"), sem("oi_ready"), sem("o_hi_ready"), sem("o_lo_ready")
        down_done, ffn_ready, res_ready = sem("down_done"), sem("ffn_ready"), sem("res_ready")
        ui_in, h2_in = [sem(f"uid_in{i}") for i in range(RING)], [sem(f"h2_in{i}") for i in range(2)]
        stored = [sem(f"stored{i}") for i in range(RING)]
        h2_rows = dram["h2"].rearrange("b t p d -> (b t) p d")
        out_rows = out.rearrange("(g p) d -> g p d", p=TOK)
        sp_seen = sem("sp_seen")
        block = ctx.enter_context(nc.Block())

        def steps(eng, run, ahead=0):
            for j in range(STEP):
                run(0, j)
            with eng.Fori(1, NU // STEP - 1) as q:
                for j in range(STEP):
                    run(q, j)
            for j in range(STEP - ahead):
                run(NU // STEP - 1, j)

        @block.sync
        def _(sp):
            def load_ui(q, j):
                k, half = RING * q + j, j % 2
                wait_alone(sp, oi_ready, 2 * (k - RING + 1), sp_seen)
                sp.dma_start(ui[:, j], dram["ui"][bass.ds(RING // 2 * q + j // 2, 1), :, :, half * DT:(half + 1) * DT
                                                  ].rearrange("b q m t -> q (b m) t")).then_inc(ui_in[j], 16)

            def load_h2(k, par):
                sp.dma_start(h2[:, par], h2_rows[bass.ds(2 * k, 2)].rearrange("g p d -> p g d")).then_inc(h2_in[par], 16)

            def store(k, j, loads):
                wait_alone(sp, res_ready, 2 * (k + 1), sp_seen)
                if loads:
                    load_h2(k + 2, j % 2)
                sp.dma_start(out_rows[bass.ds(2 * k, 2)].rearrange("g p d -> p g d"), res[:, j]).then_inc(stored[j], 16)

            for j in range(RING - 1):
                load_ui(0, j)
            for k in range(2):
                load_h2(k, k)
            for j in range(RING):
                load_ui((j + RING - 1) // RING, (j + RING - 1) % RING)
                store(j, j, True)
            with sp.Fori(1, NFT * 2 // RING - 1) as q:
                for j in range(RING):
                    load_ui(q + (j + RING - 1) // RING, (j + RING - 1) % RING)
                    store(RING * q + j, j, True)
            load_ui(NFT * 2 // RING - 1, RING - 1)
            for j in range(RING):
                store(NFT * 2 - RING + j, j, j < RING - 2)
            for j in range(RING):
                sp.wait_ge(stored[j], 16 * (NFT * 2 // RING))

        @block.gpsimd
        def _(pool):
            def add(q, j):
                k = j // 2
                pool.wait_ge(ffn_ready, STEP * q + j + 1)
                if j % 2 == 0:
                    pool.wait_ge(h2_in[k % 2], 16 * (RING // 2 * q + k // 2 + 1))
                pool.tensor_tensor(res[:, k, j % 2], res[:, k, j % 2], h2[:, k % 2, j % 2], ALU.add).then_inc(res_ready, 1)

            steps(pool, add)

        @block.scalar
        def _(act):
            act.wait_ge(scales, 6)

            def hi(q, j):
                u = STEP * q + j
                act.wait_ge(oi_ready, u + 1)
                wait(act, down_done, u - RING + 1)
                act.activation(o_part[0][:, j % RING], oi[:, j % RING], ACT.Copy).then_inc(hi_ready, 1)

            def take(q, j):
                act.wait_ge(down_done, STEP * q + j + 1)
                if j % 2 == 0:
                    wait(act, stored[j // 2], 16 * q)
                act.activation(res[:, j // 2, j % 2], bank[j % RING][0:TOK, 0:D], ACT.Copy, scale=s_4[0:TOK, 0:1]
                               ).then_inc(ffn_ready, 1)

            AHEAD = RING - 1

            def run(q, j):
                hi(q + (j + AHEAD) // STEP, (j + AHEAD) % STEP)
                take(q, j)

            for j in range(AHEAD):
                hi(0, j)
            steps(act, run, AHEAD)
            for j in range(STEP - AHEAD, STEP):
                take(NU // STEP - 1, j)

        @block.vector
        def _(dve):
            chain = Chain(dve, scales)
            chain.step(dve.tensor_scalar(tmp[:], o_top[:], s_3[:, 0:1], s_u[:, 0:1], ALU.mult, ALU.mult))
            chain.step(dve.tensor_scalar(s_4[:], tmp[:], 1.0 / QMAX, 1e-12, ALU.mult, ALU.max))
            chain.step(dve.reciprocal(tmp[:], s_4[:]))
            chain.step(dve.tensor_scalar(f_4[:], tmp[:], s_3[:, 0:1], s_u[:, 0:1], ALU.mult, ALU.mult))
            chain.step(dve.tensor_copy(tmp[:], f_4[:]))
            chain.step(dve.tensor_copy(tmp[:], s_4[:]))

            def quantise(q, j):
                u = STEP * q + j
                if j % 2 == 0:
                    dve.wait_ge(ui_in[j // 2], 16 * (q + 1))
                wait(dve, lo_ready, u - RING + 1)
                tok = slice(j % 4 * TOK, (j % 4 + 1) * TOK)
                dve.scalar_tensor_tensor(oi[:, j % RING], gs[:, bass.ds(2 * q + j // 4, 1), :, tok].rearrange(
                    "q b m t -> q (b m) t"), f_4[:, 0:1], ui[:, j // 2, :, j % 2 * TOK:(j % 2 + 1) * TOK],
                    ALU.mult, ALU.mult).then_inc(oi_ready, 1)

            def lo(q, j):
                dve.wait_ge(hi_ready, STEP * q + j + 1)
                dve.tensor_tensor(o_part[1][:, j % RING], oi[:, j % RING], o_part[0][:, j % RING].bitcast(F32),
                                  ALU.subtract).then_inc(lo_ready, 1)

            def run(q, j):
                quantise(q + (j + 1) // STEP, (j + 1) % STEP)
                lo(q, j)

            quantise(0, 0)
            steps(dve, run, 1)
            lo(NU // STEP - 1, STEP - 1)

        @block.tensor
        def _(pe):
            def unit(q, j):
                u = STEP * q + j
                pe.wait_ge(lo_ready, u + 1)
                wait(pe, ffn_ready, u - RING + 1)
                for c in range(HT):
                    for i, (a_, b_) in enumerate(PASSES):
                        mm = pe.matmul(bank[j % RING][0:TOK, 0:D], o_part[a_][:, j % RING, c],
                                       down_w[b_][:, c], start=(c == 0 and i == 0), stop=(c == HT - 1 and i == 2))
                mm.then_inc(down_done, 1)

            steps(pe, unit)


def build(nc, a, out):
    with ExitStack() as ctx:
        def scalar(name):
            return ctx.enter_context(nc.sbuf_tensor(name, [128, 1], F32))

        x_max, sx, g_top, u_top, s_g, s_u, p_top, s_3, o_top = (
            scalar(x) for x in ("x_max", "sx", "g_top", "u_top", "s_g", "s_u", "p_top", "s_3", "o_top"))
        dram = {"hx": nc.dram_tensor("hx_dram", (NCT, 128, 2, 2, D), F32, kind="Internal").ap(),
                "h2": nc.dram_tensor("h2_dram", (B, T, TOK, D), F32, kind="Internal").ap(),
                "xn3T": nc.dram_tensor("xn3T_dram", (128, CH, NTOK), F32, kind="Internal").ap(),
                "ui": nc.dram_tensor("ui_dram", (NFT, 128, HT, FT), I16, kind="Internal").ap(),
                "p": nc.dram_tensor("p_dram", (NFT, 128, HT, FT), F32, kind="Internal").ap()}
        conv_tower(nc, a, dram)
        attention(nc, a, dram, x_max)
        with ExitStack() as c1:
            def sb(name, shape, dt=F32):
                return c1.enter_context(nc.sbuf_tensor(name, shape, dt))

            down_w = [sb(f"down_w{p}", [128, NI // 128, D], F32R) for p in range(2)]
            p_max, o_max = sb("p_max", [128, NFT]), sb("o_max", [128, 2 * NFT])
            with ExitStack() as c2:
                gu_w = [c2.enter_context(nc.sbuf_tensor(f"gu_w{p}", [128, CH, 2 * NI], F32R)) for p in range(2)]
                x_int = c2.enter_context(nc.sbuf_tensor("x_int", [128, CH, NTOK], I16))
                g_max = c2.enter_context(nc.sbuf_tensor("g_max", [128, NFT * HT], F32))
                u_max = c2.enter_context(nc.sbuf_tensor("u_max", [128, NFT * HT], F32))
                ffn_weights(nc, a, gu_w, down_w)
                ffn_max(nc, dram, gu_w, x_int, x_max, sx, g_max, u_max)
                all_reduce_max(nc, "gu", ((g_top, g_max[:]), (u_top, u_max[:])))
                ffn_gate_up(nc, dram, gu_w, x_int, sx, g_top, u_top, s_g, s_u, p_max)
            all_reduce_max(nc, "pm", ((p_top, p_max[:]),))
            gs = c1.enter_context(nc.sbuf_tensor("gs", [128, NFT, HT, FT], I16))
            ffn_product_max(nc, dram, gs, p_top, s_g, s_3, o_max)
            all_reduce_max(nc, "om", ((o_top, o_max[:]),))
            ffn_down(nc, dram, down_w, gs, o_top, s_3, s_u, out)


def kernel(x, L0_tok_W1, L0_tok_b1, L0_tok_W2, L0_tok_b2, L0_tok_gamma, L0_tok_beta, L0_tok_adpfactor,
           L0_attn_Wq, L0_attn_bq, L0_attn_Wk, L0_attn_bk, L0_attn_Wv, L0_attn_bv, L0_attn_Wo, L0_attn_bo,
           L0_attn_m, L0_ffn_w_gate, L0_ffn_w_up, L0_ffn_w_down):
    import numpy as np
    import concourse.bacc as bacc
    from concourse.bass_utils import run_bass_kernel_spmd

    def conv_rows(w):
        w = np.asarray(w).reshape(D, CH, 128, GRP, TAPS, 2)
        return np.ascontiguousarray(w.transpose(2, 1, 5, 3, 4, 0).reshape(128, NW, TAPS, D))

    def chunk_rows(w):
        return np.ascontiguousarray(np.asarray(w).reshape(CH, 128, D).transpose(1, 0, 2))

    xT = np.ascontiguousarray(np.asarray(x).reshape(B, N, 2, CH, 128)[:, :, ::-1].transpose(4, 0, 3, 2, 1))
    arrays = {
        "xT": xT, "W1T": conv_rows(L0_tok_W1), "W2T": conv_rows(L0_tok_W2),
        "b1": L0_tok_b1, "b2": L0_tok_b2, "gamma": L0_tok_gamma, "beta": L0_tok_beta,
        "adp": np.asarray(L0_tok_adpfactor).reshape(1),
        "WqT": chunk_rows(L0_attn_Wq), "WkT": chunk_rows(L0_attn_Wk), "WvT": chunk_rows(L0_attn_Wv),
        "WoT": chunk_rows(L0_attn_Wo), "bq": L0_attn_bq, "bk": L0_attn_bk, "bv": L0_attn_bv, "bo": L0_attn_bo,
        "m_rep": np.ascontiguousarray(np.repeat(np.asarray(L0_attn_m), HD).reshape(CH, 128).T),
        "w_gate": L0_ffn_w_gate, "w_up": L0_ffn_w_up, "w_down": L0_ffn_w_down,
    }
    arrays = {k: np.ascontiguousarray(v) for k, v in arrays.items()}
    nc = bacc.Bacc("TRN2", target_bir_lowering=False, num_devices=1)
    a = {k: nc.dram_tensor(f"in_{k}", v.shape, mybir.dt.from_np(v.dtype), kind="ExternalInput").ap()
         for k, v in arrays.items()}
    out = nc.dram_tensor("out", (NTOK, D), F32, kind="ExternalOutput").ap()
    build(nc, a, out)
    r = run_bass_kernel_spmd(nc, [{f"in_{k}": v for k, v in arrays.items()}], core_ids=[0])
    return r.results[0]["out"].reshape(B, N, D)
```

```python
import math
from contextlib import ExitStack

import concourse.bass as bass
from concourse import mybir

F32, F32R = mybir.dt.float32, mybir.dt.float32r
I16, U16, I32 = mybir.dt.int16, mybir.dt.uint16, mybir.dt.int32
ACT = mybir.ActivationFunctionType
ALU = mybir.AluOpType
RMAX = bass.bass_isa.ReduceOp.max
AXX = mybir.AxisListType.X
PASSES = ((0, 0), (0, 1), (1, 0))

B, L, D, KC = 32, 750, 256, 12
PAD = (KC - 2) // 2
N = (L + 2 * PAD - KC) // 2 + 1
CH = D // 128
J = KC // 2
TAPS = 3
GRP = J // TAPS
NW = 2 * CH * GRP
UT = 128
ROWS = 384
KINDS = 3
NPAIR = B // 2
NCT = NPAIR * KINDS
XL = 2 * UT + J
SL = UT + 2
OFF = (PAD + 1) // 2, PAD // 2
T, TOK = 3, N // 3
HEADS, HD = 16, 16
LN_EPS = 1e-5
SURE = 0.3
STREAMS = ((0, 2, ALU.subtract, SL), (1, 3, ALU.subtract, SL - 1), (1, 2, ALU.add, UT),
           (2, 1, ALU.subtract, UT), (4, 5, ALU.add, UT), (5, 4, ALU.subtract, UT))
NS = len(STREAMS)
USES = ((0, 0), (2, 0), (3, 0), (1, 0)), ((1, 1), (4, 0), (5, 0), (0, 2))
NI = 768
BLK = 32
NTOK = B * N
FT = 500
NFT = NTOK // FT
DT = FT // 2
HT = NI // 128
MT = 2 * HT
QMAX = 32767.0


def wait(eng, sem, count):
    if not isinstance(count, int) or count > 0:
        eng.wait_ge(sem, count)


def wait_alone(eng, sem, count, seen):
    if not isinstance(count, int) or count > 0:
        eng.wait_ge(sem, count)
        eng.sem_inc(seen, 1)


class Arena:

    def __init__(self, nc, start):
        self.nc, self.at = nc, start

    def cut(self, name, shape, dt=F32):
        tile = self.nc.alloc_sbuf_tensor_at(name, shape, dt, offset=self.at)
        size = math.prod(shape[1:]) * (2 if dt == I16 else 4)
        self.at += (size + 31) // 32 * 32
        return tile[:]


def arenas(nc, ctx, name, size, count):
    start = (nc.sbuf_base + 31) // 32 * 32
    ctx.enter_context(nc.sbuf_tensor(name, [128, size // 4], F32))
    return [Arena(nc, start) for _ in range(count)]


def conv_rows(dram, n, k):
    rows = dram["hx"].rearrange("s p e k d -> (s p e) k d").rearrange("(b n) k d -> b n k d", n=ROWS)
    return rows[bass.ds(n, 1), 0:N, k].rearrange("b (t p) d -> p (b t) d", p=TOK)


class AttentionPrep:

    def __init__(self, nc, ctx, a, dram, cuts):
        def sem(name):
            return ctx.enter_context(nc.semaphore(name))

        self.a, self.dram = a, dram
        self.qkv_w_raw = cuts.cut("qkv_w_raw", [128, CH, 3 * D])
        self.qkv_w = [cuts.cut(f"qkv_w{p}", [128, CH, 3 * D], F32R) for p in range(2)]
        self.wo, self.bias_qkv = cuts.cut("wo", [128, CH, D]), cuts.cut("bias_qkv", [128, 3 * D])
        self.m_rep, self.m_exp, self.n_base, self.inv_scaling = (
            cuts.cut(x, [128, CH]) for x in ("m_rep", "m_exp", "n_base", "inv_scaling"))
        self.neg_half, self.eps = cuts.cut("a_neg_half", [128, T]), cuts.cut("a_eps", [128, T])
        self.ident, self.block_ones = cuts.cut("ident", [128, 128]), cuts.cut("block_ones", [128, 128])
        self.head_mask = cuts.cut("head_mask", [128, CH, 128])
        self.xn = cuts.cut("xn", [TOK, 2, T, D])
        self.consts_in, self.xn_in = sem("a_consts_in"), [sem(f"xn_in{i}") for i in range(2)]
        self.arena_free, self.set, self.built, self.m_steps = sem("arena_free"), sem("a_set"), sem("a_built"), sem("m_steps")
        self.qkv_w_hi, self.qkv_w_lo = sem("qkv_w_hi"), sem("qkv_w_lo")

    def load(self, sp):
        sp.sem_inc(self.arena_free, 1)
        for i, name in enumerate(("WqT", "WkT", "WvT")):
            sp.dma_start(self.qkv_w_raw[:, :, i * D:(i + 1) * D], self.a[name]).then_inc(self.consts_in, 16)
        sp.dma_start(self.m_rep, self.a["m_rep"]).then_inc(self.consts_in, 16)
        sp.dma_start(self.wo, self.a["WoT"]).then_inc(self.consts_in, 16)
        for i, name in enumerate(("bq", "bk", "bv")):
            sp.dma_start(self.bias_qkv[:, i * D:(i + 1) * D],
                         self.a[name].rearrange("(o n) -> o n", o=1).broadcast_to([128, D])).then_inc(self.consts_in, 16)
        for n in range(2):
            sp.dma_start(self.xn[:, n], conv_rows(self.dram, n, 1)).then_inc(self.xn_in[n], 16)

    def scalar(self, act):
        act.wait_ge(self.consts_in, 16 * 8)
        act.activation(self.m_exp, self.m_rep, ACT.Sigmoid).then_inc(self.m_steps, 1)
        act.activation(self.qkv_w[0], self.qkv_w_raw, ACT.Copy).then_inc(self.qkv_w_hi, 1)

    def vector(self, dve):
        dve.wait_ge(self.qkv_w_hi, 1)
        dve.tensor_tensor(self.qkv_w[1], self.qkv_w_raw, self.qkv_w[0].bitcast(F32), ALU.subtract).then_inc(self.qkv_w_lo, 1)

    def gpsimd(self, pool):
        pool.wait_ge(self.arena_free, 1)
        for tile, value in ((self.ident, 0.0), (self.block_ones, 1.0), (self.neg_half, -0.5), (self.eps, LN_EPS),
                            (self.n_base, float(N))):
            pool.memset(tile, value).then_inc(self.set, 1)
        pool.wait_ge(self.set, 5)
        pool.affine_select(out=self.ident, in_=self.ident, compare_op=ALU.not_equal, fill=1.0, base=0,
                           pattern=[[-1, 128]], channel_multiplier=1).then_inc(self.built, 1)
        heads = self.block_ones.rearrange("p (j r) -> p j r", r=HD)
        pool.affine_select(out=heads, in_=heads, compare_op=ALU.is_ge, fill=0.0, base=0,
                           pattern=[[-HD, 128 // HD], [0, HD]], channel_multiplier=1).then_inc(self.built, 1)
        pool.wait_ge(self.built, 2)
        pool.affine_select(out=heads, in_=heads, compare_op=ALU.is_ge, fill=0.0, base=HD - 1,
                           pattern=[[HD, 128 // HD], [0, HD]], channel_multiplier=-1).then_inc(self.built, 1)
        pool.wait_ge(self.m_steps, 1)
        pool.tensor_scalar(self.m_exp, self.m_exp, -1.0, None, ALU.mult).then_inc(self.m_steps, 1)
        pool.wait_ge(self.m_steps, 2)
        pool.tensor_tensor(self.inv_scaling, self.n_base, self.m_exp, ALU.pow).then_inc(self.m_steps, 1)
        pool.wait_ge(self.m_steps, 3)
        pool.wait_ge(self.built, 3)
        for c in range(CH):
            pool.tensor_scalar(self.head_mask[:, c], self.block_ones, self.inv_scaling[:, c:c + 1], None, ALU.mult
                               ).then_inc(self.m_steps, 1)


class DownLoads:

    TILES = 3

    def __init__(self, nc, ctx, dram, cuts):
        self.dram, n = dram, self.TILES
        self.gu, self.h2 = cuts.cut("gu_rows", [128, n, 2, HT, FT], I16), cuts.cut("h2_rows", [TOK, n, 2, D])
        self.gu_in, self.h2_in = ([ctx.enter_context(nc.semaphore(f"{x}{i}")) for i in range(n)] for x in ("gu_in", "h2_in"))
        self.h2_rows = dram["h2"].rearrange("b t p d -> (b t) p d")

    def load_gu(self, sp, n, j):
        sp.dma_start(self.gu[:, j], self.dram["gu"][bass.ds(n, 1)].rearrange("b q w m t -> q (b w) m t")
                     ).then_inc(self.gu_in[j], 16)

    def load_h2(self, sp, k, i):
        sp.dma_start(self.h2[:, i], self.h2_rows[bass.ds(2 * k, 2)].rearrange("g p d -> p g d")).then_inc(self.h2_in[i], 16)

    def rest(self, sp):
        for n in range(1, self.TILES - 1):
            self.load_gu(sp, n, n)
        for k in range(self.TILES):
            self.load_h2(sp, k, k)


class WeightQuantiser:

    def __init__(self, nc, ctx, a, cuts):
        def sem(name):
            return ctx.enter_context(nc.semaphore(name))

        self.a = a
        self.mats = ("w_gate", NI // 128, D), ("w_up", NI // 128, D), ("w_down", D // 128, NI)
        self.raw = [cuts.cut(f"{n}_raw", [128, r, i]) for n, r, i in self.mats]
        self.scale = [cuts.cut(f"{n}_scale", [128, r * i // BLK]) for n, r, i in self.mats]
        self.inv = [cuts.cut(f"{n}_inv", [128, r * i // BLK]) for n, r, i in self.mats]
        self.wq = [cuts.cut(f"{n}_q", [128, r, i], I16) for n, r, i in self.mats]
        self.raw_in = [sem(f"{n}_in") for n, *_ in self.mats]
        self.amax, self.scaled, self.divided, self.rounded, self.done = (
            sem(f"w_{x}") for x in ("amax", "scaled", "divided", "rounded", "dequantised"))

    def load(self, sp):
        for i, (name, _r, _i) in enumerate(self.mats):
            sp.dma_start(self.raw[i], self.a[name].rearrange("(r p) i -> p r i", p=128)).then_inc(self.raw_in[i], 16)

    def blocks(self, i, tile):
        return tile.rearrange("p r (b e) -> p (r b) e", e=BLK)

    def by_block(self, i, tile):
        _n, r, cols = self.mats[i]
        return tile[:, :, None].broadcast_to([128, r * cols // BLK, BLK])

    def vector(self, dve, s):
        if s < 3:
            dve.wait_ge(self.raw_in[s], 16)
            dve.tensor_reduce(self.scale[s], self.blocks(s, self.raw[s]), AXX, ALU.max, apply_absolute_value=True
                              ).then_inc(self.amax, 1)
            dve.wait_ge(self.amax, 2 * s + 1)
            dve.tensor_scalar(self.scale[s], self.scale[s], 1.0 / 7.0, 1e-12, ALU.mult, ALU.max).then_inc(self.amax, 1)
            dve.wait_ge(self.amax, 2 * s + 2)
            dve.reciprocal(self.inv[s], self.scale[s]).then_inc(self.scaled, 1)
        if 3 <= s < 6:
            i = s - 3
            dve.wait_ge(self.rounded, i + 1)
            dve.tensor_tensor(self.blocks(i, self.raw[i]), self.blocks(i, self.wq[i]), self.by_block(i, self.scale[i]),
                              ALU.mult).then_inc(self.done, 1)
        if 2 <= s < 5:
            i = s - 2
            dve.wait_ge(self.divided, i + 1)
            dve.tensor_scalar(self.wq[i], self.raw[i], 7.0, -8.0, ALU.min, ALU.max).then_inc(self.rounded, 1)

    def gpsimd(self, pool, s):
        if 1 <= s < 4:
            i = s - 1
            pool.wait_ge(self.scaled, i + 1)
            pool.tensor_tensor(self.blocks(i, self.raw[i]), self.blocks(i, self.raw[i]), self.by_block(i, self.inv[i]),
                               ALU.mult).then_inc(self.divided, 1)


def conv_tower(nc, a, dram, seen, arena, prep):
    ctx = ExitStack()

    def sb(name, shape, dt=F32):
        return ctx.enter_context(nc.sbuf_tensor(name, shape, dt))

    def sem(name):
        return ctx.enter_context(nc.semaphore(name))

    RING = 3

    with ctx:
        conv_w = [arena.cut(f"conv_w{p}", [128, NW, 4, 2 * D], F32R) for p in range(2)]
        x_raw = [sb(f"x_raw{i}", [128, 2 * CH, XL]) for i in range(KINDS)]
        stream = sb("stream", [128, 2 * CH, NS, SL])
        s_part = [[sb(f"s_part{p}_{buf}", [128, 2, NS, SL], F32R)[:] for buf in range(RING - 1)] for p in range(2)]
        last_parts, w_buffers = arenas(nc, ctx, "last_parts", 2 * 2 * NS * SL * 4, 2)
        for p in range(2):
            s_part[p].append(last_parts.cut(f"s_part{p}_{RING - 1}", [128, 2, NS, SL], F32R))
        bias12 = sb("bias12", [128, 2 * D])
        gamma, beta, bias_o = sb("gamma", [128, D]), sb("beta", [128, D]), sb("bias_o", [128, D])
        adp = sb("adp", [128, 1])
        neg_half, eps = sb("neg_half", [128, 2]), sb("eps", [128, 2])
        y = sb("y", [128, 2, 2 * D])
        z, gate = y[:, :, 0:D], y[:, :, D:2 * D]
        hx = sb("hx", [128, 2, 2, 2, D])
        stats = [sb(f"c_stats{i}", [128, 2, 6]) for i in range(2)]
        mv = [sb(f"c_mv{i}", [128, 2, 2]) for i in range(2)]
        var_eps = [sb(f"c_var_eps{i}", [128, 2]) for i in range(2)]
        rstd = [sb(f"c_rstd{i}", [128, 2]) for i in range(2)]
        bank = [ctx.enter_context(nc.psum_tensor(f"conv_bank{i}", [128, 512], F32)) for i in range(8)]

        w_raw = [w_buffers.cut(f"w_raw{b}", [128, TAPS, 2 * D]) for b in range(2)]
        w_sum = hx[:].rearrange("p b e k d -> p (b e k d)").rearrange("p (k d) -> p k d", k=4)[:, 0:3]

        consts_in, ones_set = sem("c_consts_in"), sem("c_ones_set")
        w_in = [sem(f"w_in{i}") for i in range(2)]
        w_sums, w_signs, w_hi, w_lo = sem("w_sums"), sem("w_signs"), sem("w_hi"), sem("w_lo")
        zeros_set, tails_set = sem("zeros_set"), sem("tails_set")
        x_in = [sem(f"x_in{i}") for i in range(KINDS)]
        stream_ready, s_hi, s_lo = sem("stream_ready"), sem("s_hi"), sem("s_lo")
        half_done, out_sum, gate_ready, gated = sem("half_done"), sem("out_sum"), sem("gate_ready"), sem("gated")
        stats_ready = [sem(f"c_stats_ready{i}") for i in range(2)]
        mv_ready = [sem(f"c_mv_ready{i}") for i in range(2)]
        veps_ready = [sem(f"c_veps_ready{i}") for i in range(2)]
        rstd_ready = [sem(f"c_rstd_ready{i}") for i in range(2)]
        z_norm, z_gamma, z_beta, sigz_ready = sem("z_norm"), sem("z_gamma"), sem("z_beta"), sem("sigz_ready")
        h_ready, xn_ready, h_bo_ready = sem("h_ready"), sem("c_xn_ready"), sem("h_bo_ready")
        hx_stored = [sem(f"hx_stored{i}") for i in range(2)]
        sp_seen, dve_seen = seen

        def steps(run, eng, lag):
            for s in range(2 * KINDS):
                run(s, s // KINDS, s, s > 0, s >= lag)
            with eng.Fori(2, NPAIR - 1, 2) as pair:
                for k in range(2 * KINDS):
                    run(pair * KINDS + k, pair + k // KINDS, k, True, True)
            for s in range(NCT, NCT + lag):
                run(s, None, s % (2 * KINDS), False, True)

        def ring(k, c):
            return (CH * k + c) % RING

        def x_pieces(pair, kind):
            first = 2 * UT * kind
            for ph in range(2):
                for b in range(2):
                    lo = max(first, b * ROWS + OFF[ph])
                    hi = min(first + XL, b * ROWS + OFF[ph] + N)
                    if lo < hi:
                        yield lo - first, ph, 2 * pair + b, lo - b * ROWS - OFF[ph], hi - lo

        FIRST = (0, 2)
        N_PIECES = [len(list(x_pieces(0, kind))) for kind in range(KINDS)]
        block = ctx.enter_context(nc.Block())

        @block.sync
        def _(sp):
            def load_w(g):
                if g >= 2:
                    sp.wait_ge(w_lo, 4 * (g - 1))
                for i, name in enumerate(("W1T", "W2T")):
                    sp.dma_start(w_raw[g % 2][:, :, i * D:(i + 1) * D], a[name][:, g]).then_inc(w_in[g % 2], 16)

            def load_x(pair, kind):
                for col, ph, batch, n0, n in x_pieces(pair, kind):
                    sp.dma_start(x_raw[kind][:, ph:2 * CH:2, col:col + n],
                                 a["xT"][:, bass.ds(batch, 1), :, ph, n0:n0 + n].rearrange("p b c n -> p (b c) n")
                                 ).then_inc(x_in[kind], 16)

            sp.wait_ge(zeros_set, 1)
            load_x(0, 0)
            load_w(0)
            load_w(1)
            for kind in range(1, KINDS):
                sp.wait_ge(zeros_set, kind + 1)
                load_x(0, kind)
            for g in range(2, NW):
                load_w(g)

            def reload(pair, kind):
                wait_alone(sp, stream_ready, CH * (KINDS * (pair - 1) + kind + 1), sp_seen)
                load_x(pair, kind)

            def store(s, par):
                wait_alone(sp, xn_ready, 2 * s + 2, sp_seen)
                wait_alone(sp, h_bo_ready, s + 1, sp_seen)
                sp.dma_start(dram["hx"][bass.ds(s, 1)].rearrange("s p e k d -> p (s e) k d"), hx[:, par]
                             ).then_inc(hx_stored[par], 16)

            for kind in range(KINDS):
                reload(1, kind)
            with sp.Fori(2, NPAIR - 1, 2) as pair:
                for k in range(2 * KINDS):
                    reload(pair + k // KINDS, k % KINDS)
                    store((pair - 2) * KINDS + k, k % 2)
            for s in range(NCT - 2 * KINDS, NCT - 2):
                store(s, s % 2)
            sp.wait_ge(half_done, CH * NCT)
            prep.load(sp)
            for s in range(NCT - 2, NCT):
                store(s, s % 2)
            for par in range(2):
                sp.wait_ge(hx_stored[par], 16 * NCT // 2)

        @block.scalar
        def _(act):
            for dst, src in ((bias12[:, 0:D], a["b1"]), (bias12[:, D:2 * D], a["b2"]), (gamma[:], a["gamma"]),
                             (beta[:], a["beta"]), (bias_o[:], a["bo"]), (adp[:], a["adp"])):
                act.dma_start(dst, src.rearrange("(o n) -> o n", o=1).broadcast_to([128, src.shape[0]])
                              ).then_inc(consts_in, 16)
            def high(s, k, c):
                act.wait_ge(stream_ready, CH * s + c + 1)
                wait(act, half_done, CH * s + c - RING + 1)
                act.activation(s_part[0][ring(k, c)], stream[:, 2 * c:2 * c + 2], ACT.Copy).then_inc(s_hi, 1)

            for g in range(NW):
                raw = w_raw[g % 2]
                parts = (raw[:, 0], 1.0), (raw[:, 2], 1.0), (w_sum[:, 1], 0.5), (w_sum[:, 2], 0.5)
                for k, (src, scale) in enumerate(parts):
                    if k == 0:
                        act.wait_ge(w_in[g % 2], 32 * (g // 2 + 1))
                    if k == 2:
                        act.wait_ge(w_signs, 2 * g + 2)
                    act.activation(conv_w[0][:, g, (0, 3, 1, 2)[k]], src, ACT.Copy, scale=scale).then_inc(w_hi, 1)
                if g in FIRST:
                    high(0, 0, FIRST.index(g))
            act.wait_ge(consts_in, 6 * 16)
            act.wait_ge(w_lo, 4 * NW)

            def run(s, pair, k, start, end):
                f = s - 2
                if start:
                    high(s, k, 0)
                if end:
                    act.wait_ge(out_sum, 5 * f + 5)
                    act.activation(gate, gate, ACT.Sigmoid, scale=adp[:, 0:1]).then_inc(gate_ready, 1)
                if start:
                    high(s, k, 1)
                if end:
                    act.wait_ge(z_beta, f + 1)
                    act.activation(gate, z, ACT.Sigmoid).then_inc(sigz_ready, 1)

            steps(run, act, 2)
            prep.scalar(act)

        @block.gpsimd
        def _(pool):
            pool.memset(neg_half[:], -0.5).then_inc(ones_set, 1)
            pool.memset(eps[:], LN_EPS).then_inc(ones_set, 1)
            pool.wait_ge(ones_set, 2)
            pool.memset(stream[:, :, :, UT:SL], 0.0).then_inc(tails_set, 1)
            pool.wait_ge(tails_set, 1)

            def streams(s, pair, k, c):
                if c == 0:
                    pool.wait_ge(x_in[k % KINDS], (pair + 1) * (16 * N_PIECES[k % KINDS]))
                wait(pool, s_lo, CH * (s - 1) + c + 1)
                for i, (p, q, op, n) in enumerate(STREAMS):
                    ins = pool.tensor_tensor(stream[:, 2 * c:2 * c + 2, i, 0:n],
                                             x_raw[k % KINDS][:, 2 * c:2 * c + 2, p:p + 2 * n - 1:2],
                                             x_raw[k % KINDS][:, 2 * c:2 * c + 2, q:q + 2 * n - 1:2], op)
                ins.then_inc(stream_ready, 1)

            for g in range(NW):
                raw = w_raw[g % 2]
                pool.wait_ge(w_in[g % 2], 32 * (g // 2 + 1))
                if g:
                    pool.wait_ge(w_signs, 2 * g)
                pool.tensor_tensor(w_sum[:, 0], raw[:, 0], raw[:, 2], ALU.add).then_inc(w_sums, 1)
                if g in FIRST:
                    streams(0, 0, 0, FIRST.index(g))
            pool.wait_ge(consts_in, 6 * 16)

            def inv_std(i, s):
                pool.wait_ge(mv_ready[i], 2 * s + 2)
                pool.tensor_tensor(var_eps[i][:], mv[i][:, :, 1], eps[:], ALU.add).then_inc(veps_ready[i], 1)
                pool.wait_ge(veps_ready[i], s + 1)
                pool.tensor_tensor(rstd[i][:], var_eps[i][:], neg_half[:], ALU.pow).then_inc(rstd_ready[i], 1)

            def finish(s, par):
                inv_std(0, s)
                pool.wait_ge(z_norm, 2 * s + 2)
                pool.tensor_tensor(z, z, gamma[:, None, :].broadcast_to([128, 2, D]), ALU.mult).then_inc(z_gamma, 1)
                pool.wait_ge(z_gamma, s + 1)
                pool.tensor_tensor(z, z, beta[:, None, :].broadcast_to([128, 2, D]), ALU.add).then_inc(z_beta, 1)
                inv_std(1, s)
                pool.wait_ge(xn_ready, 2 * s + 2)
                pool.tensor_tensor(hx[:, par, :, 0], hx[:, par, :, 0], bias_o[:, None, :].broadcast_to([128, 2, D]),
                                   ALU.add).then_inc(h_bo_ready, 1)

            def run(s, pair, k, start, end):
                if start:
                    streams(s, pair, k, 0)
                if end:
                    finish(s - 3, (k - 3) % 2)
                if start:
                    streams(s, pair, k, 1)

            steps(run, pool, 3)
            prep.gpsimd(pool)

        @block.vector
        def _(dve):
            for kind in range(KINDS):
                dve.memset(x_raw[kind][:], 0.0).then_inc(zeros_set, 1)
            def low(s, k, c):
                dve.wait_ge(s_hi, CH * s + c + 1)
                dve.tensor_tensor(s_part[1][ring(k, c)], stream[:, 2 * c:2 * c + 2],
                                  s_part[0][ring(k, c)].bitcast(F32), ALU.subtract).then_inc(s_lo, 1)

            for g in range(NW):
                raw = w_raw[g % 2]
                if g:
                    dve.wait_ge(w_lo, 4 * g)
                parts = (raw[:, 0], 1.0), (raw[:, 2], 1.0), (w_sum[:, 1], 0.5), (w_sum[:, 2], 0.5)
                dve.wait_ge(w_sums, g + 1)
                dve.tensor_tensor(w_sum[:, 1], w_sum[:, 0], raw[:, 1], ALU.add).then_inc(w_signs, 1)
                dve.tensor_tensor(w_sum[:, 2], w_sum[:, 0], raw[:, 1], ALU.subtract).then_inc(w_signs, 1)
                for k, (src, scale) in enumerate(parts):
                    f = (0, 3, 1, 2)[k]
                    dve.wait_ge(w_hi, 4 * g + k + 1)
                    dve.scalar_tensor_tensor(conv_w[1][:, g, f], src, scale, conv_w[0][:, g, f].bitcast(F32),
                                             ALU.mult, ALU.subtract).then_inc(w_lo, 1)
                if g in FIRST:
                    low(0, 0, FIRST.index(g))
            dve.wait_ge(consts_in, 6 * 16)

            def layer_stats(i, s, src):
                for e in range(2):
                    dve.bn_stats(stats[i][:, e], src[:, e]).then_inc(stats_ready[i], 1)
                wait_alone(dve, stats_ready[i], 2 * s + 2, dve_seen)
                for e in range(2):
                    dve.bn_aggr(mv[i][:, e], stats[i][:, e]).then_inc(mv_ready[i], 1)

            def layer_norm(i, s, dst, src, ready):
                dve.wait_ge(rstd_ready[i], s + 1)
                for e in range(2):
                    dve.tensor_scalar(dst[:, e], src[:, e], mv[i][:, e, 0:1], rstd[i][:, e:e + 1],
                                      ALU.subtract, ALU.mult).then_inc(ready, 1)

            def take(s, par):
                m = bank[4 * par:4 * par + 4]
                dve.wait_ge(half_done, CH * s + CH)
                dve.tensor_tensor(y[:, 0], m[1][:], bias12[:], ALU.add).then_inc(out_sum, 1)
                dve.wait_ge(out_sum, 5 * s + 1)
                dve.tensor_tensor(y[:, 1], y[:, 0], m[2][:], ALU.subtract).then_inc(out_sum, 1)
                dve.wait_ge(out_sum, 5 * s + 2)
                dve.tensor_tensor(y[:, 0], m[2][:], y[:, 0], ALU.add).then_inc(out_sum, 1)
                dve.tensor_tensor(y[:, 1], y[:, 1], m[3][:], ALU.subtract).then_inc(out_sum, 1)
                dve.wait_ge(out_sum, 5 * s + 3)
                dve.tensor_tensor(y[:, 0], m[0][:], y[:, 0], ALU.add).then_inc(out_sum, 1)
                dve.wait_ge(gate_ready, s + 1)
                dve.tensor_tensor(z, z, gate, ALU.mult).then_inc(gated, 1)
                dve.wait_ge(gated, s + 1)
                layer_stats(0, s, z)
                layer_norm(0, s, z, z, z_norm)

            def finish(s, par):
                dve.wait_ge(sigz_ready, s + 1)
                wait(dve, hx_stored[par], 8 * (s - par))
                h = hx[:, par, :, 0]
                dve.tensor_tensor(h, z, gate, ALU.mult).then_inc(h_ready, 1)
                dve.wait_ge(h_ready, s + 1)
                layer_stats(1, s, h)
                layer_norm(1, s, hx[:, par, :, 1], h, xn_ready)

            def run(s, pair, k, start, end):
                if start:
                    low(s, k, 0)
                if end:
                    take(s - 2, k % 2)
                if start:
                    low(s, k, 1)
                if end:
                    finish(s - 2, k % 2)

            steps(run, dve, 2)
            prep.vector(dve)

        @block.tensor
        def _(pe):
            def conv(s, k):
                m = bank[4 * (k % 2):4 * (k % 2) + 4]
                wait(pe, out_sum, 5 * (s - 1))
                for c in range(CH):
                    pe.wait_ge(s_lo, CH * s + c + 1)
                    for w in range(2 * GRP * c, 2 * GRP * (c + 1)):
                        if isinstance(s, int) and s == 0:
                            pe.wait_ge(w_lo, 4 * (w + 1))
                        ph, grp = w // GRP % 2, w % GRP
                        for f, (st, shift) in enumerate(USES[grp]):
                            for i, (a_, b_) in enumerate(PASSES):
                                mm = pe.matmul(m[f][:], s_part[a_][ring(k, c)][:, ph, st, shift:shift + UT],
                                               conv_w[b_][:, w, f], start=(w == 0 and i == 0),
                                               stop=(w == NW - 1 and i == 2))
                    mm.then_inc(half_done, 1)

            for s in range(2 * KINDS):
                conv(s, s)
            with pe.Fori(2, NPAIR - 1, 2) as pair:
                for k in range(2 * KINDS):
                    conv(pair * KINDS + k, k)


def attention(nc, a, dram, seen, x_max, prep, quant):
    ctx = ExitStack()

    def sb(name, shape, dt=F32):
        return ctx.enter_context(nc.sbuf_tensor(name, shape, dt))

    def sem(name):
        return ctx.enter_context(nc.semaphore(name))

    with ctx:
        NH3 = T * 2 * HEADS
        qkv_w, wo, bias_qkv, ident, head_mask = prep.qkv_w, prep.wo, prep.bias_qkv, prep.ident, prep.head_mask
        neg_half, eps, xn, xn_in = prep.neg_half, prep.eps, prep.xn, prep.xn_in
        h_bo = sb("h_bo", [TOK, 2, T, D])
        xnT = [[sb(f"xnT{p}_{i}", [128, CH, N], F32R) for i in range(2)] for p in range(2)]
        qk = sb("qk", [TOK, 2, T, 2 * D])
        v = sb("v", [TOK, 2, T, D])
        qk_sq = sb("qk_sq", [TOK, T, 2 * D])
        norm2, inv_norm, nr = sb("norm2", [TOK, NH3]), sb("inv_norm", [TOK, 2, NH3]), sb("nr", [TOK, NH3])
        qT = sb("qT", [128, 2, CH, N])
        head_m = sb("head_m", [128, 2, CH, 128])
        m_wo = sb("m_wo", [128, CH, D])
        h2 = sb("h2", [TOK, 2, T, D])
        xn3 = sb("xn3", [TOK, 2, T, D])
        xn3T = sb("xn3T", [128, 2, CH, N])
        stats, mv = sb("a_stats", [TOK, T, 6]), sb("a_mv", [TOK, T, 2])
        var_eps, rstd, shift = sb("a_var_eps", [TOK, T]), sb("a_rstd", [TOK, 2, T]), sb("a_shift", [TOK, 2, T])
        x_amax, x_amax1 = sb("x_amax", [128, B]), sb("x_amax1", [128, 1])

        bank = [ctx.enter_context(nc.psum_tensor(f"att_bank{i}", [128, 512], F32)) for i in range(8)]
        XNT, QT = bank[0:2], bank[0:2]
        QK = bank[2], bank[4], bank[5]
        V01, V2, MWO, HEADM = bank[3], bank[6], bank[7], bank[5]
        XN3T = bank[2], bank[4]
        ATT = bank[3], bank[6]

        h_in = [sem(f"h_in{i}") for i in range(2)]
        all_reduced = sem("all_reduced")
        xnT_done, xnT_hi, xnT_lo = sem("xnT_done"), sem("xnT_hi"), sem("xnT_lo")
        qk_done, v_done, qk_ready, v_ready = sem("qk_done"), sem("v_done"), sem("qk_ready"), sem("v_ready")
        sq_ready, norm2_ready, newton, inv_ready, root_ready = sem("sq_ready"), sem("norm2_ready"), sem("newton"), sem("inv_ready"), sem("root_ready")
        qkn_ready, qT_done, qT_ready = sem("qkn_ready"), sem("qT_done"), sem("qT_ready")
        headm_done, headm_ready, mwo_done, mwo_ready = (
            sem(x) for x in ("headm_done", "headm_ready", "mwo_done", "mwo_ready"))
        att_done, h2_ready, stats_ready, mv_ready = (sem(x) for x in ("att_done", "h2_ready", "a_stats_ready", "a_mv_ready"))
        veps_ready, rstd_ready, shift_ready, xn3_ready = (
            sem(x) for x in ("a_veps_ready", "a_rstd_ready", "shift_ready", "xn3_ready"))
        xn3T_done, xn3T_ready, x_amax_ready = sem("xn3T_done"), sem("xn3T_ready"), sem("x_amax_ready")
        h2_stored, xn3T_stored = [sem(f"h2_stored{i}") for i in range(2)], [sem(f"xn3T_stored{i}") for i in range(2)]
        sp_seen, dve_seen = seen


        def steps(run, eng, last=4):
            for s in range(6):
                run(s, s % 2, lambda k, s=s: s >= k)
            with eng.Fori(6, B - 1, 2) as i:
                for par in range(2):
                    run(i + par, par, lambda k: True)
            for s in range(B, B + last):
                run(s, s % 2, lambda k, s=s: s - k < B)

        def stored(par, count):
            return 8 * (count - par)

        block = ctx.enter_context(nc.Block())

        @block.sync
        def _(sp):
            quant.load(sp)

            def load(dst, n, k, sem_):
                sp.dma_start(dst, conv_rows(dram, n, k)).then_inc(sem_, 16)

            def run(s, par, has):
                if has(0) and not (isinstance(s, int) and s < 2):
                    wait_alone(sp, xnT_done, 2 * (s - 1), sp_seen)
                    load(xn[:, par], s, 1, xn_in[par])
                if has(2):
                    wait_alone(sp, h2_ready, 2 * (s - 3), sp_seen)
                    load(h_bo[:, par], s - 2, 0, h_in[par])
                if has(4):
                    m = s - 4
                    wait_alone(sp, h2_ready, 2 * m + 2, sp_seen)
                    sp.dma_start(dram["h2"][bass.ds(m, 1)].rearrange("b t p d -> p (b t) d"), h2[:, par]
                                 ).then_inc(h2_stored[par], 16)
                if has(5):
                    m, mp = s - 5, 1 - par
                    wait_alone(sp, xn3T_ready, 2 * m + 2, sp_seen)
                    sp.dma_start(dram["xn3T"][:, :, bass.ds(m * N, N)], xn3T[:, mp]).then_inc(xn3T_stored[mp], 16)

            steps(run, sp, 5)
            for par in range(2):
                sp.wait_ge(h2_stored[par], 8 * B)
                sp.wait_ge(xn3T_stored[par], 8 * B)

        @block.scalar
        def _(act):
            def run(s, par, has):
                if has(0):
                    wait(act, v_done, 3 * (s - 1))
                    for c in range(CH):
                        act.wait_ge(xnT_done, 2 * s + c + 1)
                        act.activation(xnT[0][par][:, c], XNT[c][:, 0:N], ACT.Copy).then_inc(xnT_hi, 1)
                if has(4):
                    m = s - 4
                    act.wait_ge(shift_ready, m + 1)
                    wait(act, xn3T_done, 2 * (m - 1))
                    for t in range(T):
                        act.activation(xn3[:, par, t], h2[:, par, t], ACT.Identity, scale=rstd[:, par, t:t + 1],
                                       bias=shift[:, par, t:t + 1]).then_inc(xn3_ready, 1)
                if has(1):
                    n, np_ = s - 1, 1 - par
                    wait(act, norm2_ready, 4 * n)
                    for t in range(T):
                        act.wait_ge(qk_ready, 3 * n + t + 1)
                        act.activation(qk_sq[:, t], qk[:, np_, t], ACT.Square).then_inc(sq_ready, 1)
                if has(3):
                    m = s - 3
                    act.wait_ge(mwo_done, m + 1)
                    wait(act, att_done, 2 * m)
                    act.activation(m_wo[:].rearrange("p c d -> p (c d)"), MWO[:], ACT.Copy).then_inc(mwo_ready, 1)
                if has(4):
                    m = s - 4
                    wait(act, xn3T_stored[par], stored(par, m))
                    wait(act, x_amax_ready, m - 1)
                    for c in range(CH):
                        act.wait_ge(xn3T_done, 2 * m + c + 1)
                        act.activation(xn3T[:, par, c], XN3T[c][:, 0:N], ACT.Copy).then_inc(xn3T_ready, 1)
                if has(1):
                    n = s - 1
                    act.wait_ge(norm2_ready, 4 * n + 4)
                    act.activation(nr[:], norm2[:], ACT.Sqrt).then_inc(root_ready, 1)
                if has(2):
                    n = s - 2
                    wait(act, att_done, 2 * (n - 1))
                    for c in range(CH):
                        act.wait_ge(qT_done, 2 * n + c + 1)
                        act.activation(qT[:, par, c], QT[c][:, 0:N], ACT.Copy).then_inc(qT_ready, 1)

            steps(run, act)

        @block.gpsimd
        def _(pool):
            def run(s, par, has):
                if has(1):
                    n, np_ = s - 1, 1 - par
                    pool.wait_ge(inv_ready, n + 1)
                    rows = qk[:, np_].rearrange("p t (h e) -> p (t h) e", e=HD)
                    pool.tensor_tensor(rows, rows, inv_norm[:, np_, :, None].broadcast_to([TOK, NH3, HD]), ALU.mult
                                       ).then_inc(qkn_ready, 1)
                if has(3):
                    m, mp = s - 3, 1 - par
                    pool.wait_ge(mv_ready, 3 * m + 3)
                    pool.tensor_tensor(var_eps[:], mv[:, :, 1], eps[0:TOK], ALU.add).then_inc(veps_ready, 1)
                    pool.wait_ge(veps_ready, m + 1)
                    wait(pool, xn3_ready, 3 * (m - 1))
                    pool.tensor_tensor(rstd[:, mp], var_eps[:], neg_half[0:TOK], ALU.pow).then_inc(rstd_ready, 1)

            def run_and_quantise(s, par, has):
                run(s, par, has)
                if isinstance(s, int):
                    quant.gpsimd(pool, s)

            steps(run_and_quantise, pool)
            pool.wait_ge(x_amax_ready, B + 1)
            pool.partition_all_reduce(x_max[:], x_amax1[:], 128, RMAX).then_inc(all_reduced, 1)
            pool.wait_ge(all_reduced, 1)

        @block.vector
        def _(dve):
            def run(s, par, has):
                if has(0):
                    for c in range(CH):
                        dve.wait_ge(xnT_hi, 2 * s + c + 1)
                        dve.tensor_tensor(xnT[1][par][:, c], XNT[c][:, 0:N], xnT[0][par][:, c].bitcast(F32),
                                          ALU.subtract).then_inc(xnT_lo, 1)
                if has(4):
                    dve.wait_ge(rstd_ready, s - 3)
                    dve.scalar_tensor_tensor(shift[:, par], mv[:, :, 0], -1.0, rstd[:, par], ALU.mult, ALU.mult
                                             ).then_inc(shift_ready, 1)
                if has(1):
                    n, np_ = s - 1, 1 - par
                    wait(dve, headm_done, n - 1)
                    for t in range(T):
                        dve.wait_ge(qk_done, 3 * n + t + 1)
                        dve.tensor_tensor(qk[:, np_, t], QK[t][0:TOK], bias_qkv[0:TOK, 0:2 * D], ALU.add
                                          ).then_inc(qk_ready, 1)
                    dve.wait_ge(v_done, 3 * n + 2)
                    dve.tensor_tensor(v[:, np_, 0:2], V01[0:TOK].rearrange("p (t d) -> p t d", t=2),
                                      bias_qkv[0:TOK, None, 2 * D:3 * D].broadcast_to([TOK, 2, D]), ALU.add
                                      ).then_inc(v_ready, 1)
                    wait(dve, inv_ready, n)
                    for t in range(T):
                        half = slice(t * 2 * HEADS, (t + 1) * 2 * HEADS)
                        dve.wait_ge(sq_ready, 3 * n + t + 1)
                        dve.tensor_reduce(norm2[:, half], qk_sq[:, t].rearrange("p (h e) -> p h e", e=HD), AXX, ALU.add
                                          ).then_inc(norm2_ready, 1)
                    dve.wait_ge(norm2_ready, 4 * n + 3)
                    dve.tensor_scalar(norm2[:], norm2[:], 1e-24, None, ALU.max).then_inc(norm2_ready, 1)
                    dve.wait_ge(v_done, 3 * n + 3)
                    dve.tensor_tensor(v[:, np_, 2], V2[0:TOK, 0:D], bias_qkv[0:TOK, 2 * D:3 * D], ALU.add
                                      ).then_inc(v_ready, 1)
                    inv = inv_norm[:, np_]
                    dve.wait_ge(root_ready, n + 1)
                    dve.reciprocal(inv, nr[:]).then_inc(newton, 1)
                    dve.wait_ge(newton, 3 * n + 1)
                    dve.tensor_tensor(nr[:], inv, inv, ALU.mult).then_inc(newton, 1)
                    dve.wait_ge(newton, 3 * n + 2)
                    dve.scalar_tensor_tensor(nr[:], nr[:], -0.5, norm2[:], ALU.mult, ALU.mult).then_inc(newton, 1)
                    dve.wait_ge(newton, 3 * n + 3)
                    dve.scalar_tensor_tensor(inv, nr[:], 1.5, inv, ALU.add, ALU.mult).then_inc(inv_ready, 1)
                if has(4):
                    m = s - 4
                    dve.wait_ge(xn3T_ready, 2 * m + 2)
                    dve.tensor_reduce(x_amax[:, bass.ds(m, 1)], xn3T[:, par].rearrange("p c n -> p (c n)"), AXX, ALU.max,
                                      apply_absolute_value=True).then_inc(x_amax_ready, 1)
                if has(2):
                    n = s - 2
                    wait(dve, mwo_done, n - 1)
                    dve.wait_ge(headm_done, n + 1)
                    dve.tensor_tensor(head_m[:, par].rearrange("p c q -> p (c q)"), HEADM[:, 0:D],
                                      head_mask[:].rearrange("p c q -> p (c q)"), ALU.mult).then_inc(headm_ready, 1)
                if has(3):
                    m, mp = s - 3, 1 - par
                    wait(dve, h2_stored[mp], stored(mp, m))
                    wait(dve, xn3_ready, 3 * (m - 1))
                    dve.wait_ge(h_in[mp], stored(mp, m) + 16)
                    dve.wait_ge(att_done, 2 * m + 2)
                    dve.tensor_tensor(h2[:, mp, 0:2], ATT[0][0:TOK].rearrange("p (t d) -> p t d", t=2),
                                      h_bo[:, mp, 0:2], ALU.add).then_inc(h2_ready, 1)
                    dve.tensor_tensor(h2[:, mp, 2], ATT[1][0:TOK, 0:D], h_bo[:, mp, 2], ALU.add).then_inc(h2_ready, 1)
                    dve.wait_ge(h2_ready, 2 * m + 2)
                    for t in range(T):
                        dve.bn_stats(stats[:, t], h2[:, mp, t]).then_inc(stats_ready, 1)
                    wait_alone(dve, stats_ready, 3 * m + 3, dve_seen)
                    for t in range(T):
                        dve.bn_aggr(mv[:, t], stats[:, t]).then_inc(mv_ready, 1)

            def run_and_quantise(s, par, has):
                run(s, par, has)
                if isinstance(s, int):
                    quant.vector(dve, s)

            steps(run_and_quantise, dve)
            dve.wait_ge(x_amax_ready, B)
            dve.tensor_reduce(x_amax1[:], x_amax[:], AXX, ALU.max).then_inc(x_amax_ready, 1)

        @block.tensor
        def _(pe):
            def transposes(dst, src, done):
                for c in range(CH):
                    for t in range(T):
                        tr = pe.transpose(dst[c][:, t * TOK:(t + 1) * TOK], src[:, t, c * 128:(c + 1) * 128],
                                          ident[0:TOK, 0:TOK])
                    tr.then_inc(done, 1)

            def qkv(n, par):
                pe.wait_ge(xnT_lo, 2 * n + 2)
                wait(pe, xn3T_ready, 2 * (n - 3))
                wait(pe, headm_ready, n - 1)

                def product(dst, t, lo, hi, done):
                    for c in range(CH):
                        for i, (a_, b_) in enumerate(PASSES):
                            mm = pe.matmul(dst, xnT[a_][par][:, c, t * TOK:(t + 1) * TOK], qkv_w[b_][:, c, lo:hi],
                                           start=(c == 0 and i == 0), stop=(c == CH - 1 and i == 2))
                    mm.then_inc(done, 1)

                for t in range(T):
                    product(QK[t][0:TOK], t, 0, 2 * D, qk_done)
                wait(pe, h2_ready, 2 * (n - 2))
                for t in range(T):
                    product(V2[0:TOK, 0:D] if t == 2 else V01[0:TOK, t * D:(t + 1) * D], t, 2 * D, 3 * D, v_done)

            def run(s, par, has):
                if has(0):
                    pe.wait_ge(xn_in[par], stored(par, s) + 16)
                    wait(pe, qT_ready, 2 * (s - 2))
                    if not has(3):
                        wait(pe, xnT_lo, 2 * s)
                    transposes(XNT, xn[:, par], xnT_done)
                if has(1):
                    if not has(4):
                        wait(pe, qk_ready, 3 * (s - 1))
                        wait(pe, v_ready, 2 * (s - 1))
                    qkv(s - 1, 1 - par)
                if has(3):
                    m, mp = s - 3, 1 - par
                    pe.wait_ge(headm_ready, m + 1)
                    wait(pe, mwo_ready, m)
                    for c in range(CH):
                        mm = pe.matmul(MWO[:, c * D:(c + 1) * D], head_m[:, mp, c], wo[:, c], start=True, stop=True)
                    mm.then_inc(mwo_done, 1)
                if has(4):
                    m = s - 4
                    pe.wait_ge(xn3_ready, 3 * m + 3)
                    if has(1):
                        pe.wait_ge(qk_ready, 3 * (s - 1) + 2)
                    transposes(XN3T, xn3[:, par], xn3T_done)
                if has(2):
                    n = s - 2
                    pe.wait_ge(qkn_ready, n + 1)
                    if has(0):
                        pe.wait_ge(xnT_lo, 2 * s + 2)
                    transposes(QT, qk[:, par], qT_done)
                    pe.wait_ge(v_ready, 2 * n + 2)
                    if has(1):
                        pe.wait_ge(qk_ready, 3 * (s - 1) + 3)
                    for c in range(CH):
                        f = slice(c * 128, (c + 1) * 128)
                        for t in range(T):
                            mm = pe.matmul(HEADM[:, f], v[:, par, t, f], qk[:, par, t, D + c * 128:D + (c + 1) * 128],
                                           start=(t == 0), stop=(t == T - 1))
                    mm.then_inc(headm_done, 1)
                if has(3):
                    m, mp = s - 3, 1 - par
                    pe.wait_ge(mwo_ready, m + 1)
                    pe.wait_ge(qT_ready, 2 * m + 2)
                    if has(1):
                        pe.wait_ge(v_ready, 2 * (s - 1) + 2)
                    for t in range(T):
                        dst = ATT[1][0:TOK, 0:D] if t == 2 else ATT[0][0:TOK, t * D:(t + 1) * D]
                        for c in range(CH):
                            mm = pe.matmul(dst, qT[:, mp, c, t * TOK:(t + 1) * TOK], m_wo[:, c],
                                           start=(c == 0), stop=(c == CH - 1))
                        if t:
                            mm.then_inc(att_done, 1)

            steps(run, pe)


class Chain:

    def __init__(self, eng, sem):
        self.eng, self.sem, self.n = eng, sem, 0

    def step(self, ins):
        self.n += 1
        ins.then_inc(self.sem, 1)
        self.eng.wait_ge(self.sem, self.n)


def all_reduce_max(nc, name, parts):
    with ExitStack() as ctx:
        row = [ctx.enter_context(nc.sbuf_tensor(f"{name}_row{i}", [128, 1], F32)) for i in range(len(parts))]
        low = [ctx.enter_context(nc.sbuf_tensor(f"{name}_low{i}", [128, 1], F32)) for i in range(len(parts))]
        row_low, row_max, all_max = (ctx.enter_context(nc.semaphore(f"{name}_{x}")) for x in ("row_low", "row_max", "all_max"))
        block = ctx.enter_context(nc.Block())

        @block.vector
        def _(dve):
            lows = 0
            for i, (_out, tile, sign) in enumerate(parts):
                if sign > 0:
                    dve.tensor_reduce(row[i][:], tile, AXX, ALU.max).then_inc(row_max, 1)
                else:
                    lows += 1
                    dve.tensor_reduce(low[i][:], tile, AXX, ALU.min).then_inc(row_low, 1)
                    dve.wait_ge(row_low, lows)
                    dve.tensor_scalar(row[i][:], low[i][:], -1.0, None, ALU.mult).then_inc(row_max, 1)

        @block.gpsimd
        def _(pool):
            for i, (out, _tile, _sign) in enumerate(parts):
                pool.wait_ge(row_max, i + 1)
                pool.partition_all_reduce(out[:], row[i][:], 128, RMAX).then_inc(all_max, 1)
            pool.wait_ge(all_max, len(parts))


def ffn_weights(nc, dram, quant, ident, gu_w, down_w, x_rows, x_in):
    groups = []
    for i in range(2):
        for k in range(CH):
            for r in range(0, HT, 3):
                groups.append((i, [(r + j, k) for j in range(3)],
                               lambda p, i=i, k=k, r=r: gu_w[p][:, k, i * NI + r * 128:i * NI + (r + 3) * 128]))
    for k in range(0, HT, 2):
        groups.append((2, [(r, k + j) for j in range(2) for r in range(CH)],
                       lambda p, k=k: down_w[p][:, k:k + 2].rearrange("q k d -> q (k d)")))
    with ExitStack() as ctx:
        def sem(name):
            return ctx.enter_context(nc.semaphore(name))

        bank = [ctx.enter_context(nc.psum_tensor(f"w_bank{i}", [128, 512], F32)) for i in range(8)]
        w_turned, w_hi, w_lo = (sem(x) for x in ("w_turned", "ffn_w_hi", "ffn_w_lo"))
        block = ctx.enter_context(nc.Block())

        @block.sync
        def _(sp):
            for n in range(2):
                sp.dma_start(x_rows[:, n], dram["xn3T"][:, :, n * FT:(n + 1) * FT]).then_inc(x_in[n], 16)

        @block.tensor
        def _(pe):
            for g, (i, tiles, _put) in enumerate(groups):
                wait(pe, w_lo, g - 7)
                for n, (r, k) in enumerate(tiles):
                    tr = pe.transpose(bank[g % 8][:, n * 128:(n + 1) * 128], quant.raw[i][:, r, k * 128:(k + 1) * 128],
                                      ident)
                tr.then_inc(w_turned, 1)

        @block.scalar
        def _(act):
            for g, (_i, tiles, put) in enumerate(groups):
                act.wait_ge(w_turned, g + 1)
                act.activation(put(0), bank[g % 8][:, 0:128 * len(tiles)], ACT.Copy).then_inc(w_hi, 1)

        @block.vector
        def _(dve):
            for g, (_i, tiles, put) in enumerate(groups):
                dve.wait_ge(w_hi, g + 1)
                dve.tensor_tensor(put(1), bank[g % 8][:, 0:128 * len(tiles)], put(0).bitcast(F32), ALU.subtract
                                  ).then_inc(w_lo, 1)


def gate_up_products(pe, banks, gu_w, x_part, par, tile_no, taken, ready, done, m=MT):
    ready()
    for mt in range(m):
        use = par * m + mt
        count = tile_no * m + mt + 1 - len(banks)
        wait(pe, taken, count if not isinstance(count, int) else max(count, 0))
        for c in range(CH):
            for i, (a_, b_) in enumerate(PASSES):
                mm = pe.matmul(banks[use % len(banks)][:, 0:FT], gu_w[a_][:, c, mt * 128:(mt + 1) * 128],
                               x_part[b_][:, par, c], start=(c == 0 and i == 0), stop=(c == CH - 1 and i == 2))
        mm.then_inc(done, 1)


def ffn_max(nc, dram, seen, x_rows, x_in, gu_w, x_int, x_max, sx, g_max, g_min, u_max):
    with ExitStack() as ctx:
        def sb(name, shape, dt=F32):
            return ctx.enter_context(nc.sbuf_tensor(name, shape, dt))

        def sem(name):
            return ctx.enter_context(nc.semaphore(name))

        inv_x = sb("inv_x", [128, 1])
        x_part = [sb(f"xq_part{p}", [128, 2, CH, FT], F32R) for p in range(2)]
        bank = [ctx.enter_context(nc.psum_tensor(f"max_bank{i}", [128, 512], F32)) for i in range(8)]
        scales, int_ready = sem("scales"), sem("int_ready")
        part_hi, part_ready, gu_done, gu_taken = sem("part_hi"), sem("part_ready"), sem("gu_done"), sem("gu_taken")
        sp_seen, _dve_seen = seen
        block = ctx.enter_context(nc.Block())

        @block.sync
        def _(sp):
            def load(n, par):
                wait_alone(sp, int_ready, n - 1, sp_seen)
                sp.dma_start(x_rows[:, par], dram["xn3T"][:, :, bass.ds(n * FT, FT)]).then_inc(x_in[par], 16)

            with sp.Fori(2, NFT - 1, 2) as n:
                for par in range(2):
                    load(n + par, par)

        @block.scalar
        def _(act):
            act.wait_ge(scales, 2)

            def quantise(n, par):
                act.wait_ge(x_in[par], 8 * (n - par) + 16)
                act.activation(x_int[:, :, bass.ds(n * FT, FT)], x_rows[:, par], ACT.Copy, scale=inv_x[:, 0:1]
                               ).then_inc(int_ready, 1)

            with act.Fori(0, NFT - 1, 2) as n:
                for par in range(2):
                    quantise(n + par, par)

        @block.vector
        def _(dve):
            dve.tensor_scalar(sx[:], x_max[:], 1.0 / QMAX, 1e-12, ALU.mult, ALU.max).then_inc(scales, 1)
            dve.wait_ge(scales, 1)
            dve.reciprocal(inv_x[:], sx[:]).then_inc(scales, 1)

            def split(n, par):
                dve.wait_ge(int_ready, n + 1)
                wait(dve, gu_done, MT * (n - 1))
                split_ints(dve, x_part, x_int, n, par, part_hi, part_ready)

            def maxima(n, par):
                for mt in range(MT):
                    dve.wait_ge(gu_done, MT * n + mt + 1)
                    product = bank[(par * MT + mt) % 8][:, 0:FT]
                    if mt < HT:
                        dve.tensor_reduce(g_max[:, bass.ds(n * HT + mt, 1)], product, AXX, ALU.max)
                        dve.tensor_reduce(g_min[:, bass.ds(n * HT + mt, 1)], product, AXX, ALU.min).then_inc(gu_taken, 1)
                    else:
                        dve.tensor_reduce(u_max[:, bass.ds(n * HT + mt - HT, 1)], product, AXX, ALU.max,
                                          apply_absolute_value=True).then_inc(gu_taken, 1)

            split(0, 0)
            with dve.Fori(0, NFT - 3, 2) as n:
                for par in range(2):
                    split(n + par + 1, 1 - par)
                    maxima(n + par, par)
            split(NFT - 1, 1)
            maxima(NFT - 2, 0)
            maxima(NFT - 1, 1)
            dve.wait_ge(gu_taken, MT * NFT)

        @block.tensor
        def _(pe):
            def products(n, par):
                gate_up_products(pe, bank, gu_w, x_part, par, n, gu_taken,
                                 lambda: pe.wait_ge(part_ready, n + 1), gu_done)

            for n in range(2):
                products(n, n)
            with pe.Fori(2, NFT - 1, 2) as n:
                for par in range(2):
                    products(n + par, par)


def split_ints(eng, x_part, x_int, n, par, part_hi, part_ready):
    ints = x_int[:, :, bass.ds(n * FT, FT)]
    eng.tensor_copy(x_part[0][:, par], ints).then_inc(part_hi, 1)
    eng.wait_ge(part_hi, n + 1)
    eng.tensor_tensor(x_part[1][:, par], ints, x_part[0][:, par].bitcast(F32), ALU.subtract).then_inc(part_ready, 1)


def ffn_scales(nc, sx, g_pos, g_neg, u_top, s_g, s_u, f_g, f_u, p_pos, search, p_max):
    with ExitStack() as ctx:
        def sb(name, shape, dt=F32):
            return ctx.enter_context(nc.sbuf_tensor(name, shape, dt))

        g_top, value = sb("g_top", [128, 1]), sb("p_value", [128, 1])
        tmp = [sb(f"gu_tmp{i}", [128, 1]) for i in range(2)]
        gi_top, sig_top, si_top = sb("gi_top", [128, 1], I16), sb("sig_top", [128, 1]), sb("si_top", [128, 1], U16)
        scales, gi_ready, sig_ready = (ctx.enter_context(nc.semaphore(x)) for x in ("gu_scales", "gi_top_ready", "sig_top_ready"))
        N_GATE = 5
        block = ctx.enter_context(nc.Block())

        @block.vector
        def _(dve):
            chain = Chain(dve, scales)
            chain.step(dve.tensor_tensor(g_top[:], g_pos[:], g_neg[:], ALU.max))
            for top, s, f, t in ((g_top, s_g, f_g, tmp[0]), (u_top, s_u, f_u, tmp[1])):
                chain.step(dve.tensor_scalar(t[:], top[:], sx[:, 0:1], 1.0 / QMAX, ALU.mult, ALU.mult))
                chain.step(dve.tensor_scalar(s[:], t[:], 1e-12, None, ALU.max))
                chain.step(dve.reciprocal(t[:], s[:]))
                chain.step(dve.tensor_scalar(f[:], t[:], sx[:, 0:1], None, ALU.mult))
            chain.step(dve.memset(p_max[:], 0.0))
            dve.wait_ge(sig_ready, 1)
            chain.step(dve.tensor_scalar(si_top[:], sig_top[:], 65536.0, 65535.0, ALU.mult, ALU.min))
            chain.step(dve.tensor_tensor(p_pos[:], gi_top[:], si_top[:], ALU.mult))
            chain.step(dve.tensor_scalar(value[:], p_pos[:], s_g[:, 0:1], 1.0 / 65536.0, ALU.mult, ALU.mult))
            chain.step(dve.tensor_scalar(search[:], value[:], SURE, None, ALU.is_lt))

        @block.scalar
        def _(act):
            act.wait_ge(scales, N_GATE)
            act.activation(gi_top[:], g_pos[:], ACT.Copy, scale=f_g[:, 0:1]).then_inc(gi_ready, 1)
            act.wait_ge(gi_ready, 1)
            act.activation(sig_top[:], gi_top[:], ACT.Sigmoid, scale=s_g[:, 0:1]).then_inc(sig_ready, 1)


def ffn_search(nc, gu_w, x_int, s_g, f_g, search, p_pos, p_max, s_3, f_3):
    with ExitStack() as ctx:
        def sb(name, shape, dt=F32):
            return ctx.enter_context(nc.sbuf_tensor(name, shape, dt))

        def sem(name):
            return ctx.enter_context(nc.semaphore(name))

        x_part = [sb(f"se_part{p}", [128, 2, CH, FT], F32R) for p in range(2)]
        gi, sig, si, p = sb("se_gi", [128, 2, HT, FT], I16), sb("se_sig", [128, HT, FT]), sb("se_si", [128, HT, FT], U16), sb("se_p", [128, HT, FT])
        p_row, p_all, p_top, tmp = (sb(x, [128, 1]) for x in ("p_row", "p_all", "p_top", "p_tmp"))
        bank = [ctx.enter_context(nc.psum_tensor(f"se_bank{i}", [128, 512], F32)) for i in range(HT)]
        part_hi, part_ready, g_done, g_taken, sig_ready, si_ready, p_ready, max_ready = (
            sem(f"se_{x}") for x in ("part_hi", "part_ready", "g_done", "g_taken", "sig_ready", "si_ready", "p_ready", "max_ready"))
        row_ready, all_ready, scales = sem("p_row_ready"), sem("p_all_ready"), sem("p_scales")
        block = ctx.enter_context(nc.Block())

        def tiles(eng, run):
            once = eng.value_load(search[0:1, 0:1], min_val=0, max_val=1)
            with eng.If(once != 0):
                run(0, 0)
                run(1, 1)
                with eng.Fori(2, NFT - 1, 2) as n:
                    for par in range(2):
                        run(n + par, par)

        @block.scalar
        def _(act):
            def tile(n, par):
                wait(act, p_ready, n - 1)
                for mt in range(HT):
                    act.wait_ge(g_done, HT * n + mt + 1)
                    act.activation(gi[:, par, mt], bank[mt][:, 0:FT], ACT.Copy, scale=f_g[:, 0:1]).then_inc(g_taken, 1)
                wait(act, si_ready, n)
                act.wait_ge(g_taken, HT * n + HT)
                act.activation(sig[:], gi[:, par], ACT.Sigmoid, scale=s_g[:, 0:1]).then_inc(sig_ready, 1)

            tiles(act, tile)

        @block.vector
        def _(dve):
            def tile(n, par):
                wait(dve, g_done, HT * (n - 1))
                split_ints(dve, x_part, x_int, n, par, part_hi, part_ready)
                dve.wait_ge(sig_ready, n + 1)
                dve.tensor_scalar(si[:], sig[:], 65536.0, 65535.0, ALU.mult, ALU.min).then_inc(si_ready, 1)
                dve.wait_ge(si_ready, n + 1)
                dve.tensor_tensor(p[:], gi[:, par], si[:], ALU.mult).then_inc(p_ready, 1)
                dve.wait_ge(p_ready, n + 1)
                dve.tensor_reduce(p_max[:, bass.ds(n, 1)], p[:].rearrange("q m t -> q (m t)"), AXX, ALU.max,
                                  apply_absolute_value=True).then_inc(max_ready, 1)
                dve.wait_ge(max_ready, n + 1)

            tiles(dve, tile)
            dve.tensor_reduce(p_row[:], p_max[:], AXX, ALU.max).then_inc(row_ready, 1)
            dve.wait_ge(all_ready, 1)
            chain = Chain(dve, scales)
            chain.step(dve.tensor_tensor(p_top[:], p_all[:], p_pos[:], ALU.max))
            chain.step(dve.tensor_scalar(tmp[:], p_top[:], s_g[:, 0:1], 1.0 / 65536.0, ALU.mult, ALU.mult))
            chain.step(dve.tensor_scalar(s_3[:], tmp[:], 1.0 / QMAX, 1e-12, ALU.mult, ALU.max))
            chain.step(dve.reciprocal(tmp[:], s_3[:]))
            chain.step(dve.tensor_scalar(f_3[:], tmp[:], s_g[:, 0:1], 1.0 / 65536.0, ALU.mult, ALU.mult))

        @block.gpsimd
        def _(pool):
            pool.wait_ge(row_ready, 1)
            pool.partition_all_reduce(p_all[:], p_row[:], 128, RMAX).then_inc(all_ready, 1)

        @block.tensor
        def _(pe):
            tiles(pe, lambda n, par: gate_up_products(pe, bank, gu_w, x_part, par, n, g_taken,
                                                      lambda: pe.wait_ge(part_ready, n + 1), g_done, HT))


def split_ints(eng, x_part, x_int, n, par, part_hi, part_ready):
    ints = x_int[:, :, bass.ds(n * FT, FT)]
    eng.tensor_copy(x_part[0][:, par], ints).then_inc(part_hi, 1)
    eng.wait_ge(part_hi, n + 1)
    eng.tensor_tensor(x_part[1][:, par], ints, x_part[0][:, par].bitcast(F32), ALU.subtract).then_inc(part_ready, 1)


def ffn_gate_up(nc, dram, seen, gu_w, x_int, s_g, f_g, f_u, f_3, o_max, p, o, loads):
    with ExitStack() as ctx:
        def sb(name, shape, dt=F32):
            return ctx.enter_context(nc.sbuf_tensor(name, shape, dt))

        def sem(name):
            return ctx.enter_context(nc.semaphore(name))

        x_part = [sb(f"gu_part{p}", [128, 2, CH, FT], F32R) for p in range(2)]
        gi, ui, gs = (sb(x, [128, 2, HT, FT], I16) for x in ("gi", "ui", "gs"))
        sig, si = sb("sig", [128, HT, FT]), sb("si", [128, HT, FT], U16)
        bank = [ctx.enter_context(nc.psum_tensor(f"gu_bank{i}", [128, 512], F32)) for i in range(8)]
        part_hi, part_ready, gu_done, gu_taken = sem("gu_part_hi"), sem("gu_part_ready"), sem("gu2_done"), sem("gu2_taken")
        sig_ready, si_ready, p_ready, gs_ready, o_ready, o_max_ready = (
            sem(x) for x in ("sig_ready", "si_ready", "p_ready", "gs_ready", "o_ready", "o_max_ready"))
        gs_stored = [sem(f"gs_stored{i}") for i in range(2)]
        ui_stored = [sem(f"ui_stored{i}") for i in range(2)]
        sp_seen, _dve_seen = seen
        block = ctx.enter_context(nc.Block())

        def steps(eng, run):
            run(0, 0)
            run(1, 1)
            with eng.Fori(2, NFT - 3, 2) as n:
                for par in range(2):
                    run(n + par, par)
            run(NFT - 2, 0)
            run(NFT - 1, 1)

        @block.sync
        def _(sp):
            def store(what, tile, n, par, stored):
                sp.dma_start(dram["gu"][bass.ds(n, 1), :, what].rearrange("b q m t -> q (b m) t"), tile[:, par]
                             ).then_inc(stored[par], 16)

            def store_gs(n, par):
                wait_alone(sp, gs_ready, n + 1, sp_seen)
                store(0, gs, n, par, gs_stored)

            def run(n, par):
                if not isinstance(n, int) or n > 0:
                    store_gs(n + (-1), 1 - par)
                wait_alone(sp, gu_taken, MT * n + MT, sp_seen)
                store(1, ui, n, par, ui_stored)

            steps(sp, run)
            sp.wait_ge(part_ready, NFT)
            loads.load_gu(sp, 0, 0)
            store_gs(NFT - 1, 1)
            loads.rest(sp)
            for par in range(2):
                sp.wait_ge(ui_stored[par], 8 * NFT)
                sp.wait_ge(gs_stored[par], 8 * NFT)

        @block.scalar
        def _(act):
            def quantise_p(n, par):
                act.wait_ge(p_ready, n + 1)
                wait(act, o_ready, n - 1)
                wait(act, gs_stored[par], 8 * (n - par))
                act.activation(gs[:, par], p[:, par], ACT.Copy, scale=f_3[:, 0:1]).then_inc(gs_ready, 1)

            def tile(n, par):
                wait(act, p_ready, n - 1)
                for mt in range(MT):
                    if mt == HT // 2 and (not isinstance(n, int) or n > 0):
                        quantise_p(n + (-1), 1 - par)
                    act.wait_ge(gu_done, MT * n + mt + 1)
                    if mt == HT:
                        wait(act, si_ready, n)
                        act.wait_ge(gu_taken, MT * n + HT)
                        act.activation(sig[:], gi[:, par], ACT.Sigmoid, scale=s_g[:, 0:1]).then_inc(sig_ready, 1)
                        wait(act, o_ready, n - 1)
                        wait(act, ui_stored[par], 8 * (n - par))
                    dst, f = (gi[:, par, mt], f_g) if mt < HT else (ui[:, par, mt - HT], f_u)
                    act.activation(dst, bank[(par * MT + mt) % 8][:, 0:FT], ACT.Copy, scale=f[:, 0:1]
                                   ).then_inc(gu_taken, 1)

            steps(act, tile)
            quantise_p(NFT - 1, 1)

        @block.vector
        def _(dve):
            def split(n, par):
                wait(dve, gu_done, MT * (n - 1))
                split_ints(dve, x_part, x_int, n, par, part_hi, part_ready)

            def product_p(n, par):
                wait(dve, p_ready, n)
                dve.wait_ge(sig_ready, n + 1)
                dve.tensor_scalar(si[:], sig[:], 65536.0, 65535.0, ALU.mult, ALU.min).then_inc(si_ready, 1)
                dve.wait_ge(si_ready, n + 1)
                wait(dve, gs_ready, n - 1)
                dve.tensor_tensor(p[:, par], gi[:, par], si[:], ALU.mult).then_inc(p_ready, 1)

            def product_o(n, par):
                dve.wait_ge(gs_ready, n + 1)
                dve.wait_ge(gu_taken, MT * n + MT)
                wait(dve, o_max_ready, n)
                dve.tensor_tensor(o[:], gs[:, par], ui[:, par], ALU.mult).then_inc(o_ready, 1)
                dve.wait_ge(o_ready, n + 1)
                dve.tensor_reduce(o_max[:, bass.ds(n, 1)], o[:].rearrange("q m t -> q (m t)"), AXX, ALU.max,
                                  apply_absolute_value=True).then_inc(o_max_ready, 1)

            def run(n, par):
                if not isinstance(n, int) or n < NFT - 1:
                    split(n + 1, 1 - par)
                product_p(n, par)
                if not isinstance(n, int) or n > 0:
                    product_o(n + (-1), 1 - par)

            split(0, 0)
            steps(dve, run)
            product_o(NFT - 1, 1)
            dve.wait_ge(o_max_ready, NFT)

        @block.tensor
        def _(pe):
            def products(n, par):
                gate_up_products(pe, bank, gu_w, x_part, par, n, gu_taken,
                                 lambda: pe.wait_ge(part_ready, n + 1), gu_done)

            steps(pe, products)


def ffn_down(nc, seen, loads, down_w, o_top, s_3, s_u, out):
    RING = 4
    TILES = loads.TILES
    gu, h2, gu_in, h2_in = loads.gu, loads.h2, loads.gu_in, loads.h2_in
    NU = 4 * NFT
    STEP = 4 * TILES
    with ExitStack() as ctx:
        def sb(name, shape, dt=F32):
            return ctx.enter_context(nc.sbuf_tensor(name, shape, dt))

        def sem(name):
            return ctx.enter_context(nc.semaphore(name))

        tmp, s_4, f_4 = sb("o_tmp", [128, 1]), sb("s_4", [128, 1]), sb("f_4", [128, 1])
        oi = sb("oi", [128, RING, HT, TOK], I16)
        o_part = [sb(f"o_part{i}", [128, RING, HT, TOK], F32R) for i in range(2)]
        res = sb("res", [TOK, TILES, 2, D])
        bank = [ctx.enter_context(nc.psum_tensor(f"down_bank{i}", [128, 512], F32)) for i in range(RING)]
        scales, oi_ready, hi_ready, lo_ready = sem("o_scales"), sem("oi_ready"), sem("o_hi_ready"), sem("o_lo_ready")
        down_done, ffn_ready, res_ready = sem("down_done"), sem("ffn_ready"), sem("res_ready")
        stored = [sem(f"stored{i}") for i in range(TILES)]
        out_rows = out.rearrange("(g p) d -> g p d", p=TOK)
        sp_seen, _dve_seen = seen
        block = ctx.enter_context(nc.Block())

        def steps(eng, run, ahead=0):
            for j in range(STEP):
                run(0, j)
            with eng.Fori(1, NU // STEP - 1) as q:
                for j in range(STEP):
                    run(q, j)
            for j in range(STEP - ahead):
                run(NU // STEP - 1, j)

        @block.sync
        def _(sp):
            def load_gu(q, j):
                n = TILES * q + j
                wait_alone(sp, oi_ready, 4 * (n - TILES + 1), sp_seen)
                loads.load_gu(sp, n, j)

            def store(k, i, load):
                wait_alone(sp, res_ready, 2 * (k + 1), sp_seen)
                if load:
                    loads.load_h2(sp, k + TILES, i)
                sp.dma_start(out_rows[bass.ds(2 * k, 2)].rearrange("g p d -> p g d"), res[:, i]).then_inc(stored[i], 16)

            def run(q, j, load_tile, load_half):
                if load_tile:
                    load_gu(q + (j + TILES - 1) // TILES, (j + TILES - 1) % TILES)
                for half in range(2):
                    i = 2 * j + half
                    store(2 * TILES * q + i, i % TILES, load_half(i))

            for j in range(TILES):
                run(0, j, True, lambda i: True)
            with sp.Fori(1, NFT // TILES - 1) as q:
                for j in range(TILES):
                    run(q, j, True, lambda i: True)
            for j in range(TILES):
                run(NFT // TILES - 1, j, j == 0, lambda i: i < TILES)
            for i in range(TILES):
                sp.wait_ge(stored[i], 16 * (2 * NFT // TILES))

        @block.gpsimd
        def _(pool):
            def add(q, j):
                i = j // 2 % TILES
                pool.wait_ge(ffn_ready, STEP * q + j + 1)
                if j % 2 == 0:
                    pool.wait_ge(h2_in[i], 16 * (2 * q + j // 2 // TILES + 1))
                pool.tensor_tensor(res[:, i, j % 2], res[:, i, j % 2], h2[:, i, j % 2], ALU.add).then_inc(res_ready, 1)

            steps(pool, add)

        @block.scalar
        def _(act):
            act.wait_ge(scales, 6)

            def hi(q, j):
                u = STEP * q + j
                act.wait_ge(oi_ready, u + 1)
                wait(act, down_done, u - RING + 1)
                act.activation(o_part[0][:, j % RING], oi[:, j % RING], ACT.Copy).then_inc(hi_ready, 1)

            def take(q, j):
                act.wait_ge(down_done, STEP * q + j + 1)
                i = j // 2 % TILES
                if j % 2 == 0:
                    wait(act, stored[i], 16 * (2 * q + j // 2 // TILES))
                act.activation(res[:, i, j % 2], bank[j % RING][0:TOK, 0:D], ACT.Copy, scale=s_4[0:TOK, 0:1]
                               ).then_inc(ffn_ready, 1)

            AHEAD = RING - 1

            def run(q, j):
                hi(q + (j + AHEAD) // STEP, (j + AHEAD) % STEP)
                take(q, j)

            for j in range(AHEAD):
                hi(0, j)
            steps(act, run, AHEAD)
            for j in range(STEP - AHEAD, STEP):
                take(NU // STEP - 1, j)

        @block.vector
        def _(dve):
            chain = Chain(dve, scales)
            chain.step(dve.tensor_scalar(tmp[:], o_top[:], s_3[:, 0:1], s_u[:, 0:1], ALU.mult, ALU.mult))
            chain.step(dve.tensor_scalar(s_4[:], tmp[:], 1.0 / QMAX, 1e-12, ALU.mult, ALU.max))
            chain.step(dve.reciprocal(tmp[:], s_4[:]))
            chain.step(dve.tensor_scalar(f_4[:], tmp[:], s_3[:, 0:1], s_u[:, 0:1], ALU.mult, ALU.mult))
            chain.step(dve.tensor_copy(tmp[:], f_4[:]))
            chain.step(dve.tensor_copy(tmp[:], s_4[:]))

            def quantise(q, j):
                u = STEP * q + j
                if j % 4 == 0:
                    dve.wait_ge(gu_in[j // 4], 16 * (q + 1))
                wait(dve, lo_ready, u - RING + 1)
                gs, ui = (gu[:, j // 4, w, :, j % 4 * TOK:(j % 4 + 1) * TOK] for w in range(2))
                dve.scalar_tensor_tensor(oi[:, j % RING], gs, f_4[:, 0:1], ui, ALU.mult, ALU.mult).then_inc(oi_ready, 1)

            def lo(q, j):
                dve.wait_ge(hi_ready, STEP * q + j + 1)
                dve.tensor_tensor(o_part[1][:, j % RING], oi[:, j % RING], o_part[0][:, j % RING].bitcast(F32),
                                  ALU.subtract).then_inc(lo_ready, 1)

            def run(q, j):
                quantise(q + (j + 1) // STEP, (j + 1) % STEP)
                lo(q, j)

            quantise(0, 0)
            steps(dve, run, 1)
            lo(NU // STEP - 1, STEP - 1)

        @block.tensor
        def _(pe):
            def unit(q, j):
                u = STEP * q + j
                pe.wait_ge(lo_ready, u + 1)
                wait(pe, ffn_ready, u - RING + 1)
                for c in range(HT):
                    for i, (a_, b_) in enumerate(PASSES):
                        mm = pe.matmul(bank[j % RING][0:TOK, 0:D], o_part[a_][:, j % RING, c],
                                       down_w[b_][:, c], start=(c == 0 and i == 0), stop=(c == HT - 1 and i == 2))
                mm.then_inc(down_done, 1)

            steps(pe, unit)


def build(nc, a, out):
    with ExitStack() as ctx:
        def scalar(name):
            return ctx.enter_context(nc.sbuf_tensor(name, [128, 1], F32))

        x_max, sx, g_pos, g_neg, u_top, s_g, s_u, f_g, f_u, p_pos, s_3, f_3, o_top = (
            scalar(x) for x in ("x_max", "sx", "g_pos", "g_neg", "u_top", "s_g", "s_u", "f_g", "f_u", "p_pos",
                                "s_3", "f_3", "o_top"))
        search = ctx.enter_context(nc.sbuf_tensor("search", [128, 1], I32))
        dram = {"hx": nc.dram_tensor("hx_dram", (NCT, 128, 2, 2, D), F32, kind="Internal").ap(),
                "h2": nc.dram_tensor("h2_dram", (B, T, TOK, D), F32, kind="Internal").ap(),
                "xn3T": nc.dram_tensor("xn3T_dram", (128, CH, NTOK), F32, kind="Internal").ap(),
                "gu": nc.dram_tensor("gu_dram", (NFT, 128, 2, HT, FT), I16, kind="Internal").ap()}
        seen = [ctx.enter_context(nc.semaphore(x)) for x in ("sp_seen", "dve_seen")]
        arena, cuts, cuts_x, cuts_d = arenas(nc, ctx, "arena", 2 * NW * 4 * 2 * D * 4, 4)
        gu_w = [cuts.cut(f"gu_w{p}", [128, CH, 2 * NI], F32R) for p in range(2)]
        down_w = [cuts.cut(f"down_w{p}", [128, HT, D], F32R) for p in range(2)]
        cuts_x.at = cuts_d.at = cuts.at
        x_int = cuts_x.cut("x_int", [128, CH, NTOK], I16)
        quant = WeightQuantiser(nc, ctx, a, cuts)
        cuts.at = max(cuts.at, cuts_x.at)
        prep = AttentionPrep(nc, ctx, a, dram, cuts)
        conv_tower(nc, a, dram, seen, arena, prep)
        attention(nc, a, dram, seen, x_max, prep, quant)

        def sb(name, shape):
            return ctx.enter_context(nc.sbuf_tensor(name, shape, F32))

        p_max, o_max = sb("p_max", [128, NFT]), sb("o_max", [128, NFT])
        with ExitStack() as c2:
            x_rows = c2.enter_context(nc.sbuf_tensor("x_rows", [128, 2, CH, FT], F32))
            x_in = [ctx.enter_context(nc.semaphore(f"rows_in{i}")) for i in range(2)]
            ffn_weights(nc, dram, quant, prep.ident, gu_w, down_w, x_rows, x_in)
            g_max, g_min, u_max = (c2.enter_context(nc.sbuf_tensor(x, [128, NFT * HT], F32)) for x in ("g_max", "g_min", "u_max"))
            ffn_max(nc, dram, seen, x_rows, x_in, gu_w, x_int, x_max, sx, g_max, g_min, u_max)
            all_reduce_max(nc, "gu", ((g_pos, g_max[:], 1), (g_neg, g_min[:], -1), (u_top, u_max[:], 1)))
        ffn_scales(nc, sx, g_pos, g_neg, u_top, s_g, s_u, f_g, f_u, p_pos, search, p_max)
        ffn_search(nc, gu_w, x_int, s_g, f_g, search, p_pos, p_max, s_3, f_3)
        p = cuts_x.cut("p", [128, 2, HT, FT])
        loads = DownLoads(nc, ctx, dram, cuts_d)
        ffn_gate_up(nc, dram, seen, gu_w, x_int, s_g, f_g, f_u, f_3, o_max, p, cuts_x.cut("o", [128, HT, FT]), loads)
        all_reduce_max(nc, "om", ((o_top, o_max[:], 1),))
        ffn_down(nc, seen, loads, down_w, o_top, s_3, s_u, out)


def kernel(x, L0_tok_W1, L0_tok_b1, L0_tok_W2, L0_tok_b2, L0_tok_gamma, L0_tok_beta, L0_tok_adpfactor,
           L0_attn_Wq, L0_attn_bq, L0_attn_Wk, L0_attn_bk, L0_attn_Wv, L0_attn_bv, L0_attn_Wo, L0_attn_bo,
           L0_attn_m, L0_ffn_w_gate, L0_ffn_w_up, L0_ffn_w_down):
    import numpy as np
    import concourse.bacc as bacc
    from concourse.bass_utils import run_bass_kernel_spmd

    def conv_rows(w):
        w = np.asarray(w).reshape(D, CH, 128, GRP, TAPS, 2)
        return np.ascontiguousarray(w.transpose(2, 1, 5, 3, 4, 0).reshape(128, NW, TAPS, D))

    def chunk_rows(w):
        return np.ascontiguousarray(np.asarray(w).reshape(CH, 128, D).transpose(1, 0, 2))

    xT = np.ascontiguousarray(np.asarray(x).reshape(B, N, 2, CH, 128)[:, :, ::-1].transpose(4, 0, 3, 2, 1))
    arrays = {
        "xT": xT, "W1T": conv_rows(L0_tok_W1), "W2T": conv_rows(L0_tok_W2),
        "b1": L0_tok_b1, "b2": L0_tok_b2, "gamma": L0_tok_gamma, "beta": L0_tok_beta,
        "adp": np.asarray(L0_tok_adpfactor).reshape(1),
        "WqT": chunk_rows(L0_attn_Wq), "WkT": chunk_rows(L0_attn_Wk), "WvT": chunk_rows(L0_attn_Wv),
        "WoT": chunk_rows(L0_attn_Wo), "bq": L0_attn_bq, "bk": L0_attn_bk, "bv": L0_attn_bv, "bo": L0_attn_bo,
        "m_rep": np.ascontiguousarray(np.repeat(np.asarray(L0_attn_m), HD).reshape(CH, 128).T),
        "w_gate": L0_ffn_w_gate, "w_up": L0_ffn_w_up, "w_down": L0_ffn_w_down,
    }
    arrays = {k: np.ascontiguousarray(v) for k, v in arrays.items()}
    nc = bacc.Bacc("TRN2", target_bir_lowering=False, num_devices=1)
    a = {k: nc.dram_tensor(f"in_{k}", v.shape, mybir.dt.from_np(v.dtype), kind="ExternalInput").ap()
         for k, v in arrays.items()}
    out = nc.dram_tensor("out", (NTOK, D), F32, kind="ExternalOutput").ap()
    build(nc, a, out)
    r = run_bass_kernel_spmd(nc, [{f"in_{k}": v for k, v in arrays.items()}], core_ids=[0])
    return r.results[0]["out"].reshape(B, N, D)
```
